# Optimizing a Trainium2 kernel written in Bass

```python
import numpy as np
import jax
import jax.numpy as jnp

def _softmax(x, axis=-1):
    return jax.nn.softmax(x, axis=axis)

def _gelu(x):
    return jax.nn.gelu(x, approximate=True)

def _silu(x):
    return jax.nn.silu(x)

def _sigmoid(x):
    return jax.nn.sigmoid(x)

def _layernorm(x, axis=-1, eps=1e-05):
    m = jnp.mean(x, axis=axis, keepdims=True)
    v = jnp.var(x, axis=axis, keepdims=True)
    return (x - m) / jnp.sqrt(v + eps)

def _scatter_add(tgt, idx, src, axis=0):
    return tgt.at[idx].add(src)

def _segment_sum(src, seg, n):
    return jax.ops.segment_sum(src, seg, n)
kernel_name = 'mk_gps_d2_gnn_r16_2f68b4'

def setup_inputs(seed: int=0):
    np.random.seed(seed)
    _w = jnp.asarray

    def _rec_inputs():
        import jax
        import jax.numpy as jnp
        _gk = jax.random.key(seed)
        x = -0.0003713 + 1 * jax.random.normal(jax.random.fold_in(_gk, 1), (3125, 256), jnp.float32)
        _s = jax.random.randint(jax.random.fold_in(_gk, 2), (50000,), 0, 3125, jnp.int32)
        _d = jax.random.randint(jax.random.fold_in(_gk, 3), (50000,), 0, 3125, jnp.int32)
        _loop = jnp.arange(3125, dtype=jnp.int32)
        src = jnp.concatenate([_s, _d, _loop])
        dst = jnp.concatenate([_d, _s, _loop])
        _o = jnp.argsort(dst, stable=True)
        src = src[_o]
        dst = dst[_o]
        edge_type_8 = jax.random.randint(jax.random.fold_in(_gk, 12), (103125,), 0, 8, jnp.int32)
        return (x, src, dst, edge_type_8)
    x, src, dst, edge_type_8 = _rec_inputs()

    def _L0_gnn_setup():
        import jax, jax.numpy as jnp
        import numpy as np
        N_NODES = 3125
        N_EDGES = 50000
        D_MODEL = 256
        H = 8
        D_K = 32
        key = jax.random.key(seed)
        kx, kq, kk, kv, ks, kd = jax.random.split(key, 6)
        scale = 1.0 / np.sqrt(D_MODEL)
        x = jax.random.normal(kx, (N_NODES, D_MODEL), dtype=jnp.float32)
        Wq = jax.random.normal(kq, (D_MODEL, H * D_K), dtype=jnp.float32) * scale
        Wk = jax.random.normal(kk, (D_MODEL, H * D_K), dtype=jnp.float32) * scale
        Wv = jax.random.normal(kv, (D_MODEL, H * D_K), dtype=jnp.float32) * scale
        src = jax.random.randint(ks, (N_EDGES,), 0, N_NODES, dtype=jnp.int32)
        dst = jax.random.randint(kd, (N_EDGES,), 0, N_NODES, dtype=jnp.int32)
        return {'x': x, 'Wq': Wq, 'Wk': Wk, 'Wv': Wv, 'src': src, 'dst': dst}
    _L0_gnn_all = _L0_gnn_setup()
    _L0_gnn_in = {k: v for k, v in _L0_gnn_all.items() if k in ('Wq', 'Wk', 'Wv')}
    del _L0_gnn_all

    def _L0_mix_setup():
        import jax, jax.numpy as jnp
        import numpy as np
        DIM = 256
        HEADS = 4
        HEAD_DIM = DIM // HEADS
        MLP_HIDDEN = DIM * 3
        B, N = (8, 256)
        EPS = 1e-05

        def _layernorm(x, g, b):
            mu = jnp.mean(x, axis=-1, keepdims=True)
            var = jnp.mean(jnp.square(x - mu), axis=-1, keepdims=True)
            return (x - mu) * jax.lax.rsqrt(var + EPS) * g + b
        key = jax.random.key(seed)
        ks = jax.random.split(key, 8)
        s = 0.02
        return {'x': jax.random.normal(ks[0], (B, N, DIM), dtype=jnp.float32), 'w_qkv': jax.random.normal(ks[1], (DIM, 3 * DIM), dtype=jnp.float32) * s, 'b_qkv': jnp.zeros((3 * DIM,), dtype=jnp.float32), 'norm_g': jnp.ones((DIM,), dtype=jnp.float32), 'norm_b': jnp.zeros((DIM,), dtype=jnp.float32), 'w_fc1': jax.random.normal(ks[2], (DIM, MLP_HIDDEN), dtype=jnp.float32) * s, 'b_fc1': jnp.zeros((MLP_HIDDEN,), dtype=jnp.float32), 'w_fc2': jax.random.normal(ks[3], (MLP_HIDDEN, DIM), dtype=jnp.float32) * s, 'b_fc2': jnp.zeros((DIM,), dtype=jnp.float32)}
    _L0_mix_all = _L0_mix_setup()
    _L0_mix_in = {k: v for k, v in _L0_mix_all.items() if k in ('w_qkv', 'b_qkv', 'norm_g', 'norm_b', 'w_fc1', 'b_fc1', 'w_fc2', 'b_fc2')}
    del _L0_mix_all

    def _L0_ffn_setup():
        import jax, jax.numpy as jnp
        import numpy as np
        C = 256
        HID = 1024
        E = 8
        TEMP = 1.0
        key = jax.random.key(seed)
        ks = jax.random.split(key, 7)
        x = jax.random.normal(ks[0], (8, 1024, C), dtype=jnp.float32)
        W1 = jax.random.normal(ks[1], (C, HID), dtype=jnp.float32) * 0.02
        b1 = jnp.zeros((HID,), dtype=jnp.float32)
        Wg = jax.random.normal(ks[2], (HID, E), dtype=jnp.float32) * 0.02
        bg = jnp.zeros((E,), dtype=jnp.float32)
        Wd = jax.random.normal(ks[3], (E, HID, C), dtype=jnp.float32) * 0.02
        bd = jnp.zeros((E, C), dtype=jnp.float32)
        return {'x': x, 'W1': W1, 'b1': b1, 'Wg': Wg, 'bg': bg, 'Wd': Wd, 'bd': bd}
    _L0_ffn_all = _L0_ffn_setup()
    _L0_ffn_in = {k: v for k, v in _L0_ffn_all.items() if k in ('W1', 'b1', 'Wg', 'bg', 'Wd', 'bd')}
    del _L0_ffn_all

    def _L1_gnn_setup():
        import jax, jax.numpy as jnp
        import numpy as np
        N_NODES = 1250
        N_EDGES = 20000
        NUM_RELS = 8
        DIM = 256
        BN_EPS = 1e-05
        key = jax.random.key(seed)
        k1, k2, k3, k4, k5 = jax.random.split(key, 5)
        h = jax.random.normal(k1, (N_NODES, DIM), dtype=jnp.float32)
        weight = jax.random.normal(k2, (NUM_RELS, DIM, DIM), dtype=jnp.float32) * 0.05
        gamma = jnp.ones((DIM,), dtype=jnp.float32)
        beta = jnp.zeros((DIM,), dtype=jnp.float32)
        src = jax.random.randint(k3, (N_EDGES,), 0, N_NODES, dtype=jnp.int32)
        dst = jax.random.randint(k4, (N_EDGES,), 0, N_NODES, dtype=jnp.int32)
        rel = jax.random.randint(k5, (N_EDGES,), 0, NUM_RELS, dtype=jnp.int32)
        return {'h': h, 'weight': weight, 'gamma': gamma, 'beta': beta, 'src': src, 'dst': dst, 'rel': rel}
    _L1_gnn_all = _L1_gnn_setup()
    _L1_gnn_in = {k: v for k, v in _L1_gnn_all.items() if k in ('weight', 'gamma', 'beta')}
    del _L1_gnn_all

    def _L1_mix_setup():
        import jax, jax.numpy as jnp
        import numpy as np
        A, Bc, Cc = (0.5, 1.0, 1.0)
        H = 8
        EPS = 1e-12

        def _normalize(t):
            n = jnp.linalg.norm(t, axis=-1, keepdims=True)
            return t / jnp.maximum(n, EPS)
        key = jax.random.key(seed)
        ks = jax.random.split(key, 5)
        B, N, C = (8, 128, 256)
        D = C // H
        x = jax.random.normal(ks[0], (B, N, C), dtype=jnp.float32)
        Wqkv = jax.random.normal(ks[1], (3 * H * D, C), dtype=jnp.float32) * 0.02
        bqkv = jnp.zeros((3 * H * D,), dtype=jnp.float32)
        Wproj = jax.random.normal(ks[2], (C, H * D), dtype=jnp.float32) * 0.02
        bproj = jnp.zeros((C,), dtype=jnp.float32)
        temperature = jnp.ones((1, H, 1, 1), dtype=jnp.float32)
        return {'x': x, 'Wqkv': Wqkv, 'bqkv': bqkv, 'Wproj': Wproj, 'bproj': bproj, 'temperature': temperature}
    _L1_mix_all = _L1_mix_setup()
    _L1_mix_in = {k: v for k, v in _L1_mix_all.items() if k in ('Wqkv', 'bqkv', 'Wproj', 'bproj', 'temperature')}
    del _L1_mix_all

    def _L1_ffn_setup():
        import jax, jax.numpy as jnp
        import numpy as np
        E = 8
        K = 2
        D = 256
        H = 512
        DOUT = 256
        EPS = 1e-05
        key = jax.random.key(seed)
        ks = jax.random.split(key, 9)
        s = 0.02
        return {'x': jax.random.normal(ks[0], (4, 512, D), jnp.float32), 'gamma': 1.0 + 0.05 * jax.random.normal(ks[1], (D,), jnp.float32), 'beta': 0.05 * jax.random.normal(ks[2], (D,), jnp.float32), 'Wr': 0.01 * jax.random.normal(ks[3], (D, E), jnp.float32), 'br': jnp.zeros((E,), jnp.float32), 'W1': s * jax.random.normal(ks[4], (E, D, H), jnp.float32), 'b1': s * jax.random.normal(ks[5], (E, H), jnp.float32), 'W2': s * jax.random.normal(ks[6], (E, H, DOUT), jnp.float32), 'b2': s * jax.random.normal(ks[7], (E, DOUT), jnp.float32)}
    _L1_ffn_all = _L1_ffn_setup()
    _L1_ffn_in = {k: v for k, v in _L1_ffn_all.items() if k in ('gamma', 'beta', 'Wr', 'br', 'W1', 'b1', 'W2', 'b2')}
    del _L1_ffn_all
    return {'x': x, 'src': src, 'dst': dst, 'edge_type_8': edge_type_8, 'L0_gnn_Wq': _L0_gnn_in['Wq'], 'L0_gnn_Wk': _L0_gnn_in['Wk'], 'L0_gnn_Wv': _L0_gnn_in['Wv'], 'L0_mix_w_qkv': _L0_mix_in['w_qkv'], 'L0_mix_b_qkv': _L0_mix_in['b_qkv'], 'L0_mix_norm_g': _L0_mix_in['norm_g'], 'L0_mix_norm_b': _L0_mix_in['norm_b'], 'L0_mix_w_fc1': _L0_mix_in['w_fc1'], 'L0_mix_b_fc1': _L0_mix_in['b_fc1'], 'L0_mix_w_fc2': _L0_mix_in['w_fc2'], 'L0_mix_b_fc2': _L0_mix_in['b_fc2'], 'L0_ffn_W1': _L0_ffn_in['W1'], 'L0_ffn_b1': _L0_ffn_in['b1'], 'L0_ffn_Wg': _L0_ffn_in['Wg'], 'L0_ffn_bg': _L0_ffn_in['bg'], 'L0_ffn_Wd': _L0_ffn_in['Wd'], 'L0_ffn_bd': _L0_ffn_in['bd'], 'L1_gnn_weight': _L1_gnn_in['weight'], 'L1_gnn_gamma': _L1_gnn_in['gamma'], 'L1_gnn_beta': _L1_gnn_in['beta'], 'L1_mix_Wqkv': _L1_mix_in['Wqkv'], 'L1_mix_bqkv': _L1_mix_in['bqkv'], 'L1_mix_Wproj': _L1_mix_in['Wproj'], 'L1_mix_bproj': _L1_mix_in['bproj'], 'L1_mix_temperature': _L1_mix_in['temperature'], 'L1_ffn_gamma': _L1_ffn_in['gamma'], 'L1_ffn_beta': _L1_ffn_in['beta'], 'L1_ffn_Wr': _L1_ffn_in['Wr'], 'L1_ffn_br': _L1_ffn_in['br'], 'L1_ffn_W1': _L1_ffn_in['W1'], 'L1_ffn_b1': _L1_ffn_in['b1'], 'L1_ffn_W2': _L1_ffn_in['W2'], 'L1_ffn_b2': _L1_ffn_in['b2']}

def reference(x, src, dst, edge_type_8, L0_gnn_Wq, L0_gnn_Wk, L0_gnn_Wv, L0_mix_w_qkv, L0_mix_b_qkv, L0_mix_norm_g, L0_mix_norm_b, L0_mix_w_fc1, L0_mix_b_fc1, L0_mix_w_fc2, L0_mix_b_fc2, L0_ffn_W1, L0_ffn_b1, L0_ffn_Wg, L0_ffn_bg, L0_ffn_Wd, L0_ffn_bd, L1_gnn_weight, L1_gnn_gamma, L1_gnn_beta, L1_mix_Wqkv, L1_mix_bqkv, L1_mix_Wproj, L1_mix_bproj, L1_mix_temperature, L1_ffn_gamma, L1_ffn_beta, L1_ffn_Wr, L1_ffn_br, L1_ffn_W1, L1_ffn_b1, L1_ffn_W2, L1_ffn_b2):
    import jax
    import jax.numpy as jnp

    def _L0_gnn_ref(x, Wq, Wk, Wv, src, dst):
        import jax, jax.numpy as jnp
        import numpy as np
        N_NODES = 3125
        N_EDGES = 50000
        D_MODEL = 256
        H = 8
        D_K = 32
        q = (x @ Wq).reshape(N_NODES, H, D_K)
        k = (x @ Wk).reshape(N_NODES, H, D_K)
        v = (x @ Wv).reshape(N_NODES, H, D_K)
        score = jnp.sum(k[src] * q[dst], axis=-1, keepdims=True)
        score = jnp.exp(jnp.clip(score / np.sqrt(D_K), -5.0, 5.0))
        wv = jax.ops.segment_sum(v[src] * score, dst, num_segments=N_NODES)
        z = jax.ops.segment_sum(score, dst, num_segments=N_NODES)
        out = wv / (z + 1e-09)
        return out.reshape(N_NODES, H * D_K)

    def _L0_mix_ref(x, w_qkv, b_qkv, norm_g, norm_b, w_fc1, b_fc1, w_fc2, b_fc2):
        import jax, jax.numpy as jnp
        import numpy as np
        DIM = 256
        HEADS = 4
        HEAD_DIM = DIM // HEADS
        MLP_HIDDEN = DIM * 3
        B, N = (8, 256)
        EPS = 1e-05

        def _layernorm(x, g, b):
            mu = jnp.mean(x, axis=-1, keepdims=True)
            var = jnp.mean(jnp.square(x - mu), axis=-1, keepdims=True)
            return (x - mu) * jax.lax.rsqrt(var + EPS) * g + b
        Bx, Nx, C = x.shape
        scale = HEAD_DIM ** (-0.5)
        qkv = (x @ w_qkv + b_qkv).reshape(Bx, Nx, 3, HEADS, HEAD_DIM)
        qkv = jnp.transpose(qkv, (2, 0, 3, 1, 4))
        q, k, v = (qkv[0], qkv[1], qkv[2])
        k = k * scale
        attn = jnp.einsum('bhnd,bhne->bhde', k, v)
        attn = jax.nn.softmax(attn, axis=-1)
        xf = jnp.einsum('bhde,bhne->bhnd', attn, q)
        xf = jnp.transpose(xf, (0, 2, 1, 3)).reshape(Bx, Nx, C)
        x = x + xf
        h = _layernorm(x, norm_g, norm_b)
        h = jax.nn.gelu(h @ w_fc1 + b_fc1, approximate=False) @ w_fc2 + b_fc2
        return x + h

    def _L0_ffn_ref(x, W1, b1, Wg, bg, Wd, bd):
        import jax, jax.numpy as jnp
        import numpy as np
        C = 256
        HID = 1024
        E = 8
        TEMP = 1.0
        orig_shape = x.shape
        xf = x.reshape(-1, orig_shape[-1])
        H = jax.nn.gelu(xf @ W1 + b1, approximate=False)
        probs = jax.nn.softmax((H @ Wg + bg) / TEMP, axis=-1)
        assign = jnp.argmax(probs, axis=-1)
        out = jnp.zeros_like(xf)
        for e in range(Wd.shape[0]):
            y = H @ Wd[e] + bd[e]
            sel = (assign == e)[:, None]
            out = out + jnp.where(sel, probs[:, e:e + 1] * y, 0.0)
        return out.reshape(orig_shape)

    def _L1_gnn_ref(h, weight, gamma, beta, src, dst, rel):
        import jax, jax.numpy as jnp
        import numpy as np
        N_NODES = 1250
        N_EDGES = 20000
        NUM_RELS = 8
        DIM = 256
        BN_EPS = 1e-05
        all_h = jnp.einsum('ni,rio->nro', h, weight)
        msg = all_h[src, rel]
        agg = jax.ops.segment_sum(msg, dst, num_segments=h.shape[0])
        mean = jnp.mean(agg, axis=0)
        var = jnp.mean(jnp.square(agg - mean), axis=0)
        out = (agg - mean) * jax.lax.rsqrt(var + BN_EPS) * gamma + beta
        return out

    def _L1_mix_ref(x, Wqkv, bqkv, Wproj, bproj, temperature):
        import jax, jax.numpy as jnp
        import numpy as np
        A, Bc, Cc = (0.5, 1.0, 1.0)
        H = 8
        EPS = 1e-12

        def _normalize(t):
            n = jnp.linalg.norm(t, axis=-1, keepdims=True)
            return t / jnp.maximum(n, EPS)
        B, N, C = x.shape
        D = C // H
        scale = float(D) ** 0.25
        qkv = (x @ Wqkv.T + bqkv).reshape(B, N, 3, H, D)
        qkv = jnp.transpose(qkv, (2, 0, 3, 1, 4))
        q, k, v = (qkv[0], qkv[1], qkv[2])
        q = q * scale
        v1 = jnp.concatenate([jnp.ones((B, H, N, 1), dtype=v.dtype), v], axis=-1)
        qn = _normalize(q) * (scale * temperature)
        kn = _normalize(k) * scale
        vN = v1 / N
        kv_mod = jnp.einsum('bhni,bhnj,bhne->bhije', kn, kn, vN)
        kv = jnp.einsum('bhnd,bhne->bhde', kn, vN)
        vsum = jnp.sum(vN, axis=-2)[:, :, None, :]
        y = A * jnp.einsum('bhni,bhnj,bhije->bhne', qn, qn, kv_mod) + scale ** 2 * Bc * jnp.einsum('bhnd,bhde->bhne', qn, kv) + scale ** 4 * Cc * vsum
        y_norm, y = (y[..., :1], y[..., 1:])
        y = y / y_norm
        out = jnp.transpose(y, (0, 2, 1, 3)).reshape(B, N, H * D)
        return out @ Wproj.T + bproj

    def _L1_ffn_ref(x, gamma, beta, Wr, br, W1, b1, W2, b2):
        import jax, jax.numpy as jnp
        import numpy as np
        E = 8
        K = 2
        D = 256
        H = 512
        DOUT = 256
        EPS = 1e-05
        mu = jnp.mean(x, axis=-1, keepdims=True)
        var = jnp.mean(jnp.square(x - mu), axis=-1, keepdims=True)
        xn = (x - mu) * jax.lax.rsqrt(var + EPS) * gamma + beta
        logits = jnp.einsum('bsd,de->bse', xn, Wr) + br
        top_vals, top_idx = jax.lax.top_k(logits, K)
        w = jax.nn.softmax(top_vals, axis=-1)
        w_full = jnp.einsum('bsk,bske->bse', w, jax.nn.one_hot(top_idx, E, dtype=w.dtype))
        y = jnp.zeros(x.shape[:-1] + (DOUT,), x.dtype)
        for e in range(E):
            h = jax.nn.gelu(jnp.einsum('bsd,dh->bsh', xn, W1[e]) + b1[e], approximate=False)
            y_e = jnp.einsum('bsh,hd->bsd', h, W2[e]) + b2[e]
            y = y + y_e * w_full[..., e, None]
        return y
    xn = _layernorm(x, axis=-1)
    x = x + _L0_gnn_ref(xn, L0_gnn_Wq, L0_gnn_Wk, L0_gnn_Wv, src, dst) + _L0_mix_ref(xn[None], L0_mix_w_qkv, L0_mix_b_qkv, L0_mix_norm_g, L0_mix_norm_b, L0_mix_w_fc1, L0_mix_b_fc1, L0_mix_w_fc2, L0_mix_b_fc2)[0]
    x = x + _L0_ffn_ref(_layernorm(x, axis=-1)[None], L0_ffn_W1, L0_ffn_b1, L0_ffn_Wg, L0_ffn_bg, L0_ffn_Wd, L0_ffn_bd)[0]
    xn = _layernorm(x, axis=-1)
    x = x + _L1_gnn_ref(xn, L1_gnn_weight, L1_gnn_gamma, L1_gnn_beta, src, dst, edge_type_8) + _L1_mix_ref(xn[None], L1_mix_Wqkv, L1_mix_bqkv, L1_mix_Wproj, L1_mix_bproj, L1_mix_temperature)[0]
    x = x + _L1_ffn_ref(_layernorm(x, axis=-1)[None], L1_ffn_gamma, L1_ffn_beta, L1_ffn_Wr, L1_ffn_br, L1_ffn_W1, L1_ffn_b1, L1_ffn_W2, L1_ffn_b2)[0]
    return x

_drawn_inputs = setup_inputs


def setup_inputs(seed=0):
    import zlib

    import numpy as np

    out = dict(_drawn_inputs(seed))
    spreads = {'L0_mix_b_qkv': (0.0, 0.1),
     'L0_mix_norm_g': (1.0, 0.6),
     'L0_mix_norm_b': (0.0, 0.8),
     'L0_mix_b_fc1': (0.0, 0.54),
     'L0_mix_b_fc2': (0.0, 0.1),
     'L0_ffn_b1': (0.0, 0.8),
     'L0_ffn_bg': (0.0, 0.771),
     'L0_ffn_bd': (0.0, 0.8),
     'L1_gnn_gamma': (1.0, 0.2),
     'L1_gnn_beta': (0.0, 0.297),
     'L1_mix_bqkv': (0.0, 0.565),
     'L1_mix_bproj': (0.0, 0.344),
     'L1_mix_temperature': (1.0, 0.6),
     'L1_ffn_br': (0.0, 0.461)}
    factors = {'L0_ffn_W1': 5.285,
     'L0_ffn_Wg': 5.644,
     'L0_ffn_Wd': 6.412,
     'L1_mix_Wqkv': 8.0,
     'L1_mix_Wproj': 4.233,
     'L1_ffn_gamma': 24.008,
     'L1_ffn_beta': 24.051,
     'L1_ffn_Wr': 2.765,
     'L1_ffn_b1': 49.687,
     'L1_ffn_b2': 8.0}
    for name, (base, spread) in spreads.items():
        noise = np.random.default_rng([zlib.crc32(name.encode()), seed]).standard_normal(out[name].shape)
        drawn = base * np.exp(spread * noise) if base else spread * noise
        out[name] = jnp.asarray(drawn.astype(out[name].dtype))
    for name, factor in factors.items():
        out[name] = (out[name] * factor).astype(out[name].dtype)
    return out
```

```python
import numpy as np
from contextlib import ExitStack, contextmanager

import concourse.bass as bass
from concourse import mybir

F32 = mybir.dt.float32
I32 = mybir.dt.int32
U32 = mybir.dt.uint32
ALU = mybir.AluOpType
ACT = mybir.ActivationFunctionType
AX = mybir.AxisListType

N = 3125
D = 256
TN = 125
NT = N // TN
P = 128
KD = D // P
E = 103125
UJ = 3
UE = TN * UJ
NU = E // UE
UC = 5
UP = NU // UC
NB = 4
NUP = NU + NB - 1
NPASS = -(-NU // NB)
HG, DK = 8, 32
HM, DM = 4, 64
R = 8
EPS = 1e-5
FM = 3 * D
CM = FM // P
F0, C0 = 1024, 8
X0 = 8
F1, C1 = 512, 4
NS = DK // 2 + 1
HH = 4
VE = DK + 1


class Chain:

    def __init__(self, eng, sem, per_step):
        self.eng, self.sem, self.per, self.step, self.n = eng, sem, per_step, 0, 0

    def at(self, step):
        assert self.n in (0, self.per), (self.n, self.per)
        self.step, self.n = step, 0

    def link(self, ins):
        self.n += 1
        ins.then_inc(self.sem, 1)
        self.eng.wait_ge(self.sem, self.step * self.per + self.n)


def pairs(eng, body):
    body(0, 0)
    body(0, 1)
    with eng.Fori(1, NT // 2) as i:
        body(i, 0)
        body(i, 1)
    body(NT // 2, 0)


def after(eng, sem, value):
    if not isinstance(value, int) or value > 0:
        eng.wait_ge(sem, value)


def bcast(ap1, n):
    return ap1.rearrange("(a f) -> a f", a=1).partition_broadcast(n) if hasattr(ap1, "partition_broadcast") else ap1


class Shared:
    pass


@contextmanager
def layer(nc, s):
    with ExitStack() as held:
        nums = []

        def new_sem(name):
            sem = held.enter_context(nc.semaphore(name))
            nums.append(sem.num)
            return sem
        s.new_sem = new_sem
        yield held
        assert sorted(nums) == list(range(min(nums), max(nums) + 1))
        nc.all_engine_barrier()
        nc.gpsimd.sem_clear(range(min(nums), max(nums) + 1))
        nc.all_engine_barrier()


def build_shared(nc, ctx, ins):
    s = Shared()
    s.sb = lambda name, shape, dt=F32: ctx.enter_context(nc.sbuf_tensor(name, shape, dt))
    s.x = s.sb("x_res", [TN, NT, D])
    s.y = s.sb("y_res", [TN, NT, D])
    s.ident = s.sb("ident", [P, P])
    s.srci = s.sb("srci", [TN, NUP, UJ], I32)
    s.reli = s.sb("reli", [TN, NUP, UJ], I32)
    s.dstf = s.sb("dstf", [TN, NUP, UJ])
    s.meta = s.sb("meta", [1, 3, NT], I32)
    s.iota_f = s.sb("iota_f", [TN, TN])
    s.iota_p = s.sb("iota_p", [TN, 1])
    s.mv = s.sb("mv", [TN, NT, 2])
    s.rstd = s.sb("rstd", [TN, NT])
    s.zero = s.sb("zero", [P, 512])
    dr = lambda name, shape: nc.dram_tensor(name, shape, F32, kind="Internal").ap()
    s.kv_d = dr("kv_d", [N, 2 * D])
    s.q_d = dr("q_d", [N, D])
    s.xnT_d = dr("xnT_d", [NT, P, KD, TN])
    s.h_d = dr("h_d", [N * R, D])
    s.dst_d = nc.dram_tensor("dst_d", [NUP * UE], I32, kind="Internal").ap()
    s.kv_gathered, s.rows_gathered = ([ctx.enter_context(nc.semaphore(f"{n}_gathered{a}")) for a in range(NB)]
                                      for n in ("kv", "rows"))
    return s


def build_layer0(nc, s, ctx):
    sb = lambda name, shape: ctx.enter_context(nc.sbuf_tensor(name, shape, F32))
    s.wqf = sb("wqf", [P, KD, D])
    s.bqf = sb("bqf", [TN, D])
    s.kvm = sb("kvm", [P, 2 * P])


def stage_prepare(nc, s, ins):
    with ExitStack() as ctx:
        sb = lambda name, shape, dt=F32: ctx.enter_context(nc.sbuf_tensor(name, shape, dt))
        raw = {k: sb("raw_" + k, [UP, UC, UE], I32) for k in ("dst", "src", "rel")}
        flt = {k: sb("flt_" + k, [UP, UC, UE]) for k in ("dst", "src", "rel")}
        mx = sb("mx", [UP, UC])
        mn = sb("mn", [UP, UC])
        b125 = sb("b125", [UP, NT])
        gup = sb("gup", [UP, UC])
        gdn = sb("gdn", [UP, UC])
        ov1 = sb("ov1", [UP, UC, NT])
        ov2 = sb("ov2", [UP, UC, NT])
        hl = sb("hl", [UP, UC, 2 * NT])
        red = sb("red", [2 * NT, 1])
        row = sb("row", [1, 2 * NT])
        m = sb("mrow", [1, 5, NT])
        npass = sb("npass", [1, NPASS])
        more = sb("more", [1, NT, NPASS])
        pad = sb("pad", [TN, (NB - 1) * UJ], I32)
        ps = [ctx.enter_context(nc.psum_tensor(f"prep_ps{i}", [P, 512], F32)) for i in range(4)]
        sem = lambda name: s.new_sem("p_" + name)
        s_x, s_raw = sem("x"), {k: sem("raw_" + k) for k in raw}
        s_const, s_iota, s_dst, s_pad = sem("const"), sem("iota"), sem("dst"), sem("pad")
        s_flt, s_tr, s_ev, s_hl, s_hlt, s_red, s_row, s_dch = (
            sem(n) for n in ("flt", "tr", "ev", "hl", "hlt", "red", "row", "dch"))
        order = ("dst", "src", "rel")
        target = {"dst": s.dstf, "src": s.srci, "rel": s.reli}
        with nc.Block() as block:
            @block.sync
            def _(sp):
                for k, a in (("dst", ins["dst"]), ("src", ins["src"]), ("rel", ins["edge_type_8"])):
                    sp.dma_start(raw[k][:, :, :], a.rearrange("(c p f) -> p c f", c=UC, p=UP)).then_inc(s_raw[k], 16)
                sp.dma_start(s.dst_d[0:E].rearrange("(p f) -> p f", p=TN), ins["dst"].rearrange("(p f) -> p f", p=TN)).then_inc(s_dst, 16)
                sp.wait_ge(s_pad, 4)
                sp.dma_start(s.dst_d[E:].rearrange("(p f) -> p f", p=TN), pad[:, :]).then_inc(s_dst, 16)
                sp.dma_start(s.x[:, :, :], ins["x"].rearrange("(t p) d -> p t d", p=TN)).then_inc(s_x, 16)
                sp.wait_ge(s_x, 16)
                sp.wait_ge(s_dst, 32)

            @block.gpsimd
            def _(pool):
                nc.gpsimd.iota(b125[:, :], pattern=[[TN, NT]], base=0, channel_multiplier=0,
                               allow_small_or_imprecise_dtypes=True).then_inc(s_iota, 1)
                nc.gpsimd.iota(gup[:, :], pattern=[[UP, UC]], base=1, channel_multiplier=1,
                               allow_small_or_imprecise_dtypes=True).then_inc(s_iota, 1)
                nc.gpsimd.iota(s.iota_f[:, :], pattern=[[1, TN]], base=0, channel_multiplier=0,
                               allow_small_or_imprecise_dtypes=True).then_inc(s_iota, 1)
                nc.gpsimd.iota(s.iota_p[:, :], pattern=[[0, 1]], base=0, channel_multiplier=1,
                               allow_small_or_imprecise_dtypes=True).then_inc(s_iota, 1)
                nc.gpsimd.memset(s.zero[:, :], 0.0).then_inc(s_iota, 1)
                nc.gpsimd.iota(npass[:, :], pattern=[[NB, NPASS]], base=0, channel_multiplier=0,
                               allow_small_or_imprecise_dtypes=True).then_inc(s_iota, 1)
                nc.gpsimd.memset(s.ident[:, :], 0.0).then_inc(s_const, 1)
                pool.wait_ge(s_const, 1)
                nc.gpsimd.affine_select(out=s.ident[:, :], in_=s.ident[:, :], compare_op=ALU.not_equal, fill=1.0,
                                        base=0, pattern=[[-1, P]], channel_multiplier=1).then_inc(s_const, 1)

            @block.vector
            def _(dve):
                ch = Chain(dve, s_dch, 100)
                nc.vector.memset(pad[:, :], -1).then_inc(s_pad, 1)
                nc.vector.memset(s.dstf[:, NU:NUP, :], -1.0).then_inc(s_pad, 1)
                nc.vector.memset(s.srci[:, NU:NUP, :], 0).then_inc(s_pad, 1)
                nc.vector.memset(s.reli[:, NU:NUP, :], 0).then_inc(s_pad, 1)
                for k in ("dst", "src"):
                    dve.wait_ge(s_raw[k], 16)
                    nc.vector.tensor_copy(flt[k][:, :, :], raw[k][:, :, :]).then_inc(s_flt, 1)
                dve.wait_ge(s_raw["rel"], 16)
                dve.wait_ge(s_flt, 2)
                nc.vector.scalar_tensor_tensor(out=flt["rel"][:, :, :], in0=flt["src"][:, :, :], scalar=float(R),
                                               in1=raw["rel"][:, :, :], op0=ALU.mult, op1=ALU.add).then_inc(s_flt, 1)
                ch.link(nc.vector.tensor_reduce(mx[:, :], flt["dst"][:, :, :], AX.X, ALU.max))
                ch.link(nc.vector.tensor_reduce(mn[:, :], flt["dst"][:, :, :], AX.X, ALU.min))
                ch.link(nc.vector.tensor_scalar(mn[:, :], mn[:, :], -(TN - 1.0), None, ALU.add))
                dve.wait_ge(s_iota, 6)
                ch.link(nc.vector.tensor_scalar(gdn[:, :], gup[:, :], -1.0, NU + 1.0, ALU.mult, ALU.add))
                for c in range(UC):
                    nc.vector.tensor_scalar(ov1[:, c, :], b125[:, :], mx[:, c:c + 1], None, ALU.is_le).then_inc(s_dch, 1)
                    ch.n += 1
                    ch.link(nc.vector.tensor_scalar(ov2[:, c, :], b125[:, :], mn[:, c:c + 1], None, ALU.is_ge))
                ch.link(nc.vector.tensor_tensor(ov1[:, :, :], ov1[:, :, :], ov2[:, :, :], ALU.mult))
                for c in range(UC):
                    nc.vector.tensor_scalar(hl[:, c, 0:NT], ov1[:, c, :], gup[:, c:c + 1], None, ALU.mult).then_inc(s_hl, 1)
                    nc.vector.tensor_scalar(hl[:, c, NT:2 * NT], ov1[:, c, :], gdn[:, c:c + 1], None, ALU.mult).then_inc(s_hl, 1)
                for n, (k, c) in enumerate((k, c) for k in order for c in range(UC)):
                    dve.wait_ge(s_tr, n + 1)
                    nc.vector.tensor_copy(target[k][:, c * UP:(c + 1) * UP, :].rearrange("p u j -> p j u"),
                                          ps[n % 2][0:TN, 0:UJ * UP].rearrange("p (j u) -> p j u", j=UJ)).then_inc(s_ev, 1)
                dve.wait_ge(s_hlt, 1)
                nc.vector.tensor_reduce(red[:, :], ps[2][0:2 * NT, 0:UC * UP], AX.X, ALU.max).then_inc(s_red, 1)
                dve.wait_ge(s_row, 1)
                ch.link(nc.vector.tensor_copy(row[:, :], ps[3][0:1, 0:2 * NT]))
                ch.link(nc.vector.tensor_scalar(m[:, 0, :], row[:, NT:2 * NT], -1.0, float(NU), ALU.mult, ALU.add))
                ch.link(nc.vector.tensor_scalar(m[:, 0, :], m[:, 0, :], NU - 1.0, None, ALU.min))
                ch.link(nc.vector.tensor_scalar(m[:, 3, :], m[:, 0, :], 1.0, None, ALU.add))
                ch.link(nc.vector.tensor_tensor(m[:, 1, :], row[:, 0:NT], m[:, 3, :], ALU.max))
                ch.link(nc.vector.tensor_tensor(m[:, 3, :], m[:, 1, :], m[:, 0, :], ALU.subtract))
                ch.link(nc.vector.tensor_tensor(more[:, :, :], npass[:, :].unsqueeze(1).to_broadcast([1, NT, NPASS]),
                                                m[:, 3, :].unsqueeze(2).to_broadcast([1, NT, NPASS]), ALU.is_lt))
                ch.link(nc.vector.tensor_reduce(m[:, 3, :], more[:, :, :], AX.X, ALU.add))
                ch.link(nc.vector.memset(m[:, 4, :], 0.0))
                for b in range(1, NT):
                    ch.link(nc.vector.tensor_tensor(m[:, 4, b:b + 1], m[:, 4, b - 1:b], m[:, 3, b - 1:b], ALU.add))
                ch.link(nc.vector.tensor_copy(s.meta[:, 0, :], m[:, 4, :]))
                ch.link(nc.vector.tensor_tensor(m[:, 3, :], m[:, 4, :], m[:, 3, :], ALU.add))
                ch.link(nc.vector.tensor_copy(s.meta[:, 1, :], m[:, 3, :]))
                ch.link(nc.vector.scalar_tensor_tensor(out=m[:, 2, :], in0=m[:, 4, :], scalar=-float(NB), in1=m[:, 0, :],
                                                       op0=ALU.mult, op1=ALU.add))
                ch.link(nc.vector.tensor_copy(s.meta[:, 2, :], m[:, 2, :]))

            @block.tensor
            def _(pe):
                pe.wait_ge(s_const, 2)
                for n, (k, c) in enumerate((k, c) for k in order for c in range(UC)):
                    pe.wait_ge(s_flt, order.index(k) + 1)
                    if n >= 2:
                        pe.wait_ge(s_ev, n - 1)
                    for j in range(UJ):
                        last = nc.tensor.transpose(ps[n % 2][0:TN, j * UP:(j + 1) * UP],
                                                   flt[k][:, c, :].rearrange("p (e j) -> p e j", j=UJ)[:, :, j],
                                                   s.ident[0:UP, 0:UP])
                    last.then_inc(s_tr, 1)
                pe.wait_ge(s_hl, 2 * UC)
                for c in range(UC):
                    last = nc.tensor.transpose(ps[2][0:2 * NT, c * UP:(c + 1) * UP], hl[:, c, :], s.ident[0:UP, 0:UP])
                last.then_inc(s_hlt, 1)
                pe.wait_ge(s_red, 1)
                nc.tensor.transpose(ps[3][0:1, 0:2 * NT], red[:, :], s.ident[0:2 * NT, 0:2 * NT]).then_inc(s_row, 1)


def stage_ln(nc, s, src, tag):
    with ExitStack() as ctx:
        st = ctx.enter_context(nc.sbuf_tensor(f"st_{tag}", [TN, NT, 6], F32))
        sd = ctx.enter_context(nc.sbuf_tensor(f"sd_{tag}", [TN, NT], F32))
        s_st, s_var, s_sd, s_mv = (s.new_sem(f"ln_{n}_{tag}") for n in ("st", "var", "sd", "mv"))
        with nc.Block() as block:
            @block.vector
            def _(dve):
                with dve.Fori(0, NT) as t:
                    nc.vector.bn_stats(st[:, bass.ds(t, 1), :], src[:, bass.ds(t, 1), :]).then_inc(s_st, 1)
                dve.wait_ge(s_st, NT)
                for t in range(NT):
                    nc.vector.bn_aggr(s.mv[:, t, :], st[:, t, :]).then_inc(s_mv, 1)
                dve.wait_ge(s_mv, NT)
                nc.vector.tensor_scalar(sd[:, :], s.mv[:, :, 1], EPS, None, ALU.add).then_inc(s_var, 1)
                dve.wait_ge(s_sd, 1)
                nc.vector.reciprocal(s.rstd[:, :], sd[:, :])

            @block.scalar
            def _(act):
                act.wait_ge(s_var, 1)
                nc.scalar.activation(sd[:, :], sd[:, :], ACT.Sqrt).then_inc(s_sd, 1)


def stage_project(nc, s, ins):
    W = 5 * D
    with ExitStack() as ctx:
        sb = lambda name, shape, dt=F32: ctx.enter_context(nc.sbuf_tensor(name, shape, dt))
        sem = lambda name: s.new_sem("a_" + name)
        pb = lambda name: ctx.enter_context(nc.psum_tensor(name, [P, 512], F32))
        w = sb("w_proj", [P, KD, W])
        bias = sb("b_proj", [TN, 2 * D])
        xs = [sb(f"xs{i}", [TN, D]) for i in range(2)]
        xT = [sb(f"xT{i}", [P, KD, TN]) for i in range(2)]
        kvs = [sb(f"kvs{i}", [TN, 2 * D]) for i in range(2)]
        qs = [sb(f"qs{i}", [TN, D]) for i in range(2)]
        km = [sb(f"km{i}", [TN, 2 * D]) for i in range(2)]
        psT = [pb(f"psT{i}") for i in range(2)]
        psKV, psQ, psM, psA = (pb(n) for n in ("psKV", "psQ", "psM", "psA"))
        s_w, s_b, s_xs, s_tr, s_xT, s_kv, s_q, s_m, s_kvs, s_qs, s_km, s_y, s_acc, s_a0 = (
            sem(n) for n in ("w", "b", "xs", "tr", "xT", "kv", "q", "m", "kvs", "qs", "km", "y", "acc", "a0"))
        s_xTo, s_kvo, s_qo = ([sem(f"{n}{i}") for i in range(2)] for n in ("xTo", "kvo", "qo"))
        with nc.Block() as block:
            @block.sync
            def _(sp):
                sp.dma_start(w[:, :, 0:D], ins["L0_gnn_Wk"].rearrange("(k p) n -> p k n", p=P)).then_inc(s_w, 16)
                sp.dma_start(w[:, :, D:2 * D], ins["L0_gnn_Wv"].rearrange("(k p) n -> p k n", p=P)).then_inc(s_w, 16)
                sp.dma_start(w[:, :, 2 * D:3 * D], ins["L0_gnn_Wq"].rearrange("(k p) n -> p k n", p=P)).then_inc(s_w, 16)
                sp.dma_start(w[:, :, 3 * D:5 * D],
                             ins["L0_mix_w_qkv"][:, D:3 * D].rearrange("(k p) n -> p k n", p=P)).then_inc(s_w, 16)
                sp.dma_start(bias[:, :], ins["L0_mix_b_qkv"][D:3 * D].partition_broadcast(TN)).then_inc(s_b, 16)

                def store(i, k):
                    t = 2 * i + k
                    sp.wait_ge(s_xT, t + 1)
                    sp.dma_start(s.xnT_d[bass.ds(t, 1)].rearrange("a p k n -> p (a k) n"), xT[k][:, :, :]).then_inc(s_xTo[k], 16)
                    sp.wait_ge(s_kvs, t + 1)
                    sp.dma_start(s.kv_d[bass.ds(t * TN, TN), :], kvs[k][:, :]).then_inc(s_kvo[k], 16)
                    sp.wait_ge(s_qs, t + 1)
                    sp.dma_start(s.q_d[bass.ds(t * TN, TN), :], qs[k][:, :]).then_inc(s_qo[k], 16)
                pairs(sp, store)
                for k in range(2):
                    for sm in (s_xTo[k], s_kvo[k], s_qo[k]):
                        sp.wait_ge(sm, 16 * (13 - k))

            @block.vector
            def _(dve):
                def norm(i, k):
                    t = 2 * i + k
                    after(dve, s_y, 2 * i)
                    nc.vector.tensor_scalar(xs[k][:, :], s.x[:, bass.ds(t, 1), :].rearrange("p a d -> p (a d)"),
                                            s.mv[:, bass.ds(t, 1), 0], s.rstd[:, bass.ds(t, 1)],
                                            ALU.subtract, ALU.mult).then_inc(s_xs, 1)
                    dve.wait_ge(s_tr, t + 1)
                    after(dve, s_xTo[k], 16 * i)
                    nc.vector.tensor_copy(xT[k][:, :, :], psT[k][:, 0:KD * TN].rearrange("p (k n) -> p k n", k=KD)).then_inc(s_xT, 1)
                    dve.wait_ge(s_q, t + 1)
                    after(dve, s_qo[k], 16 * i)
                    nc.vector.tensor_copy(qs[k][:, :], psQ[0:TN, 0:D]).then_inc(s_qs, 1)
                    dve.wait_ge(s_b, 16)
                    dve.wait_ge(s_m, t + 1)
                    after(dve, s_acc, 2 * i)
                    nc.vector.tensor_tensor(km[k][:, :], psM[0:TN, :], bias[:, :], ALU.add).then_inc(s_km, 1)
                pairs(dve, norm)
                dve.wait_ge(s_acc, NT + 1)
                nc.vector.tensor_copy(s.kvm[:, :], psA[:, 0:2 * P])

            @block.scalar
            def _(act):
                def evac(i, k):
                    t = 2 * i + k
                    act.wait_ge(s_xs, t + 1)
                    nc.scalar.activation(s.y[:, bass.ds(t, 1), :].rearrange("p a d -> p (a d)"), xs[k][:, :], ACT.Copy).then_inc(s_y, 1)
                    act.wait_ge(s_kv, t + 1)
                    after(act, s_kvo[k], 16 * i)
                    nc.scalar.activation(kvs[k][:, :], psKV[0:TN, :], ACT.Copy).then_inc(s_kvs, 1)
                pairs(act, evac)

            @block.tensor
            def _(pe):
                nc.tensor.matmul(psA[:, 0:2 * P], s.zero[0:TN, 0:P], s.zero[0:TN, 0:2 * P], start=True, stop=False)
                pe.wait_ge(s_w, 64)

                def tile(i, k):
                    t = 2 * i + k
                    pe.wait_ge(s_xs, t + 1)
                    for c in range(KD):
                        last = nc.tensor.transpose(psT[k][:, c * TN:(c + 1) * TN], xs[k][:, c * P:(c + 1) * P], s.ident[0:TN, 0:TN])
                    last.then_inc(s_tr, 1)
                    pe.wait_ge(s_xT, t + 1)
                    for ps, lo, hi, free, done in ((psKV, 0, 2 * D, s_kvs, s_kv), (psQ, 2 * D, 3 * D, s_qs, s_q), (psM, 3 * D, 5 * D, s_km, s_m)):
                        after(pe, free, t)
                        for c in range(KD):
                            last = nc.tensor.matmul(ps[0:TN, 0:hi - lo], xT[k][:, c, :], w[:, c, lo:hi], start=(c == 0), stop=(c == KD - 1))
                        last.then_inc(done, 1)
                    pe.wait_ge(s_km, t + 1)
                    for h in range(2):
                        last = nc.tensor.matmul(psA[:, h * P:(h + 1) * P], km[k][:, h * P:(h + 1) * P],
                                                km[k][:, D + h * P:D + (h + 1) * P], start=False, stop=False)
                    last.then_inc(s_acc, 1)
                pairs(pe, tile)
                nc.tensor.matmul(psA[:, 0:2 * P], s.zero[0:TN, 0:P], s.zero[0:TN, 0:2 * P], start=False, stop=True).then_inc(s_acc, 1)


def each_block(nc, eng, s, start, one_pass, end):
    with eng.Fori(0, NT) as b:
        first = eng.value_load(s.meta[0:1, 0, bass.ds(b, 1)], min_val=0, max_val=NPASS * NT)
        stop = eng.value_load(s.meta[0:1, 1, bass.ds(b, 1)], min_val=1, max_val=NPASS * NT)
        shift = eng.value_load(s.meta[0:1, 2, bass.ds(b, 1)], min_val=-NB * NPASS * NT, max_val=NU - 1)
        start(b)
        with eng.Fori(first, stop) as n:
            g = nc.s_assert_within(n * NB + shift, 0, NU - 1, skip_runtime_bounds_check_because=(
                "a pass starts below its block's last unit, and that is at most NU - 1"))
            one_pass(b, g, n)
        end(b)


def stage_attention(nc, s, ins):
    CLIP = 5.0 * float(np.sqrt(DK))
    W = D + HG
    with ExitStack() as ctx:
        sb = lambda name, shape, dt=F32: ctx.enter_context(nc.sbuf_tensor(name, shape, dt))
        sem = lambda name: s.new_sem("g_" + name)
        q = sb("q_all", [TN, NT, D])
        node = sb("node", [TN, 1])
        units = []
        for a in range(NB):
            u = Shared()
            u.a = a
            u.drow = sb(f"drow{a}", [TN, UE], I32)
            u.idx = sb(f"idx{a}", [TN, UJ], I32)
            u.kv = sb(f"kv{a}", [TN, UJ, 2 * D])
            u.oT = sb(f"oT{a}", [TN, UJ, TN])
            u.oh = sb(f"oh{a}", [TN, UJ, TN])
            u.prod = sb(f"prod{a}", [TN, UJ, D])
            u.red = sb(f"red{a}", [TN, UJ, HG])
            u.wv = sb(f"wv{a}", [TN, UJ, W])
            u.s_kv = s.kv_gathered[a]
            u.s_row, u.s_used, u.s_idx, u.s_oT, u.s_g, u.s_clip, u.s_sc, u.s_wv, u.s_sct, u.s_ot, u.s_oh = (
                sem(f"{name}{a}") for name in ("row", "used", "idx", "oT", "g", "clip", "sc", "wv", "sct", "ot", "oh"))
            units.append(u)
        zr = sb("zr", [TN, HG])
        gat = sb("gat", [TN, D])
        psG = [ctx.enter_context(nc.psum_tensor(f"psG{i}", [P, 1024], F32)) for i in range(2)]
        psH = [ctx.enter_context(nc.psum_tensor(f"g_psH{i}", [P, 512], F32)) for i in range(2)]
        psO = ctx.enter_context(nc.psum_tensor("psO", [P, 512], F32))
        s_q, s_blk, s_out, s_dch, s_bch, s_go, s_prod = (sem(n) for n in ("q", "blk", "out", "dch", "bch", "go", "prod"))
        with nc.Block() as block:
            @block.sync
            def _(sp):
                sp.dma_start(q[:, :, :], s.q_d.rearrange("(t p) d -> p t d", p=TN)).then_inc(s_q, 16)

                def load(b, g, n):
                    for u in units:
                        sp.wait_ge(u.s_used, n + 1)
                        sp.dma_start(u.drow[:, :], s.dst_d[bass.ds((g + u.a) * UE, UE)].partition_broadcast(TN)).then_inc(u.s_row, 16)
                each_block(nc, sp, s, lambda b: None, load, lambda b: None)

            @block.gpsimd
            def _(pool):
                def gather(b, g, n):
                    for u in units:
                        pool.wait_ge(u.s_wv, n + 1)
                        nc.gpsimd.tensor_copy(u.idx[:, :], s.srci[:, bass.ds(g + u.a, 1), :]).then_inc(u.s_idx, 1)
                        pool.wait_ge(u.s_idx, n + 1)
                        pool.sem_inc(s_go, 1)
                        for j in range(UJ):
                            nc.gpsimd.indirect_dma_start(
                                out=u.kv[:, j, :], out_offset=None, in_=s.kv_d,
                                in_offset=bass.IndirectOffsetOnAxis(ap=u.idx[:, j:j + 1], axis=0)).then_inc(u.s_kv, 16)
                each_block(nc, pool, s, lambda b: None, gather, lambda b: None)

            @block.vector
            def _(dve):
                for u in units:
                    dve.sem_inc(u.s_used, 1)
                    dve.sem_inc(u.s_wv, 1)
                nc.vector.tensor_copy(node[:, :], s.iota_p[:, :]).then_inc(s_bch, 1)
                dve.wait_ge(s_bch, 1)
                ch = Chain(dve, s_dch, 2 * NB)

                def onehot(n, u):
                    dve.wait_ge(u.s_row, 16 * n + 16)
                    nc.vector.tensor_scalar(u.oT[:, :, :], u.drow[:, :].rearrange("p (e j) -> p j e", j=UJ),
                                            node[:, 0:1], None, ALU.is_equal).then_inc(u.s_oT, 1)
                    dve.wait_ge(u.s_oT, n + 1)
                    dve.sem_inc(u.s_used, 1)

                def scores(n, u):
                    dve.wait_ge(u.s_kv, 16 * UJ * n + 16 * UJ)
                    dve.wait_ge(u.s_g, n + 1)
                    ch.link(nc.vector.tensor_tensor(u.prod[:, :, :], u.kv[:, :, 0:D],
                                                    turn_of(psG, u.a)[0:TN, 0:UJ * D].rearrange("p (j d) -> p j d", d=D), ALU.mult))
                    dve.sem_inc(s_prod, 1)
                    ch.link(nc.vector.tensor_reduce(u.red[:, :, :], u.prod[:, :, :].rearrange("p j (h d) -> p j h d", h=HG),
                                                    AX.X, ALU.add))
                    dve.wait_ge(u.s_sct, n + 1)
                    nc.vector.tensor_scalar(u.red[:, :, :], u.red[:, :, :], -CLIP, CLIP, ALU.max, ALU.min).then_inc(u.s_clip, 1)

                def weigh(n, u):
                    dve.wait_ge(u.s_sc, n + 1)
                    nc.vector.tensor_tensor(u.wv[:, :, 0:D].rearrange("p j (h d) -> p j h d", h=HG),
                                            u.kv[:, :, D:2 * D].rearrange("p j (h d) -> p j h d", h=HG),
                                            u.wv[:, :, D:W].unsqueeze(3).to_broadcast([TN, UJ, HG, DK]),
                                            ALU.mult).then_inc(u.s_wv, 1)

                def one_pass(b, g, n):
                    ch.at(n)
                    onehot(n, units[0])
                    onehot(n, units[1])
                    for u in units:
                        if u.a + 2 < NB:
                            onehot(n, units[u.a + 2])
                        scores(n, u)
                        if u.a >= 1:
                            weigh(n, units[u.a - 1])
                    weigh(n, units[-1])

                def end(b):
                    dve.wait_ge(s_blk, b + 1)
                    nc.vector.tensor_scalar(zr[:, :], psO[0:TN, D:W], 1e-9, None, ALU.add).then_inc(s_bch, 1)
                    dve.wait_ge(s_bch, 3 * b + 2)
                    nc.vector.reciprocal(zr[:, :], zr[:, :]).then_inc(s_bch, 1)
                    dve.wait_ge(s_bch, 3 * b + 3)
                    nc.vector.tensor_tensor(gat[:, :].rearrange("p (h d) -> p h d", h=HG),
                                            psO[0:TN, 0:D].rearrange("p (h d) -> p h d", h=HG),
                                            zr[:, :].unsqueeze(2).to_broadcast([TN, HG, DK]), ALU.mult).then_inc(s_out, 1)
                    dve.wait_ge(s_out, b + 1)
                    nc.vector.tensor_tensor(flat(s.x[:, bass.ds(b, 1), :]), flat(s.x[:, bass.ds(b, 1), :]), gat[:, :], ALU.add)
                    nc.vector.tensor_scalar(node[:, :], node[:, :], float(TN), None, ALU.add).then_inc(s_bch, 1)
                    dve.wait_ge(s_bch, 3 * b + 4)
                each_block(nc, dve, s, lambda b: None, one_pass, end)

            @block.scalar
            def _(act):
                def one_pass(b, g, n):
                    for u in units:
                        act.wait_ge(u.s_sct, n + 1)
                        act.wait_ge(u.s_ot, n + 1)
                        nc.scalar.activation(u.oh[:, :, :], turn_of(psH, u.a)[0:TN, 0:UJ * TN].rearrange("p (j d) -> p j d", j=UJ),
                                             ACT.Copy).then_inc(u.s_oh, 1)
                        act.wait_ge(u.s_clip, n + 1)
                        nc.scalar.activation(u.wv[:, :, D:W], u.red[:, :, :], ACT.Exp, scale=1.0 / float(np.sqrt(DK))).then_inc(u.s_sc, 1)
                each_block(nc, act, s, lambda b: None, one_pass, lambda b: None)

            @block.tensor
            def _(pe):
                for u in units:
                    pe.sem_inc(u.s_sct, 1)
                pe.wait_ge(s_q, 16)

                def start(b):
                    pe.wait_ge(s_bch, 3 * b + 1)
                    nc.tensor.matmul(psO[0:TN, 0:W], s.zero[0:TN, 0:TN], s.zero[0:TN, 0:W], start=True, stop=False)

                def spread(b, n, u):
                    pe.wait_ge(u.s_oT, n + 1)
                    if u.a >= len(psG):
                        pe.wait_ge(s_prod, NB * n + u.a - len(psG) + 1)
                    for j in range(UJ):
                        last = nc.tensor.matmul(turn_of(psG, u.a)[0:TN, j * D:(j + 1) * D], u.oT[:, j, :],
                                                flat(q[:, bass.ds(b, 1), :]), start=True, stop=True)
                    last.then_inc(u.s_g, 1)
                    if u.a >= len(psH):
                        pe.wait_ge(units[u.a - len(psH)].s_oh, n + 1)
                    for j in range(UJ):
                        last = nc.tensor.transpose(turn_of(psH, u.a)[0:TN, j * TN:(j + 1) * TN], u.oT[:, j, :], s.ident[0:TN, 0:TN])
                    last.then_inc(u.s_ot, 1)

                def one_pass(b, g, n):
                    spread(b, n, units[0])
                    spread(b, n, units[1])
                    for u in units:
                        if u.a + 2 < NB:
                            spread(b, n, units[u.a + 2])
                        pe.wait_ge(u.s_oh, n + 1)
                        pe.wait_ge(u.s_wv, n + 2)
                        for j in range(UJ):
                            last = nc.tensor.matmul(psO[0:TN, 0:W], u.oh[:, j, :], u.wv[:, j, :], start=False, stop=False)
                        last.then_inc(u.s_sct, 1)

                def end(b):
                    nc.tensor.matmul(psO[0:TN, 0:W], s.zero[0:TN, 0:TN], s.zero[0:TN, 0:W], start=False, stop=True).then_inc(s_blk, 1)
                each_block(nc, pe, s, start, one_pass, end)


def turn_of(buffers, n):
    return buffers[n % len(buffers)]


def flat(ap):
    return ap.rearrange("p a d -> p (a d)")


def stage_fold(nc, s, ins):
    with ExitStack() as ctx:
        sb = lambda name, shape, dt=F32: ctx.enter_context(nc.sbuf_tensor(name, shape, dt))
        sem = lambda name: s.new_sem("f_" + name)
        pb = lambda name: ctx.enter_context(nc.psum_tensor(name, [P, 512], F32))
        wq = sb("wq_raw", [P, KD, D])
        wqT = sb("wqT", [P, 2, D])
        bq = sb("bq_col", [P, 2])
        bqw = sb("bq_wide", [P, 2, TN])
        a = sb("attn", [P, 2, DM])
        amx = sb("attn_max", [P, 2])
        bd = sb("attn_diag", [P, 2, P])
        bt = sb("attn_turned", [P, 2, P])
        psW, psB, psF, psb = (pb(n) for n in ("psW", "psB", "psF", "psb"))
        s_w, s_b, s_wt, s_wte, s_sub, s_exp, s_bd, s_bt, s_bte, s_f, s_dch = (
            sem(n) for n in ("w", "b", "wt", "wte", "sub", "exp", "bd", "bt", "bte", "f", "dch"))
        with nc.Block() as block:
            @block.sync
            def _(sp):
                sp.dma_start(wq[:, :, :], ins["L0_mix_w_qkv"][:, 0:D].rearrange("(k p) n -> p k n", p=P)).then_inc(s_w, 16)
                sp.dma_start(bq[:, :], ins["L0_mix_b_qkv"][0:D].rearrange("(c p) -> p c", p=P)).then_inc(s_b, 16)

            @block.vector
            def _(dve):
                ch = Chain(dve, s_dch, 100)
                ch.link(nc.vector.memset(bd[:, :, :], 0.0))
                kv = s.kvm[:, :].rearrange("p (c n) -> p c n", c=2)
                for h in range(2):
                    rows = slice(h * DM, (h + 1) * DM)
                    ch.link(nc.vector.tensor_copy(a[rows, :, :], kv[rows, :, h * DM:(h + 1) * DM]))
                ch.link(nc.vector.tensor_reduce(amx[:, :], a[:, :, :], AX.X, ALU.max))
                nc.vector.tensor_tensor(a[:, :, :], a[:, :, :], amx[:, :].unsqueeze(2).to_broadcast([P, 2, DM]),
                                        ALU.subtract).then_inc(s_sub, 1)
                dve.wait_ge(s_exp, 1)
                ch.link(nc.vector.tensor_reduce(amx[:, :], a[:, :, :], AX.X, ALU.add))
                ch.link(nc.vector.reciprocal(amx[:, :], amx[:, :]))
                for h in range(2):
                    rows = slice(h * DM, (h + 1) * DM)
                    nc.vector.tensor_tensor(bd[rows, :, h * DM:(h + 1) * DM], a[rows, :, :],
                                            amx[rows, :].unsqueeze(2).to_broadcast([DM, 2, DM]), ALU.mult).then_inc(s_bd, 1)
                dve.wait_ge(s_wt, 1)
                nc.vector.tensor_copy(wqT[:, :, :], psW[:, :].rearrange("p (c n) -> p c n", c=2)).then_inc(s_wte, 1)
                dve.wait_ge(s_b, 16)
                nc.vector.tensor_copy(bqw[:, :, :], bq[:, :].unsqueeze(2).to_broadcast([P, 2, TN])).then_inc(s_wte, 1)
                dve.wait_ge(s_bt, 1)
                nc.vector.tensor_copy(bt[:, :, :], psB[:, 0:2 * P].rearrange("p (c n) -> p c n", c=2)).then_inc(s_bte, 1)
                dve.wait_ge(s_f, 1)
                nc.vector.tensor_copy(s.wqf[:, :, :], psF[:, :].rearrange("p (k n) -> p k n", k=KD))
                nc.vector.tensor_copy(s.bqf[:, :], psb[0:TN, 0:D])

            @block.scalar
            def _(act):
                act.wait_ge(s_sub, 1)
                nc.scalar.activation(a[:, :, :], a[:, :, :], ACT.Exp, scale=float(DM) ** -0.5).then_inc(s_exp, 1)

            @block.tensor
            def _(pe):
                pe.wait_ge(s_w, 16)
                for c in range(2):
                    for k in range(KD):
                        last = nc.tensor.transpose(psW[:, c * D + k * P:c * D + (k + 1) * P], wq[:, k, c * P:(c + 1) * P], s.ident[:, :])
                last.then_inc(s_wt, 1)
                pe.wait_ge(s_bd, 2)
                for c in range(2):
                    last = nc.tensor.transpose(psB[:, c * P:(c + 1) * P], bd[:, c, :], s.ident[:, :])
                last.then_inc(s_bt, 1)
                pe.wait_ge(s_wte, 2)
                pe.wait_ge(s_bte, 1)
                for c in range(2):
                    for k in range(KD):
                        nc.tensor.matmul(psF[:, k * D + c * P:k * D + (c + 1) * P], wqT[:, c, k * P:(k + 1) * P], bt[:, c, :], start=True, stop=True)
                    last = nc.tensor.matmul(psb[0:TN, c * P:(c + 1) * P], bqw[:, c, :], bt[:, c, :], start=True, stop=True)
                last.then_inc(s_f, 1)


def stage_mix_attend(nc, s, ins):
    with ExitStack() as ctx:
        sb = lambda name, shape, dt=F32: ctx.enter_context(nc.sbuf_tensor(name, shape, dt))
        sem = lambda name: s.new_sem("m_" + name)
        xT = [sb(f"mxT{i}", [P, KD, TN]) for i in range(2)]
        att = [sb(f"att{i}", [TN, D]) for i in range(2)]
        psF = [ctx.enter_context(nc.psum_tensor(f"mpsF{i}", [P, 512], F32)) for i in range(2)]
        s_f, s_att, s_y = (sem(n) for n in ("f", "att", "y"))
        s_xT = [sem(f"xT{i}") for i in range(2)]
        with nc.Block() as block:
            @block.sync
            def _(sp):
                def load(i, k):
                    t = 2 * i + k
                    after(sp, s_f, 2 * i)
                    sp.dma_start(xT[k][:, :, :], s.xnT_d[bass.ds(t, 1)].rearrange("a p k n -> p (a k) n")).then_inc(s_xT[k], 16)
                pairs(sp, load)

            @block.tensor
            def _(pe):
                def tile(i, k):
                    t = 2 * i + k
                    pe.wait_ge(s_xT[k], 16 * i + 16)
                    after(pe, s_att, 2 * i)
                    for c in range(KD):
                        last = nc.tensor.matmul(psF[k][0:TN, 0:D], xT[k][:, c, :], s.wqf[:, c, :], start=(c == 0), stop=(c == KD - 1))
                    last.then_inc(s_f, 1)
                pairs(pe, tile)

            @block.vector
            def _(dve):
                def tile(i, k):
                    t = 2 * i + k
                    dve.wait_ge(s_f, t + 1)
                    nc.vector.tensor_tensor(att[k][:, :], psF[k][0:TN, 0:D], s.bqf[:, :], ALU.add).then_inc(s_att, 1)
                    dve.wait_ge(s_att, t + 1)
                    nc.vector.tensor_tensor(flat(s.y[:, bass.ds(t, 1), :]), flat(s.y[:, bass.ds(t, 1), :]), att[k][:, :], ALU.add)
                pairs(dve, tile)


def stage_mix_mlp(nc, s, ins):
    with ExitStack() as ctx:
        sb = lambda name, shape, dt=F32: ctx.enter_context(nc.sbuf_tensor(name, shape, dt))
        sem = lambda name: s.new_sem("n_" + name)
        pb = lambda name: ctx.enter_context(nc.psum_tensor("n_" + name, [P, 512], F32))
        w1 = sb("w_fc1", [P, KD, FM])
        w2 = sb("w_fc2", [P, CM, D])
        b1 = sb("b_fc1", [P, CM])
        b2 = sb("b_fc2", [TN, D])
        g = sb("norm_g", [P, KD])
        b = sb("norm_b", [P, KD])
        xs = [sb(f"n_xs{i}", [TN, D]) for i in range(2)]
        xT = [sb(f"n_xT{i}", [P, KD, TN]) for i in range(2)]
        hT = [sb(f"n_hT{i}", [P, CM, TN]) for i in range(2)]
        o = [sb(f"n_o{i}", [TN, D]) for i in range(2)]
        psT = [pb(f"psT{i}") for i in range(2)]
        psH = [pb(f"psH{i}") for i in range(2)]
        psY = [pb(f"psY{i}") for i in range(2)]
        s_w, s_xs, s_tr, s_xT, s_h, s_hT, s_y, s_o, s_dch = (sem(n) for n in ("w", "xs", "tr", "xT", "h", "hT", "y", "o", "dch"))
        HB = CM // 2
        with nc.Block() as block:
            @block.sync
            def _(sp):
                sp.dma_start(w1[:, :, :], ins["L0_mix_w_fc1"].rearrange("(k p) n -> p k n", p=P)).then_inc(s_w, 16)
                sp.dma_start(w2[:, :, :], ins["L0_mix_w_fc2"].rearrange("(c p) n -> p c n", p=P)).then_inc(s_w, 16)
                sp.dma_start(b1[:, :], ins["L0_mix_b_fc1"].rearrange("(c p) -> p c", p=P)).then_inc(s_w, 16)
                sp.dma_start(g[:, :], ins["L0_mix_norm_g"].rearrange("(c p) -> p c", p=P)).then_inc(s_w, 16)
                sp.dma_start(b[:, :], ins["L0_mix_norm_b"].rearrange("(c p) -> p c", p=P)).then_inc(s_w, 16)
                sp.dma_start(b2[:, :], ins["L0_mix_b_fc2"].partition_broadcast(TN)).then_inc(s_w, 16)

            @block.vector
            def _(dve):
                ch = Chain(dve, s_dch, 2)
                dve.wait_ge(s_w, 96)

                def norm(i, k, t):
                    after(dve, s_tr, 2 * i)
                    nc.vector.tensor_scalar(xs[k][:, :], flat(s.y[:, bass.ds(t, 1), :]), s.mv[:, bass.ds(t, 1), 0],
                                            s.rstd[:, bass.ds(t, 1)], ALU.subtract, ALU.mult).then_inc(s_xs, 1)

                def tile(i, k):
                    t = 2 * i + k
                    ch.at(t)
                    norm(i, k, t)
                    dve.wait_ge(s_y, t + 1)
                    ch.link(nc.vector.tensor_tensor(o[k][:, :], psY[k][0:TN, 0:D], b2[:, :], ALU.add))
                    ch.link(nc.vector.tensor_tensor(o[k][:, :], o[k][:, :], flat(s.y[:, bass.ds(t, 1), :]), ALU.add))
                    nc.vector.tensor_tensor(flat(s.x[:, bass.ds(t, 1), :]), flat(s.x[:, bass.ds(t, 1), :]), o[k][:, :],
                                            ALU.add).then_inc(s_o, 1)
                pairs(dve, tile)

            @block.scalar
            def _(act):
                act.wait_ge(s_w, 96)

                def tile(i, k):
                    t = 2 * i + k
                    act.wait_ge(s_tr, t + 1)
                    for c in range(KD):
                        nc.scalar.activation(xT[k][:, c, :], psT[k][:, c * TN:(c + 1) * TN], ACT.Identity,
                                             bias=b[:, c:c + 1], scale=g[:, c:c + 1]).then_inc(s_xT, 1)
                    for c in range(CM):
                        act.wait_ge(s_h, 2 * t + 1 + c // HB)
                        nc.scalar.activation(hT[k][:, c, :], psH[c // HB][:, (c % HB) * TN:(c % HB + 1) * TN], ACT.Gelu,
                                             bias=b1[:, c:c + 1]).then_inc(s_hT, 1)
                pairs(act, tile)

            @block.tensor
            def _(pe):
                pe.wait_ge(s_w, 96)

                def tile(i, k):
                    t = 2 * i + k
                    pe.wait_ge(s_xs, t + 1)
                    for c in range(KD):
                        last = nc.tensor.transpose(psT[k][:, c * TN:(c + 1) * TN], xs[k][:, c * P:(c + 1) * P], s.ident[0:TN, 0:TN])
                    last.then_inc(s_tr, 1)
                    pe.wait_ge(s_xT, KD * t + KD)
                    after(pe, s_hT, CM * t)
                    for m in range(CM):
                        for c in range(KD):
                            last = nc.tensor.matmul(psH[m // HB][:, (m % HB) * TN:(m % HB + 1) * TN], w1[:, c, m * P:(m + 1) * P], xT[k][:, c, :],
                                                    start=(c == 0), stop=(c == KD - 1))
                        if m % HB == HB - 1:
                            last.then_inc(s_h, 1)
                    after(pe, s_o, 2 * i)
                    for m in range(CM):
                        if m % HB == 0:
                            pe.wait_ge(s_hT, CM * t + m + HB)
                        last = nc.tensor.matmul(psY[k][0:TN, 0:D], hT[k][:, m, :], w2[:, m, :], start=(m == 0), stop=(m == CM - 1))
                    last.then_inc(s_y, 1)
                pairs(pe, tile)


def stage_experts0(nc, s, ins):
    with ExitStack() as ctx:
        sb = lambda name, shape, dt=F32: ctx.enter_context(nc.sbuf_tensor("e_" + name, shape, dt))
        sem = lambda name: s.new_sem("e_" + name)
        pb = lambda name: ctx.enter_context(nc.psum_tensor("e_" + name, [P, 512], F32))
        w1 = sb("w1", [P, KD, F0])
        b1 = sb("b1", [P, C0])
        wg = sb("wg", [P, C0, X0])
        bg = sb("bg", [TN, X0])
        wd = sb("wd", [P, C0, X0, D])
        bd = sb("bd", [X0, D])
        lower = sb("lower", [TN, X0, X0])
        xs = [sb(f"xs{i}", [TN, D]) for i in range(2)]
        xT = [sb(f"xT{i}", [P, KD, TN]) for i in range(2)]
        hT = [sb(f"hT{i}", [P, C0, TN]) for i in range(2)]
        lg, ex, gate = sb("lg", [TN, X0]), sb("ex", [TN, X0]), sb("gate", [TN, X0])
        m1, sm = sb("m1", [TN, 1]), sb("sm", [TN, 1])
        cmp_, eq, rank = sb("cmp", [TN, X0, X0]), sb("eq", [TN, X0, X0]), sb("rank", [TN, X0])
        gT = sb("gT", [X0, TN])
        acc = sb("acc", [TN, D])
        psT = [pb(f"psT{i}") for i in range(2)]
        psH = [pb(f"psH{i}") for i in range(2)]
        psY = [pb(f"psY{i}") for i in range(2)]
        psS = pb("psS")
        s_w1, s_w, s_low, s_xs, s_tr, s_xT, s_h, s_hT, s_lg, s_lgs, s_ex, s_gate, s_gt, s_gT, s_b, s_acc, s_y, s_yev, s_dch = (
            sem(n) for n in ("w1", "w", "low", "xs", "tr", "xT", "h", "hT", "lg", "lgs", "ex", "gate", "gt", "gT", "b", "acc", "y", "yev", "dch"))
        NP = X0 // 2
        with nc.Block() as block:
            @block.sync
            def _(sp):
                sp.dma_start(w1[:, :, :], ins["L0_ffn_W1"].rearrange("(k p) n -> p k n", p=P)).then_inc(s_w1, 16)
                sp.dma_start(b1[:, :], ins["L0_ffn_b1"].rearrange("(c p) -> p c", p=P)).then_inc(s_w1, 16)
                sp.dma_start(wg[:, :, :], ins["L0_ffn_Wg"].rearrange("(c p) e -> p c e", p=P)).then_inc(s_w, 16)
                sp.dma_start(bg[:, :], ins["L0_ffn_bg"].partition_broadcast(TN)).then_inc(s_w, 16)
                sp.dma_start(bd[:, :], ins["L0_ffn_bd"]).then_inc(s_w, 16)
                for e in range(X0):
                    sp.dma_start(wd[:, :, e, :], ins["L0_ffn_Wd"][e].rearrange("(c p) n -> p c n", p=P)).then_inc(s_w, 16)

            @block.gpsimd
            def _(pool):
                nc.gpsimd.memset(lower[:, :, :], 1.0).then_inc(s_low, 1)
                pool.wait_ge(s_low, 1)
                nc.gpsimd.affine_select(out=lower[:, :, :], in_=lower[:, :, :], compare_op=ALU.is_gt, fill=0.0, base=0,
                                        pattern=[[1, X0], [-1, X0]], channel_multiplier=0).then_inc(s_low, 1)

            @block.vector
            def _(dve):
                ch = Chain(dve, s_dch, 10 + X0)
                dve.wait_ge(s_w, 16 * (3 + X0))
                dve.wait_ge(s_low, 2)

                def tile(i, k):
                    t = 2 * i + k
                    ch.at(t)
                    after(dve, s_tr, 2 * i)
                    nc.vector.tensor_scalar(xs[k][:, :], flat(s.x[:, bass.ds(t, 1), :]), s.mv[:, bass.ds(t, 1), 0],
                                            s.rstd[:, bass.ds(t, 1)], ALU.subtract, ALU.mult).then_inc(s_xs, 1)
                    dve.wait_ge(s_tr, t + 1)
                    nc.vector.tensor_copy(xT[k][:, :, :], psT[k][:, 0:KD * TN].rearrange("p (k n) -> p k n", k=KD)).then_inc(s_xT, 1)
                    dve.wait_ge(s_lg, t + 1)
                    ch.link(nc.vector.tensor_tensor(lg[:, :], psS[0:TN, 0:X0], bg[:, :], ALU.add))
                    ch.link(nc.vector.tensor_reduce(m1[:, :], lg[:, :], AX.X, ALU.max))
                    nc.vector.tensor_scalar(lg[:, :], lg[:, :], m1[:, 0:1], None, ALU.subtract).then_inc(s_lgs, 1)
                    dve.wait_ge(s_ex, t + 1)
                    ch.link(nc.vector.tensor_reduce(sm[:, :], ex[:, :], AX.X, ALU.add))
                    ch.link(nc.vector.reciprocal(sm[:, :], sm[:, :]))
                    ch.link(nc.vector.tensor_scalar(ex[:, :], ex[:, :], sm[:, 0:1], None, ALU.mult))
                    others = ex[:, :].unsqueeze(1).to_broadcast([TN, X0, X0])
                    own = ex[:, :].unsqueeze(2).to_broadcast([TN, X0, X0])
                    ch.link(nc.vector.tensor_tensor(eq[:, :, :], others, own, ALU.is_equal))
                    ch.link(nc.vector.tensor_tensor(eq[:, :, :], eq[:, :, :], lower[:, :, :], ALU.mult))
                    ch.link(nc.vector.tensor_tensor(cmp_[:, :, :], others, own, ALU.is_gt))
                    ch.link(nc.vector.tensor_tensor(cmp_[:, :, :], cmp_[:, :, :], eq[:, :, :], ALU.add))
                    ch.link(nc.vector.tensor_reduce(rank[:, :], cmp_[:, :, :], AX.X, ALU.add))
                    nc.vector.scalar_tensor_tensor(out=gate[:, :], in0=rank[:, :], scalar=1.0, in1=ex[:, :],
                                                   op0=ALU.is_lt, op1=ALU.mult).then_inc(s_gate, 1)
                    dve.wait_ge(s_gt, t + 1)
                    nc.vector.tensor_copy(gT[:, :], psS[0:X0, P:P + TN]).then_inc(s_gT, 1)
                    dve.wait_ge(s_gate, t + 1)
                    dve.wait_ge(s_acc, t + 1)
                    for e in range(X0):
                        dve.wait_ge(s_y, NP * t + e // 2 + 1)
                        step = nc.vector.scalar_tensor_tensor(out=acc[:, :], in0=psY[e // 2 % 2][0:TN, (e % 2) * D:(e % 2 + 1) * D],
                                                              scalar=gate[:, e:e + 1], in1=acc[:, :], op0=ALU.mult, op1=ALU.add)
                        ch.link(step)
                        if e % 2:
                            dve.sem_inc(s_yev, 1)
                    nc.vector.tensor_tensor(flat(s.x[:, bass.ds(t, 1), :]), flat(s.x[:, bass.ds(t, 1), :]), acc[:, :], ALU.add)
                pairs(dve, tile)

            @block.scalar
            def _(act):
                act.wait_ge(s_w1, 32)

                def tile(i, k):
                    t = 2 * i + k
                    for c in range(C0):
                        act.wait_ge(s_h, 2 * t + 1 + c // 4)
                        nc.scalar.activation(hT[k][:, c, :], psH[c // 4][:, (c % 4) * TN:(c % 4 + 1) * TN], ACT.Gelu,
                                             bias=b1[:, c:c + 1]).then_inc(s_hT, 1)
                    act.wait_ge(s_lgs, t + 1)
                    nc.scalar.activation(ex[:, :], lg[:, :], ACT.Exp).then_inc(s_ex, 1)
                    act.wait_ge(s_b, t + 1)
                    nc.scalar.activation(acc[:, :], psS[0:TN, D:2 * D], ACT.Copy).then_inc(s_acc, 1)
                pairs(act, tile)

            @block.tensor
            def _(pe):
                pe.wait_ge(s_w1, 32)

                def tile(i, k):
                    t = 2 * i + k
                    pe.wait_ge(s_xs, t + 1)
                    for c in range(KD):
                        last = nc.tensor.transpose(psT[k][:, c * TN:(c + 1) * TN], xs[k][:, c * P:(c + 1) * P], s.ident[0:TN, 0:TN])
                    last.then_inc(s_tr, 1)
                    pe.wait_ge(s_xT, t + 1)
                    after(pe, s_hT, C0 * t)
                    for m in range(C0):
                        for c in range(KD):
                            last = nc.tensor.matmul(psH[m // 4][:, (m % 4) * TN:(m % 4 + 1) * TN], w1[:, c, m * P:(m + 1) * P], xT[k][:, c, :],
                                                    start=(c == 0), stop=(c == KD - 1))
                        if m % 4 == 3:
                            last.then_inc(s_h, 1)
                    if isinstance(i, int) and i == 0 and k == 0:
                        pe.wait_ge(s_w, 16 * (3 + X0))
                    after(pe, s_acc, t)
                    for m in range(C0):
                        if m % 4 == 0:
                            pe.wait_ge(s_hT, C0 * t + m + 4)
                        last = nc.tensor.matmul(psS[0:TN, 0:X0], hT[k][:, m, :], wg[:, m, :], start=(m == 0), stop=(m == C0 - 1))
                    last.then_inc(s_lg, 1)

                    def experts(p):
                        if not (isinstance(t, int) and NP * t + p < 2):
                            pe.wait_ge(s_yev, NP * t + p - 1)
                        for m in range(C0):
                            last = nc.tensor.matmul(psY[p % 2][0:TN, :], hT[k][:, m, :],
                                                    wd[:, m, 2 * p:2 * p + 2, :].rearrange("p e n -> p (e n)"), start=(m == 0), stop=(m == C0 - 1))
                        last.then_inc(s_y, 1)
                    experts(0)
                    pe.wait_ge(s_gate, t + 1)
                    nc.tensor.transpose(psS[0:X0, P:P + TN], gate[:, :], s.ident[0:TN, 0:TN]).then_inc(s_gt, 1)
                    experts(1)
                    pe.wait_ge(s_gT, t + 1)
                    nc.tensor.matmul(psS[0:TN, D:2 * D], gT[:, :], bd[:, :], start=True, stop=True).then_inc(s_b, 1)
                    experts(2)
                    experts(3)
                pairs(pe, tile)


def rotations(dbl, h0):
    base = dbl[:, h0:h0 + HH, 0:DK]
    rows, heads, cols = base.ap
    return bass.AP(base.tensor, base.offset, [rows, [cols[0], NS], heads, cols])


def build_layer1(nc, s, ctx):
    sb = lambda name, shape: ctx.enter_context(nc.sbuf_tensor(name, shape, F32))
    s.qk1 = sb("qk1", [TN, NT, 2 * D])
    s.v1 = sb("v1", [TN, NT, D])


def build_moments(nc, s, ctx):
    s.mom = [ctx.enter_context(nc.sbuf_tensor(f"mom{g}", [P, NS + 1, HH * VE], F32)) for g in range(2)]
    s.mom0 = ctx.enter_context(nc.sbuf_tensor("mom_const", [TN, 2, HH * VE], F32))
    s.bsc, s.bbe = (ctx.enter_context(nc.sbuf_tensor(n, [TN, D], F32)) for n in ("bsc", "bbe"))


def stage_project1(nc, s, ins):
    SC = float(DK) ** 0.25
    with ExitStack() as ctx:
        sb = lambda name, shape, dt=F32: ctx.enter_context(nc.sbuf_tensor("b_" + name, shape, dt))
        sem = lambda name: s.new_sem("b_" + name)
        pb = lambda name: ctx.enter_context(nc.psum_tensor("b_" + name, [P, 512], F32))
        NR = R * D // 512
        wr = sb("wr", [P, KD, R, D])
        wraw = sb("wraw", [P, 3 * KD, D])
        wT = sb("wT", [P, KD, 3 * D])
        bias = sb("bias", [TN, 3 * D])
        fac = sb("fac", [TN, 2 * HG])
        xs = [sb(f"xs{i}", [TN, D]) for i in range(2)]
        xT = [sb(f"xT{i}", [P, KD, TN]) for i in range(2)]
        hs = [sb(f"hs{i}", [TN, R * D]) for i in range(2)]
        qk = sb("qk", [TN, 2 * D])
        sq = sb("sq", [TN, 2 * D])
        nrm = sb("nrm", [TN, 2 * HG])
        psT = [pb(f"psT{i}") for i in range(2)]
        psR = [pb(f"psR{i}") for i in range(3)]
        psQ, psV = pb("psQ"), pb("psV")
        s_raw, s_w, s_b, s_wt, s_wte, s_fac, s_xs, s_tr, s_xT, s_r, s_hs, s_q, s_v, s_ss, s_sqrt, s_vo, s_qke, s_dch = (
            sem(n) for n in ("raw", "w", "b", "wt", "wte", "fac", "xs", "tr", "xT", "r", "hs", "q", "v", "ss", "sqrt", "vo", "qke", "dch"))
        s_ho = [sem(f"ho{i}") for i in range(2)]
        with nc.Block() as block:
            @block.sync
            def _(sp):
                sp.dma_start(wraw[:, :, :], ins["L1_mix_Wqkv"].rearrange("(c p) n -> p c n", p=P)).then_inc(s_raw, 16)
                for r in range(R):
                    sp.dma_start(wr[:, :, r, :], ins["L1_gnn_weight"][r].rearrange("(k p) n -> p k n", p=P)).then_inc(s_w, 16)
                sp.dma_start(bias[:, :], ins["L1_mix_bqkv"].partition_broadcast(TN)).then_inc(s_b, 16)
                sp.dma_start(fac[:, 0:HG], ins["L1_mix_temperature"].rearrange("a h b c -> (a h b c)").partition_broadcast(TN)).then_inc(s_b, 16)

                def store(i, k):
                    t = 2 * i + k
                    sp.wait_ge(s_hs, NR * t + NR)
                    sp.dma_start(s.h_d.rearrange("(n r) d -> n (r d)", r=R)[bass.ds(t * TN, TN), :], hs[k][:, :]).then_inc(s_ho[k], 16)
                pairs(sp, store)
                sp.wait_ge(s_ho[0], 16 * 13)
                sp.wait_ge(s_ho[1], 16 * 12)

            @block.vector
            def _(dve):
                ch = Chain(dve, s_dch, 5)
                for n in range(3):
                    dve.wait_ge(s_wt, n + 1)
                    nc.vector.tensor_copy(wT[:, :, n * D:(n + 1) * D].rearrange("p k (c n) -> p c k n", c=2),
                                          psR[n][:, :].rearrange("p (c k n) -> p c k n", c=2, k=KD)).then_inc(s_wte, 1)
                dve.wait_ge(s_b, 32)
                nc.vector.tensor_scalar(fac[:, 0:HG], fac[:, 0:HG], SC * SC, None, ALU.mult).then_inc(s_fac, 1)
                nc.vector.memset(fac[:, HG:2 * HG], SC).then_inc(s_fac, 1)
                dve.wait_ge(s_fac, 2)

                def tile(i, k):
                    t = 2 * i + k
                    ch.at(t)
                    nc.vector.tensor_scalar(xs[k][:, :], flat(s.x[:, bass.ds(t, 1), :]), s.mv[:, bass.ds(t, 1), 0],
                                            s.rstd[:, bass.ds(t, 1)], ALU.subtract, ALU.mult).then_inc(s_xs, 1)
                    dve.wait_ge(s_tr, t + 1)
                    nc.vector.tensor_copy(xT[k][:, :, :], psT[k][:, 0:KD * TN].rearrange("p (k n) -> p k n", k=KD)).then_inc(s_xT, 1)
                    dve.wait_ge(s_q, t + 1)
                    ch.link(nc.vector.tensor_tensor(qk[:, :], psQ[0:TN, :], bias[:, 0:2 * D], ALU.add))
                    dve.sem_inc(s_qke, 1)
                    ch.link(nc.vector.tensor_tensor(sq[:, :], qk[:, :], qk[:, :], ALU.mult))
                    nc.vector.tensor_reduce(nrm[:, :], sq[:, :].rearrange("p (h d) -> p h d", d=DK), AX.X, ALU.add).then_inc(s_ss, 1)
                    dve.wait_ge(s_v, t + 1)
                    nc.vector.tensor_tensor(flat(s.v1[:, bass.ds(t, 1), :]), psV[0:TN, 0:D], bias[:, 2 * D:3 * D], ALU.add).then_inc(s_vo, 1)
                    dve.wait_ge(s_sqrt, t + 1)
                    ch.link(nc.vector.tensor_scalar(nrm[:, 0:HG], nrm[:, 0:HG], SC, 1e-12, ALU.mult, ALU.max))
                    nc.vector.tensor_scalar(nrm[:, HG:2 * HG], nrm[:, HG:2 * HG], 1e-12, None, ALU.max).then_inc(s_fac, 1)
                    dve.wait_ge(s_fac, t + 3)
                    ch.link(nc.vector.reciprocal(nrm[:, :], nrm[:, :]))
                    ch.link(nc.vector.tensor_tensor(nrm[:, :], nrm[:, :], fac[:, :], ALU.mult))
                    nc.vector.tensor_tensor(flat(s.qk1[:, bass.ds(t, 1), :]).rearrange("p (h d) -> p h d", d=DK),
                                            qk[:, :].rearrange("p (h d) -> p h d", d=DK),
                                            nrm[:, :].unsqueeze(2).to_broadcast([TN, 2 * HG, DK]), ALU.mult)
                pairs(dve, tile)

            @block.scalar
            def _(act):
                def tile(i, k):
                    t = 2 * i + k
                    after(act, s_ho[k], 16 * i)
                    for n in range(NR):
                        act.wait_ge(s_r, NR * t + n + 1)
                        nc.scalar.activation(hs[k][:, n * 512:(n + 1) * 512], turn_of(psR, n)[0:TN, :], ACT.Copy).then_inc(s_hs, 1)
                    act.wait_ge(s_ss, t + 1)
                    nc.scalar.activation(nrm[:, :], nrm[:, :], ACT.Sqrt).then_inc(s_sqrt, 1)
                pairs(act, tile)

            @block.tensor
            def _(pe):
                pe.wait_ge(s_raw, 16)
                for n in range(3):
                    for c in range(2):
                        for k in range(KD):
                            last = nc.tensor.transpose(psR[n][:, c * D + k * P:c * D + (k + 1) * P], wraw[:, 2 * n + c, k * P:(k + 1) * P], s.ident[:, :])
                    last.then_inc(s_wt, 1)
                pe.wait_ge(s_wte, 3)
                pe.wait_ge(s_w, 16 * R)

                def tile(i, k):
                    t = 2 * i + k
                    pe.wait_ge(s_xs, t + 1)
                    for c in range(KD):
                        last = nc.tensor.transpose(psT[k][:, c * TN:(c + 1) * TN], xs[k][:, c * P:(c + 1) * P], s.ident[0:TN, 0:TN])
                    last.then_inc(s_tr, 1)
                    pe.wait_ge(s_xT, t + 1)
                    after(pe, s_qke, t)
                    for c in range(KD):
                        last = nc.tensor.matmul(psQ[0:TN, :], xT[k][:, c, :], wT[:, c, 0:2 * D], start=(c == 0), stop=(c == KD - 1))
                    last.then_inc(s_q, 1)
                    after(pe, s_vo, t)
                    for c in range(KD):
                        last = nc.tensor.matmul(psV[0:TN, 0:D], xT[k][:, c, :], wT[:, c, 2 * D:3 * D], start=(c == 0), stop=(c == KD - 1))
                    last.then_inc(s_v, 1)
                    for n in range(NR):
                        after(pe, s_hs, NR * t + max(n - len(psR) + 1, 0))
                        for c in range(KD):
                            last = nc.tensor.matmul(turn_of(psR, n)[0:TN, :], xT[k][:, c, :],
                                                    wr[:, c, 2 * n:2 * n + 2, :].rearrange("p r d -> p (r d)"), start=(c == 0), stop=(c == KD - 1))
                        last.then_inc(s_r, 1)
                pairs(pe, tile)


def stage_moments(nc, s, half):
    SC = float(DK) ** 0.25
    A, B, C = 0.5, 1.0, 1.0
    W = HH * VE
    PER = 3
    h0 = half * HH
    with ExitStack() as ctx:
        tag = f"k{half}_"
        sb = lambda name, shape, dt=F32: ctx.enter_context(nc.sbuf_tensor(tag + name, shape, dt))
        sem = lambda name: s.new_sem(tag + name)
        dbl = [sb(f"dbl{i}", [TN, HH, 2 * DK]) for i in range(2)]
        kk = [sb(f"kk{i}", [TN, NS + 1, P]) for i in range(2)]
        v1 = [sb(f"v1{i}", [TN, HH, VE]) for i in range(2)]
        wt = sb("wt", [P, NS + 1])
        one = sb("one", [TN, TN])
        ps = [ctx.enter_context(nc.psum_tensor(f"{tag}ps{i}", [P, 512], F32)) for i in range((NS + 1) // PER)]
        psC = ctx.enter_context(nc.psum_tensor(tag + "psC", [P, 512], F32))
        s_init, s_dbl, s_v, s_kk, s_m, s_end = (sem(n) for n in ("init", "dbl", "v", "kk", "m", "end"))
        with nc.Block() as block:
            @block.scalar
            def _(act):
                act.wait_ge(s_init, 8)

                def tile(i, k):
                    t = 2 * i + k
                    after(act, s_m, 2 * i)
                    keys = flat(s.qk1[:, bass.ds(t, 1), D + h0 * DK:D + (h0 + HH) * DK]).rearrange("p (h d) -> p h d", d=DK)
                    for c in range(2):
                        nc.scalar.activation(dbl[k][:, :, c * DK:(c + 1) * DK], keys, ACT.Copy).then_inc(s_dbl, 1)
                    nc.scalar.activation(kk[k][:, NS, :].rearrange("p (h d) -> p h d", d=DK), keys, ACT.Copy).then_inc(s_dbl, 1)
                    nc.scalar.activation(v1[k][:, :, 1:VE], flat(s.v1[:, bass.ds(t, 1), h0 * DK:(h0 + HH) * DK]).rearrange("p (h d) -> p h d", d=DK),
                                         ACT.Copy).then_inc(s_v, 1)
                pairs(act, tile)

            @block.vector
            def _(dve):
                nc.vector.memset(one[:, :], 1.0).then_inc(s_init, 1)
                for k in range(2):
                    nc.vector.memset(v1[k][:, :, :], 1.0).then_inc(s_init, 1)
                nc.vector.memset(wt[:, 0:1], A / N).then_inc(s_init, 1)
                nc.vector.memset(wt[:, 1:NS - 1], 2 * A / N).then_inc(s_init, 1)
                nc.vector.memset(wt[:, NS - 1:NS], A / N).then_inc(s_init, 1)
                nc.vector.memset(wt[:, NS:NS + 1], SC ** 2 * B / N).then_inc(s_init, 1)
                nc.vector.memset(s.mom[half][:, :, :], 0.0).then_inc(s_init, 1)

                def tile(i, k):
                    t = 2 * i + k
                    dve.wait_ge(s_dbl, 3 * t + 3)
                    after(dve, s_m, 2 * i)
                    nc.vector.tensor_tensor(kk[k][:, 0:NS, :].rearrange("p r (h d) -> p r h d", d=DK), rotations(dbl[k], 0),
                                            dbl[k][:, :, 0:DK].unsqueeze(1).to_broadcast([TN, NS, HH, DK]), ALU.mult).then_inc(s_kk, 1)
                pairs(dve, tile)
                dve.wait_ge(s_end, 1)
                dve.wait_ge(s_init, 8)
                for h in range(HH):
                    rows, cols = slice(h * DK, (h + 1) * DK), slice(h * VE, (h + 1) * VE)
                    for n, bank in enumerate(ps):
                        nc.vector.tensor_tensor(s.mom[half][rows, n * PER:(n + 1) * PER, cols],
                                                bank[rows, 0:PER * W].rearrange("p (r c) -> p r c", r=PER)[:, :, cols],
                                                wt[rows, n * PER:(n + 1) * PER].unsqueeze(2).to_broadcast([DK, PER, VE]), ALU.mult)
                nc.vector.tensor_scalar(s.mom0[:, half, :], psC[0:TN, 0:W], SC ** 4 * C / N, None, ALU.mult)

            @block.tensor
            def _(pe):
                for bank in (*ps, psC):
                    nc.tensor.matmul(bank[:, 0:PER * W], s.zero[:, 0:P], s.zero[:, 0:PER * W], start=True, stop=False)
                pe.wait_ge(s_init, 8)

                def tile(i, k):
                    t = 2 * i + k
                    pe.wait_ge(s_v, t + 1)
                    values = v1[k][:, :, :].rearrange("p h d -> p (h d)")
                    nc.tensor.matmul(psC[0:TN, 0:W], one[:, :], values, start=False, stop=False)
                    pe.wait_ge(s_kk, t + 1)
                    for r in range(NS + 1):
                        last = nc.tensor.matmul(ps[r // PER][:, r % PER * W:(r % PER + 1) * W], kk[k][:, r, :], values, start=False, stop=False)
                    last.then_inc(s_m, 1)
                pairs(pe, tile)
                for bank in (*ps, psC):
                    last = nc.tensor.matmul(bank[:, 0:PER * W], s.zero[:, 0:P], s.zero[:, 0:PER * W], start=False, stop=True)
                last.then_inc(s_end, 1)


def stage_relations(nc, s, ins):
    SLOTS = [(a, j) for a in range(NB) for j in range(UJ)]
    with ExitStack() as ctx:
        sb = lambda name, shape, dt=F32: ctx.enter_context(nc.sbuf_tensor("r_" + name, shape, dt))
        sem = lambda name: s.new_sem("r_" + name)
        iota_b = sb("iota_b", [TN, TN])
        idx = [sb(f"idx{a}", [TN, UJ], I32) for a in range(NB)]
        rows = [sb(f"rows{a}_{j}", [TN, D]) for a, j in SLOTS]
        oh = [sb(f"oh{a}_{j}", [TN, TN]) for a, j in SLOTS]
        psO = ctx.enter_context(nc.psum_tensor("r_psO", [P, 512], F32))
        s_blk, s_bch, s_go = (sem(n) for n in ("blk", "bch", "go"))
        s_sct, s_oh, s_idx = ([sem(f"{n}{a}") for a in range(NB)] for n in ("sct", "oh", "idx"))
        s_rows = s.rows_gathered
        with nc.Block() as block:
            @block.gpsimd
            def _(pool):
                def gather(b, g, n):
                    for a in range(NB):
                        pool.wait_ge(s_sct[a], n + 1)
                        nc.gpsimd.tensor_copy(idx[a][:, :], s.reli[:, bass.ds(g + a, 1), :]).then_inc(s_idx[a], 1)
                        pool.wait_ge(s_idx[a], n + 1)
                        pool.sem_inc(s_go, 1)
                        for j in range(UJ):
                            nc.gpsimd.indirect_dma_start(out=rows[a * UJ + j][:, :], out_offset=None, in_=s.h_d,
                                                         in_offset=bass.IndirectOffsetOnAxis(ap=idx[a][:, j:j + 1], axis=0)).then_inc(s_rows[a], 16)
                each_block(nc, pool, s, lambda b: None, gather, lambda b: None)

            @block.vector
            def _(dve):
                nc.vector.tensor_copy(iota_b[:, :], s.iota_f[:, :]).then_inc(s_bch, 1)
                dve.wait_ge(s_bch, 1)

                def one_pass(b, g, n):
                    for a in range(NB):
                        dve.wait_ge(s_sct[a], n + 1)
                        for j in range(UJ):
                            last = nc.vector.tensor_scalar(oh[a * UJ + j][:, :], iota_b[:, :], s.dstf[:, bass.ds(g + a, 1), j], None, ALU.is_equal)
                        last.then_inc(s_oh[a], 1)

                def end(b):
                    dve.wait_ge(s_blk, b + 1)
                    nc.vector.tensor_scalar(flat(s.y[:, bass.ds(b, 1), :]), psO[0:TN, 0:D], 1.0, None, ALU.mult).then_inc(s_bch, 1)
                    nc.vector.tensor_scalar(iota_b[:, :], iota_b[:, :], float(TN), None, ALU.add).then_inc(s_bch, 1)
                    dve.wait_ge(s_bch, 2 * b + 3)
                each_block(nc, dve, s, lambda b: None, one_pass, end)

            @block.tensor
            def _(pe):
                for a in range(NB):
                    pe.sem_inc(s_sct[a], 1)

                def start(b):
                    pe.wait_ge(s_bch, 2 * b + 1)
                    nc.tensor.matmul(psO[0:TN, 0:D], s.zero[0:TN, 0:TN], s.zero[0:TN, 0:D], start=True, stop=False)

                def one_pass(b, g, n):
                    for a in range(NB):
                        pe.wait_ge(s_oh[a], n + 1)
                        pe.wait_ge(s_rows[a], 16 * UJ * n + 16 * UJ)
                        for j in range(UJ):
                            last = nc.tensor.matmul(psO[0:TN, 0:D], oh[a * UJ + j][:, :], rows[a * UJ + j][:, :], start=False, stop=False)
                        last.then_inc(s_sct[a], 1)

                def end(b):
                    nc.tensor.matmul(psO[0:TN, 0:D], s.zero[0:TN, 0:TN], s.zero[0:TN, 0:D], start=False, stop=True).then_inc(s_blk, 1)
                each_block(nc, pe, s, start, one_pass, end)


def stage_batchnorm(nc, s, ins):
    with ExitStack() as ctx:
        sb = lambda name, shape, dt=F32: ctx.enter_context(nc.sbuf_tensor("v_" + name, shape, dt))
        sem = lambda name: s.new_sem("v_" + name)
        one = sb("one", [TN, TN])
        mean = sb("mean", [TN, D])
        var = sb("var", [TN, D])
        sq = [sb(f"sq{i}", [TN, D]) for i in range(2)]
        psM, psV = (ctx.enter_context(nc.psum_tensor("v_" + n, [P, 512], F32)) for n in ("psM", "psV"))
        s_in, s_one, s_sum, s_mean, s_c, s_sq, s_v, s_var, s_sd, s_dch = (
            sem(n) for n in ("in", "one", "sum", "mean", "c", "sq", "v", "var", "sd", "dch"))
        with nc.Block() as block:
            @block.sync
            def _(sp):
                sp.dma_start(s.bsc[:, :], ins["L1_gnn_gamma"].partition_broadcast(TN)).then_inc(s_in, 16)
                sp.dma_start(s.bbe[:, :], ins["L1_gnn_beta"].partition_broadcast(TN)).then_inc(s_in, 16)

            @block.vector
            def _(dve):
                nc.vector.memset(one[:, :], 1.0).then_inc(s_one, 1)
                dve.wait_ge(s_sum, 1)
                nc.vector.tensor_scalar(mean[:, :], psM[0:TN, 0:D], 1.0 / N, None, ALU.mult).then_inc(s_mean, 1)
                dve.wait_ge(s_mean, 1)

                def tile(i, k):
                    t = 2 * i + k
                    row = flat(s.y[:, bass.ds(t, 1), :])
                    nc.vector.tensor_tensor(row, row, mean[:, :], ALU.subtract).then_inc(s_c, 1)
                    dve.wait_ge(s_c, t + 1)
                    after(dve, s_v, 2 * i)
                    nc.vector.tensor_tensor(sq[k][:, :], row, row, ALU.mult).then_inc(s_sq, 1)
                pairs(dve, tile)
                dve.wait_ge(s_v, NT + 1)
                nc.vector.tensor_scalar(var[:, :], psV[0:TN, 0:D], 1.0 / N, EPS, ALU.mult, ALU.add).then_inc(s_var, 1)
                dve.wait_ge(s_sd, 1)
                nc.vector.reciprocal(var[:, :], var[:, :]).then_inc(s_dch, 1)
                dve.wait_ge(s_dch, 1)
                dve.wait_ge(s_in, 32)
                nc.vector.tensor_tensor(s.bsc[:, :], s.bsc[:, :], var[:, :], ALU.mult)

            @block.scalar
            def _(act):
                act.wait_ge(s_var, 1)
                nc.scalar.activation(var[:, :], var[:, :], ACT.Sqrt).then_inc(s_sd, 1)

            @block.tensor
            def _(pe):
                pe.wait_ge(s_one, 1)
                for t in range(NT):
                    last = nc.tensor.matmul(psM[0:TN, 0:D], one[:, :], s.y[:, t, :], start=(t == 0), stop=(t == NT - 1))
                last.then_inc(s_sum, 1)
                nc.tensor.matmul(psV[0:TN, 0:D], s.zero[0:TN, 0:TN], s.zero[0:TN, 0:D], start=True, stop=False)

                def tile(i, k):
                    pe.wait_ge(s_sq, 2 * i + k + 1)
                    nc.tensor.matmul(psV[0:TN, 0:D], one[:, :], sq[k][:, :], start=False, stop=False).then_inc(s_v, 1)
                pairs(pe, tile)
                nc.tensor.matmul(psV[0:TN, 0:D], s.zero[0:TN, 0:TN], s.zero[0:TN, 0:D], start=False, stop=True).then_inc(s_v, 1)


def stage_mix1(nc, s, ins):
    W = HH * VE
    BK = 4
    GROUPS = [(a, min(a + BK, NS + 1)) for a in range(0, NS + 1, BK)]
    NG = len(GROUPS)
    with ExitStack() as ctx:
        sb = lambda name, shape, dt=F32: ctx.enter_context(nc.sbuf_tensor("q_" + name, shape, dt))
        sem = lambda name: s.new_sem("q_" + name)
        pb = lambda name: ctx.enter_context(nc.psum_tensor("q_" + name, [P, 512], F32))
        wraw = sb("wraw", [P, 2, D])
        wT = sb("wT", [P, KD, D])
        bias = sb("bias", [TN, D])
        dbl = sb("dbl", [TN, HG, 2 * DK])
        qq = [sb(f"qq{g}", [TN, NS + 1, P]) for g in range(2)]
        qT = [sb(f"qT{g}", [P, NS + 1, TN]) for g in range(2)]
        y1 = [sb(f"y1{g}", [TN, HH, VE]) for g in range(2)]
        rc = [sb(f"rc{g}", [TN, HH]) for g in range(2)]
        o = sb("o", [TN, D])
        oT = sb("oT", [P, KD, TN])
        res = sb("res", [TN, D])
        psT = [pb(f"psT{i}") for i in range(3)]
        psY = [pb(f"psY{i}") for i in range(2)]
        psO, psP = pb("psO"), pb("psP")
        s_raw, s_b, s_wt, s_wte, s_dbl, s_qq, s_tr, s_ev, s_y, s_y1, s_o, s_ot, s_oT, s_p, s_res, s_dch = (
            sem(n) for n in ("raw", "b", "wt", "wte", "dbl", "qq", "tr", "ev", "y", "y1", "o", "ot", "oT", "p", "res", "dch"))
        with nc.Block() as block:
            @block.sync
            def _(sp):
                sp.dma_start(wraw[:, :, :], ins["L1_mix_Wproj"].rearrange("(c p) n -> p c n", p=P)).then_inc(s_raw, 16)
                sp.dma_start(bias[:, :], ins["L1_mix_bproj"].partition_broadcast(TN)).then_inc(s_b, 16)

            @block.vector
            def _(dve):
                ch = Chain(dve, s_dch, 8)
                dve.wait_ge(s_wt, 1)
                nc.vector.tensor_copy(wT[:, :, :].rearrange("p k (c n) -> p c k n", c=2),
                                      psO[:, :].rearrange("p (c k n) -> p c k n", c=2, k=KD)).then_inc(s_wte, 1)
                dve.wait_ge(s_b, 16)
                nc.vector.tensor_tensor(bias[:, :], bias[:, :], s.bbe[:, :], ALU.add).then_inc(s_wte, 1)
                dve.wait_ge(s_wte, 2)

                def tile(i, k):
                    t = 2 * i + k
                    ch.at(t)
                    queries = flat(s.qk1[:, bass.ds(t, 1), 0:D]).rearrange("p (h d) -> p h d", d=DK)
                    after(dve, s_tr, 2 * NG * t)
                    ch.link(nc.vector.tensor_scalar(dbl[:, :, 0:DK], queries, 1.0, None, ALU.mult))
                    nc.vector.tensor_scalar(dbl[:, :, DK:2 * DK], queries, 1.0, None, ALU.mult).then_inc(s_dbl, 1)
                    dve.wait_ge(s_dbl, t + 1)
                    for g in range(2):
                        nc.vector.tensor_copy(qq[g][:, NS, :].rearrange("p (h d) -> p h d", d=DK), dbl[:, g * HH:(g + 1) * HH, 0:DK])
                        nc.vector.tensor_tensor(qq[g][:, 0:NS, :].rearrange("p r (h d) -> p r h d", d=DK), rotations(dbl, g * HH),
                                                dbl[:, g * HH:(g + 1) * HH, 0:DK].unsqueeze(1).to_broadcast([TN, NS, HH, DK]), ALU.mult).then_inc(s_qq, 1)
                    row, out = flat(s.y[:, bass.ds(t, 1), :]), flat(s.x[:, bass.ds(t, 1), :])
                    ch.link(nc.vector.tensor_tensor(res[:, :], row, s.bsc[:, :], ALU.mult))
                    ch.link(nc.vector.tensor_tensor(res[:, :], res[:, :], bias[:, :], ALU.add))
                    ch.link(nc.vector.tensor_tensor(out, out, res[:, :], ALU.add))
                    for g in range(2):
                        dve.wait_ge(s_y, 2 * t + g + 1)
                        nc.vector.tensor_tensor(y1[g][:, :, :].rearrange("p h d -> p (h d)"), psY[g][0:TN, 0:W], s.mom0[:, g, :], ALU.add).then_inc(s_y1, 1)
                        dve.wait_ge(s_y1, 2 * t + g + 1)
                        ch.link(nc.vector.reciprocal(rc[g][:, :].unsqueeze(2), y1[g][:, :, 0:1]))
                        nc.vector.tensor_tensor(o[:, g * P:(g + 1) * P].rearrange("p (h d) -> p h d", d=DK), y1[g][:, :, 1:VE],
                                                rc[g][:, :].unsqueeze(2).to_broadcast([TN, HH, DK]), ALU.mult).then_inc(s_o, 1)
                    dve.wait_ge(s_ot, t + 1)
                    nc.vector.tensor_copy(oT[:, :, :], psO[:, 0:KD * TN].rearrange("p (k n) -> p k n", k=KD)).then_inc(s_oT, 1)
                    dve.wait_ge(s_p, t + 1)
                    ch.link(nc.vector.tensor_copy(res[:, :], psP[0:TN, 0:D]))
                    ch.link(nc.vector.tensor_tensor(out, out, res[:, :], ALU.add))
                pairs(dve, tile)

            @block.scalar
            def _(act):
                def tile(i, k):
                    t = 2 * i + k
                    for g in range(2):
                        for n, (a, b) in enumerate(GROUPS):
                            act.wait_ge(s_tr, 2 * NG * t + g * NG + n + 1)
                            if n == 0:
                                after(act, s_y, 2 * t + g - 1)
                            nc.scalar.activation(qT[g][:, a:b, :], turn_of(psT, g * NG + n)[:, 0:(b - a) * TN].rearrange("p (r n) -> p r n", r=b - a),
                                                 ACT.Copy).then_inc(s_ev, 1)
                pairs(act, tile)

            @block.tensor
            def _(pe):
                pe.wait_ge(s_raw, 16)
                for c in range(2):
                    for k in range(KD):
                        last = nc.tensor.transpose(psO[:, c * D + k * P:c * D + (k + 1) * P], wraw[:, c, k * P:(k + 1) * P], s.ident[:, :])
                last.then_inc(s_wt, 1)
                pe.wait_ge(s_wte, 2)

                def tile(i, k):
                    t = 2 * i + k

                    def turn(g):
                        pe.wait_ge(s_qq, 2 * t + g + 1)
                        for n, (a, b) in enumerate(GROUPS):
                            at = g * NG + n
                            if at < 3:
                                after(pe, s_ev, 2 * NG * t)
                            else:
                                pe.wait_ge(s_ev, 2 * NG * t + at - 2)
                            for r in range(a, b):
                                last = nc.tensor.transpose(turn_of(psT, at)[:, (r - a) * TN:(r - a + 1) * TN], qq[g][:, r, :], s.ident[0:TN, 0:TN])
                            last.then_inc(s_tr, 1)

                    def contract(g):
                        after(pe, s_y1, 2 * t)
                        for n, (a, b) in enumerate(GROUPS):
                            pe.wait_ge(s_ev, 2 * NG * t + g * NG + n + 1)
                            for r in range(a, b):
                                last = nc.tensor.matmul(psY[g][0:TN, 0:W], qT[g][:, r, :], s.mom[g][:, r, :], start=(r == 0), stop=(r == NS))
                        last.then_inc(s_y, 1)
                    turn(0)
                    turn(1)
                    contract(0)
                    contract(1)
                    pe.wait_ge(s_o, 2 * t + 2)
                    for c in range(KD):
                        last = nc.tensor.transpose(psO[:, c * TN:(c + 1) * TN], o[:, c * P:(c + 1) * P], s.ident[0:TN, 0:TN])
                    last.then_inc(s_ot, 1)
                    pe.wait_ge(s_oT, t + 1)
                    for c in range(KD):
                        last = nc.tensor.matmul(psP[0:TN, 0:D], oT[:, c, :], wT[:, c, :], start=(c == 0), stop=(c == KD - 1))
                    last.then_inc(s_p, 1)
                pairs(pe, tile)


def stage_normalise(nc, s):
    with nc.Block() as block:
        @block.vector
        def _(dve):
            with dve.Fori(0, NT) as t:
                nc.vector.tensor_scalar(flat(s.y[:, bass.ds(t, 1), :]), flat(s.x[:, bass.ds(t, 1), :]), s.mv[:, bass.ds(t, 1), 0],
                                        s.rstd[:, bass.ds(t, 1)], ALU.subtract, ALU.mult)


def stage_experts1(nc, s, ins, out):
    with ExitStack() as ctx:
        sb = lambda name, shape, dt=F32: ctx.enter_context(nc.sbuf_tensor("z_" + name, shape, dt))
        sem = lambda name: s.new_sem("z_" + name)
        pb = lambda name: ctx.enter_context(nc.psum_tensor("z_" + name, [P, 512], F32))
        w1 = sb("w1", [P, X0, KD, F1])
        b1 = sb("b1", [P, X0, C1])
        w2 = sb("w2", [P, X0, C1, D])
        b2 = sb("b2", [X0, D])
        wr = sb("wr", [P, KD, X0])
        br = sb("br", [TN, X0])
        ga = sb("ga", [P, KD])
        be = sb("be", [P, KD])
        lower = sb("lower", [TN, X0, X0])
        xs = [sb(f"xs{i}", [TN, D]) for i in range(2)]
        xT = [sb(f"xT{i}", [P, KD, TN]) for i in range(2)]
        hT = [sb(f"hT{i}", [P, C1, TN]) for i in range(2)]
        lg, lm, ex, gate = sb("lg", [TN, X0]), sb("lm", [TN, X0]), sb("ex", [TN, X0]), sb("gate", [TN, X0])
        m1, sm = sb("m1", [TN, 1]), sb("sm", [TN, 1])
        cmp_, eq, rank = sb("cmp", [TN, X0, X0]), sb("eq", [TN, X0, X0]), sb("rank", [TN, X0])
        gT = sb("gT", [X0, TN])
        acc = [sb(f"acc{i}", [TN, D]) for i in range(2)]
        psT = pb("psT")
        psH = [pb(f"psH{i}") for i in range(2)]
        psY = [pb(f"psY{i}") for i in range(3)]
        psL, psS = pb("psL"), pb("psS")
        s_w1, s_w, s_low, s_xs, s_tr, s_xT, s_h, s_hT, s_lg, s_lgs, s_ex, s_gate, s_gt, s_gT, s_b, s_acc, s_y, s_yev, s_fin, s_dch = (
            sem(n) for n in ("w1", "w", "low", "xs", "tr", "xT", "h", "hT", "lg", "lgs", "ex", "gate", "gt", "gT", "b", "acc", "y", "yev", "fin", "dch"))
        s_out = [sem(f"out{i}") for i in range(2)]
        with nc.Block() as block:
            @block.sync
            def _(sp):
                sp.dma_start(ga[:, :], ins["L1_ffn_gamma"].rearrange("(c p) -> p c", p=P)).then_inc(s_w1, 16)
                sp.dma_start(be[:, :], ins["L1_ffn_beta"].rearrange("(c p) -> p c", p=P)).then_inc(s_w1, 16)
                sp.dma_start(wr[:, :, :], ins["L1_ffn_Wr"].rearrange("(k p) e -> p k e", p=P)).then_inc(s_w1, 16)
                sp.dma_start(b1[:, :, :], ins["L1_ffn_b1"].rearrange("e (c p) -> p e c", p=P)).then_inc(s_w1, 16)
                sp.dma_start(br[:, :], ins["L1_ffn_br"].partition_broadcast(TN)).then_inc(s_w1, 16)
                sp.dma_start(b2[:, :], ins["L1_ffn_b2"]).then_inc(s_w1, 16)
                for e in range(X0):
                    sp.dma_start(w1[:, e, :, :], ins["L1_ffn_W1"][e].rearrange("(k p) n -> p k n", p=P)).then_inc(s_w, 16)
                    sp.dma_start(w2[:, e, :, :], ins["L1_ffn_W2"][e].rearrange("(c p) n -> p c n", p=P)).then_inc(s_w, 16)

                def store(i, k):
                    t = 2 * i + k
                    sp.wait_ge(s_fin, t + 1)
                    sp.dma_start(out[bass.ds(t * TN, TN), :], acc[k][:, :]).then_inc(s_out[k], 16)
                pairs(sp, store)
                sp.wait_ge(s_out[0], 16 * 13)
                sp.wait_ge(s_out[1], 16 * 12)

            @block.gpsimd
            def _(pool):
                nc.gpsimd.memset(lower[:, :, :], 1.0).then_inc(s_low, 1)
                pool.wait_ge(s_low, 1)
                nc.gpsimd.affine_select(out=lower[:, :, :], in_=lower[:, :, :], compare_op=ALU.is_gt, fill=0.0, base=0,
                                        pattern=[[1, X0], [-1, X0]], channel_multiplier=0).then_inc(s_low, 1)

            @block.vector
            def _(dve):
                ch = Chain(dve, s_dch, 10 + X0)
                dve.wait_ge(s_w1, 96)
                dve.wait_ge(s_low, 2)

                def tile(i, k):
                    t = 2 * i + k
                    ch.at(t)
                    nc.vector.tensor_scalar(xs[k][:, :], flat(s.y[:, bass.ds(t, 1), :]), s.mv[:, bass.ds(t, 1), 0],
                                            s.rstd[:, bass.ds(t, 1)], ALU.subtract, ALU.mult).then_inc(s_xs, 1)
                    dve.wait_ge(s_lg, t + 1)
                    ch.link(nc.vector.tensor_tensor(lg[:, :], psL[0:TN, 0:X0], br[:, :], ALU.add))
                    others = lg[:, :].unsqueeze(1).to_broadcast([TN, X0, X0])
                    own = lg[:, :].unsqueeze(2).to_broadcast([TN, X0, X0])
                    ch.link(nc.vector.tensor_reduce(m1[:, :], lg[:, :], AX.X, ALU.max))
                    nc.vector.tensor_scalar(lm[:, :], lg[:, :], m1[:, 0:1], None, ALU.subtract).then_inc(s_lgs, 1)
                    ch.link(nc.vector.tensor_tensor(eq[:, :, :], others, own, ALU.is_equal))
                    ch.link(nc.vector.tensor_tensor(eq[:, :, :], eq[:, :, :], lower[:, :, :], ALU.mult))
                    ch.link(nc.vector.tensor_tensor(cmp_[:, :, :], others, own, ALU.is_gt))
                    ch.link(nc.vector.tensor_tensor(cmp_[:, :, :], cmp_[:, :, :], eq[:, :, :], ALU.add))
                    ch.link(nc.vector.tensor_reduce(rank[:, :], cmp_[:, :, :], AX.X, ALU.add))
                    dve.wait_ge(s_ex, t + 1)
                    ch.link(nc.vector.scalar_tensor_tensor(out=ex[:, :], in0=rank[:, :], scalar=2.0, in1=ex[:, :],
                                                           op0=ALU.is_lt, op1=ALU.mult))
                    ch.link(nc.vector.tensor_reduce(sm[:, :], ex[:, :], AX.X, ALU.add))
                    ch.link(nc.vector.reciprocal(sm[:, :], sm[:, :]))
                    nc.vector.tensor_scalar(gate[:, :], ex[:, :], sm[:, 0:1], None, ALU.mult).then_inc(s_gate, 1)
                    dve.wait_ge(s_gt, t + 1)
                    nc.vector.tensor_copy(gT[:, :], psS[0:X0, P:P + TN]).then_inc(s_gT, 1)
                    dve.wait_ge(s_gate, t + 1)
                    dve.wait_ge(s_b, t + 1)
                    after(dve, s_out[k], 16 * i)
                    row = flat(s.x[:, bass.ds(t, 1), :])
                    ch.link(nc.vector.tensor_tensor(acc[k][:, :], psS[0:TN, D:2 * D], row, ALU.add))
                    for e in range(X0):
                        dve.wait_ge(s_y, X0 * t + e + 1)
                        step = nc.vector.scalar_tensor_tensor(out=acc[k][:, :], in0=turn_of(psY, e)[0:TN, 0:D],
                                                              scalar=gate[:, e:e + 1], in1=acc[k][:, :], op0=ALU.mult, op1=ALU.add)
                        if e < X0 - 1:
                            ch.link(step)
                            dve.sem_inc(s_yev, 1)
                        else:
                            step.then_inc(s_fin, 1)
                            dve.wait_ge(s_fin, t + 1)
                            dve.sem_inc(s_yev, 1)
                pairs(dve, tile)

            @block.scalar
            def _(act):
                act.wait_ge(s_w1, 96)

                def tile(i, k):
                    t = 2 * i + k
                    act.wait_ge(s_tr, t + 1)
                    for c in range(KD):
                        nc.scalar.activation(xT[k][:, c, :], psT[:, c * TN:(c + 1) * TN], ACT.Identity,
                                             bias=be[:, c:c + 1], scale=ga[:, c:c + 1]).then_inc(s_xT, 1)
                    act.wait_ge(s_lgs, t + 1)
                    after(act, s_gate, t)
                    nc.scalar.activation(ex[:, :], lm[:, :], ACT.Exp).then_inc(s_ex, 1)
                    for e in range(X0):
                        act.wait_ge(s_h, X0 * t + e + 1)
                        after(act, s_y, X0 * t + e - 1)
                        for c in range(C1):
                            nc.scalar.activation(hT[e % 2][:, c, :], psH[e % 2][:, c * TN:(c + 1) * TN], ACT.Gelu,
                                                 bias=b1[:, e, c:c + 1]).then_inc(s_hT, 1)
                pairs(act, tile)

            @block.tensor
            def _(pe):
                pe.wait_ge(s_w1, 96)

                def tile(i, k):
                    t = 2 * i + k
                    pe.wait_ge(s_xs, t + 1)
                    after(pe, s_xT, KD * t)
                    for c in range(KD):
                        last = nc.tensor.transpose(psT[:, c * TN:(c + 1) * TN], xs[k][:, c * P:(c + 1) * P], s.ident[0:TN, 0:TN])
                    last.then_inc(s_tr, 1)
                    pe.wait_ge(s_xT, KD * t + KD)
                    after(pe, s_gate, t)
                    for c in range(KD):
                        last = nc.tensor.matmul(psL[0:TN, 0:X0], xT[k][:, c, :], wr[:, c, :], start=(c == 0), stop=(c == KD - 1))
                    last.then_inc(s_lg, 1)
                    if isinstance(i, int) and i == 0 and k == 0:
                        pe.wait_ge(s_w, 32 * X0)

                    def up(e):
                        if isinstance(t, int) and t == 0:
                            after(pe, s_hT, C1 * (e - 1))
                        else:
                            pe.wait_ge(s_hT, C1 * X0 * t + C1 * (e - 1))
                        for m in range(C1):
                            for c in range(KD):
                                last = nc.tensor.matmul(psH[e % 2][:, m * TN:(m + 1) * TN], w1[:, e, c, m * P:(m + 1) * P], xT[k][:, c, :],
                                                        start=(c == 0), stop=(c == KD - 1))
                        last.then_inc(s_h, 1)

                    def down(e):
                        if isinstance(t, int) and t == 0:
                            after(pe, s_yev, e - 2)
                        else:
                            pe.wait_ge(s_yev, X0 * t + e - 2 if e >= 3 else X0 * t)
                        pe.wait_ge(s_hT, C1 * X0 * t + C1 * (e + 1))
                        for m in range(C1):
                            last = nc.tensor.matmul(turn_of(psY, e)[0:TN, 0:D], hT[e % 2][:, m, :], w2[:, e, m, :], start=(m == 0), stop=(m == C1 - 1))
                        last.then_inc(s_y, 1)
                    up(0)
                    for e in range(X0):
                        if e < X0 - 1:
                            up(e + 1)
                        if e == 1:
                            pe.wait_ge(s_gate, t + 1)
                            nc.tensor.transpose(psS[0:X0, P:P + TN], gate[:, :], s.ident[0:TN, 0:TN]).then_inc(s_gt, 1)
                            pe.wait_ge(s_gT, t + 1)
                            nc.tensor.matmul(psS[0:TN, D:2 * D], gT[:, :], b2[:, :], start=True, stop=True).then_inc(s_b, 1)
                        down(e)
                pairs(pe, tile)


def program(nc, ins, outs):
    with ExitStack() as ctx:
        ctx.enter_context(nc.allow_non_contiguous_dma(reason="bias vectors, one element to a partition"))
        s = build_shared(nc, ctx, ins)
        with layer(nc, s) as held:
            stage_prepare(nc, s, ins)
            stage_ln(nc, s, s.x, "x")
            build_layer0(nc, s, held)
            stage_project(nc, s, ins)
            stage_attention(nc, s, ins)
            stage_fold(nc, s, ins)
            stage_mix_attend(nc, s, ins)
            stage_ln(nc, s, s.y, "m")
            stage_mix_mlp(nc, s, ins)
            stage_ln(nc, s, s.x, "e")
            stage_experts0(nc, s, ins)
        with layer(nc, s) as held:
            stage_ln(nc, s, s.x, "f")
            with ExitStack() as mixer:
                build_layer1(nc, s, mixer)
                stage_project1(nc, s, ins)
                stage_relations(nc, s, ins)
                build_moments(nc, s, mixer)
                stage_moments(nc, s, 0)
                stage_moments(nc, s, 1)
                stage_batchnorm(nc, s, ins)
                stage_mix1(nc, s, ins)
            stage_ln(nc, s, s.x, "g")
            stage_normalise(nc, s)
            stage_ln(nc, s, s.y, "h")
            stage_experts1(nc, s, ins, outs[0])


_INS = ['x', 'src', 'dst', 'edge_type_8', 'L0_gnn_Wq', 'L0_gnn_Wk', 'L0_gnn_Wv', 'L0_mix_w_qkv', 'L0_mix_b_qkv', 'L0_mix_norm_g', 'L0_mix_norm_b', 'L0_mix_w_fc1', 'L0_mix_b_fc1', 'L0_mix_w_fc2', 'L0_mix_b_fc2', 'L0_ffn_W1', 'L0_ffn_b1', 'L0_ffn_Wg', 'L0_ffn_bg', 'L0_ffn_Wd', 'L0_ffn_bd', 'L1_gnn_weight', 'L1_gnn_gamma', 'L1_gnn_beta', 'L1_mix_Wqkv', 'L1_mix_bqkv', 'L1_mix_Wproj', 'L1_mix_bproj', 'L1_mix_temperature', 'L1_ffn_gamma', 'L1_ffn_beta', 'L1_ffn_Wr', 'L1_ffn_br', 'L1_ffn_W1', 'L1_ffn_b1', 'L1_ffn_W2', 'L1_ffn_b2']
_OUTS = [((3125, 256), 'float32')]


def kernel(**inputs):
    import numpy as _np
    import concourse.bacc as _bacc
    from concourse import mybir as _mybir
    from concourse.bass_utils import run_bass_kernel_spmd as _run

    nc = _bacc.Bacc("TRN2", target_bir_lowering=False, num_devices=1)
    arrays, args = {}, {}
    for name in _INS:
        a = _np.ascontiguousarray(inputs[name])
        arrays[f"in_{name}_dram"] = a
        args[name] = nc.dram_tensor(f"in_{name}_dram", a.shape, _mybir.dt.from_np(a.dtype), kind="ExternalInput").ap()
    outs = []
    for i, (shape, dtype) in enumerate(_OUTS):
        dt = _mybir.dt.from_np(_np.dtype(dtype))
        outs.append(nc.dram_tensor(f"out_{i}_dram", shape, dt, kind="ExternalOutput").ap())
    program(nc, args, outs)
    r = _run(nc, [arrays], core_ids=[0])
    return r.results[0]["out_0_dram"]
```

```python
import numpy as np
from contextlib import ExitStack, contextmanager

import concourse.bass as bass
from concourse import mybir

F32 = mybir.dt.float32
I32 = mybir.dt.int32
U32 = mybir.dt.uint32
ALU = mybir.AluOpType
ACT = mybir.ActivationFunctionType
AX = mybir.AxisListType

N = 3125
D = 256
TN = 125
NT = N // TN
P = 128
KD = D // P
E = 103125
UJ = 3
UE = TN * UJ
NU = E // UE
UC = 5
UP = NU // UC
NB = 6
NUP = NU + NB - 1
NPASS = -(-NU // NB)
HG, DK = 8, 32
HM, DM = 4, 64
R = 8
EPS = 1e-5
FM = 3 * D
CM = FM // P
F0, C0 = 1024, 8
X0 = 8
F1, C1 = 512, 4
TILES0 = (N + X0 * (TN - 1)) // TN
TILES1 = (2 * N + X0 * (TN - 1)) // TN
NS = DK // 2 + 1
HH = 4
VE = DK + 1


class Chain:

    def __init__(self, eng, sem, per_step):
        self.eng, self.sem, self.per, self.step, self.n = eng, sem, per_step, 0, 0

    def at(self, step):
        assert self.n in (0, self.per), (self.n, self.per)
        self.step, self.n = step, 0

    def link(self, ins):
        self.n += 1
        ins.then_inc(self.sem, 1)
        self.eng.wait_ge(self.sem, self.step * self.per + self.n)


def pairs(eng, body):
    body(0, 0)
    body(0, 1)
    with eng.Fori(1, NT // 2) as i:
        body(i, 0)
        body(i, 1)
    body(NT // 2, 0)


def later(b):
    return not isinstance(b, int) or b > 0


def duos(eng, tiles, *parts):
    peeled = max(1, *(lag for lag, body in parts))
    last, odd = (tiles - 1) // 2, tiles % 2

    def pair(i, slots):
        for lag, body in parts:
            if not isinstance(i, int) or i >= lag:
                body(i - lag, slots if lag == 0 else (0, 1))
    for i in range(peeled):
        pair(i, (0, 1))
    with eng.Fori(peeled, tiles // 2) as i:
        pair(i, (0, 1))
    if odd:
        pair(last, (0,))
    for lag, body in parts:
        for i in range(last - lag + 1, last + 1):
            body(i, (0,) if odd and i == last else (0, 1))


def after(eng, sem, value):
    if not isinstance(value, int) or value > 0:
        eng.wait_ge(sem, value)


def bcast(ap1, n):
    return ap1.rearrange("(a f) -> a f", a=1).partition_broadcast(n) if hasattr(ap1, "partition_broadcast") else ap1


class Shared:
    pass


@contextmanager
def layer(nc, s):
    with ExitStack() as held:
        nums = []

        def new_sem(name):
            sem = held.enter_context(nc.semaphore(name))
            nums.append(sem.num)
            return sem
        s.new_sem = new_sem
        yield held
        nums.sort()
        nc.all_engine_barrier()
        starts = [n for n in nums if n - 1 not in nums]
        for a in starts:
            nc.gpsimd.sem_clear(range(a, next(n for n in range(a, a + len(nums) + 1) if n not in nums)))
        nc.all_engine_barrier()


def build_shared(nc, ctx, ins):
    s = Shared()
    s.sb = lambda name, shape, dt=F32: ctx.enter_context(nc.sbuf_tensor(name, shape, dt))
    s.x = s.sb("x_res", [TN, NT, D])
    s.y = s.sb("y_res", [TN, NT, D])
    s.ident = s.sb("ident", [P, P])
    s.srci = s.sb("srci", [TN, NUP, UJ], I32)
    s.reli = s.sb("reli", [TN, NUP, UJ], I32)
    s.dstf = s.sb("dstf", [TN, NUP, UJ])
    s.meta = s.sb("meta", [1, 3, NT], I32)
    s.iota_f = s.sb("iota_f", [TN, TN])
    s.iota_p = s.sb("iota_p", [TN, 1])
    s.mv = s.sb("mv", [TN, NT, 2])
    s.rstd = s.sb("rstd", [TN, NT])
    s.zero = s.sb("zero", [P, 512])
    dr = lambda name, shape: nc.dram_tensor(name, shape, F32, kind="Internal").ap()
    s.kv_d = dr("kv_d", [N, 2 * D])
    s.q_d = dr("q_d", [N, D])
    s.xnT_d = dr("xnT_d", [NT, P, KD, TN])
    s.h_d = dr("h_d", [N * R, D])
    s.dst_d = nc.dram_tensor("dst_d", [NUP * UE], I32, kind="Internal").ap()
    s.sorted_d = dr("sorted_d", [TILES1 * TN, D])
    s.done_d = dr("done_d", [TILES1 * TN, D])
    s.scattered = [ctx.enter_context(nc.semaphore(f"scattered{k}")) for k in range(2)]
    s.scattered_n, s.gathered_n = [0] * 2, [0] * 4
    s.gathered = [ctx.enter_context(nc.semaphore(f"gathered{k}")) for k in range(4)]
    s.kv_gathered, s.rows_gathered = ([ctx.enter_context(nc.semaphore(f"{n}_gathered{a}")) for a in range(NB)]
                                      for n in ("kv", "rows"))
    return s


def build_layer0(nc, s, ctx):
    sb = lambda name, shape: ctx.enter_context(nc.sbuf_tensor(name, shape, F32))
    s.wqf = sb("wqf", [P, KD, D])
    s.bqf = sb("bqf", [TN, D])
    s.kvm = sb("kvm", [P, 2 * P])


def stage_prepare(nc, s, ins):
    with ExitStack() as ctx:
        sb = lambda name, shape, dt=F32: ctx.enter_context(nc.sbuf_tensor(name, shape, dt))
        raw = {k: sb("raw_" + k, [UP, UC, UE], I32) for k in ("dst", "src", "rel")}
        flt = {k: sb("flt_" + k, [UP, UC, UE]) for k in ("dst", "src", "rel")}
        mx = sb("mx", [UP, UC])
        mn = sb("mn", [UP, UC])
        b125 = sb("b125", [UP, NT])
        gup = sb("gup", [UP, UC])
        gdn = sb("gdn", [UP, UC])
        ov1 = sb("ov1", [UP, UC, NT])
        ov2 = sb("ov2", [UP, UC, NT])
        hl = sb("hl", [UP, UC, 2 * NT])
        red = sb("red", [2 * NT, 1])
        row = sb("row", [1, 2 * NT])
        m = sb("mrow", [1, 5, NT])
        npass = sb("npass", [1, NPASS])
        more = sb("more", [1, NT, NPASS])
        pad = sb("pad", [TN, (NB - 1) * UJ], I32)
        ps = [ctx.enter_context(nc.psum_tensor(f"prep_ps{i}", [P, 512], F32)) for i in range(4)]
        sem = lambda name: s.new_sem("p_" + name)
        s_x, s_raw = sem("x"), {k: sem("raw_" + k) for k in raw}
        s_const, s_iota, s_dst, s_pad, s_clear = (sem(n) for n in ("const", "iota", "dst", "pad", "clear"))
        s_flt, s_tr, s_ev, s_hl, s_hlt, s_red, s_row, s_dch = (
            sem(n) for n in ("flt", "tr", "ev", "hl", "hlt", "red", "row", "dch"))
        order = ("dst", "src", "rel")
        target = {"dst": s.dstf, "src": s.srci, "rel": s.reli}
        with nc.Block() as block:
            @block.sync
            def _(sp):
                for k, a in (("dst", ins["dst"]), ("src", ins["src"]), ("rel", ins["edge_type_8"])):
                    sp.dma_start(raw[k][:, :, :], a.rearrange("(c p f) -> p c f", c=UC, p=UP)).then_inc(s_raw[k], 16)
                sp.dma_start(s.dst_d[0:E].rearrange("(p f) -> p f", p=TN), ins["dst"].rearrange("(p f) -> p f", p=TN)).then_inc(s_dst, 16)
                sp.wait_ge(s_pad, 4)
                sp.dma_start(s.dst_d[E:].rearrange("(p f) -> p f", p=TN), pad[:, :]).then_inc(s_dst, 16)
                sp.dma_start(s.x[:, :, :], ins["x"].rearrange("(t p) d -> p t d", p=TN)).then_inc(s_x, 16)
                sp.wait_ge(s_iota, 6)
                sp.dma_start(s.sorted_d.rearrange("(t p) d -> p t d", p=TN),
                             s.zero[0:TN, 0:D].unsqueeze(1).to_broadcast([TN, TILES1, D])).then_inc(s_clear, 16)
                sp.wait_ge(s_x, 16)
                sp.wait_ge(s_dst, 32)
                sp.wait_ge(s_clear, 16)

            @block.gpsimd
            def _(pool):
                nc.gpsimd.iota(b125[:, :], pattern=[[TN, NT]], base=0, channel_multiplier=0,
                               allow_small_or_imprecise_dtypes=True).then_inc(s_iota, 1)
                nc.gpsimd.iota(gup[:, :], pattern=[[UP, UC]], base=1, channel_multiplier=1,
                               allow_small_or_imprecise_dtypes=True).then_inc(s_iota, 1)
                nc.gpsimd.iota(s.iota_f[:, :], pattern=[[1, TN]], base=0, channel_multiplier=0,
                               allow_small_or_imprecise_dtypes=True).then_inc(s_iota, 1)
                nc.gpsimd.iota(s.iota_p[:, :], pattern=[[0, 1]], base=0, channel_multiplier=1,
                               allow_small_or_imprecise_dtypes=True).then_inc(s_iota, 1)
                nc.gpsimd.memset(s.zero[:, :], 0.0).then_inc(s_iota, 1)
                nc.gpsimd.iota(npass[:, :], pattern=[[NB, NPASS]], base=0, channel_multiplier=0,
                               allow_small_or_imprecise_dtypes=True).then_inc(s_iota, 1)
                nc.gpsimd.memset(s.ident[:, :], 0.0).then_inc(s_const, 1)
                pool.wait_ge(s_const, 1)
                nc.gpsimd.affine_select(out=s.ident[:, :], in_=s.ident[:, :], compare_op=ALU.not_equal, fill=1.0,
                                        base=0, pattern=[[-1, P]], channel_multiplier=1).then_inc(s_const, 1)

            @block.vector
            def _(dve):
                ch = Chain(dve, s_dch, 100)
                nc.vector.memset(pad[:, :], -1).then_inc(s_pad, 1)
                nc.vector.memset(s.dstf[:, NU:NUP, :], -1.0).then_inc(s_pad, 1)
                nc.vector.memset(s.srci[:, NU:NUP, :], 0).then_inc(s_pad, 1)
                nc.vector.memset(s.reli[:, NU:NUP, :], 0).then_inc(s_pad, 1)
                for k in ("dst", "src"):
                    dve.wait_ge(s_raw[k], 16)
                    nc.vector.tensor_copy(flt[k][:, :, :], raw[k][:, :, :]).then_inc(s_flt, 1)
                dve.wait_ge(s_raw["rel"], 16)
                dve.wait_ge(s_flt, 2)
                nc.vector.scalar_tensor_tensor(out=flt["rel"][:, :, :], in0=flt["src"][:, :, :], scalar=float(R),
                                               in1=raw["rel"][:, :, :], op0=ALU.mult, op1=ALU.add).then_inc(s_flt, 1)
                ch.link(nc.vector.tensor_reduce(mx[:, :], flt["dst"][:, :, :], AX.X, ALU.max))
                ch.link(nc.vector.tensor_reduce(mn[:, :], flt["dst"][:, :, :], AX.X, ALU.min))
                ch.link(nc.vector.tensor_scalar(mn[:, :], mn[:, :], -(TN - 1.0), None, ALU.add))
                dve.wait_ge(s_iota, 6)
                ch.link(nc.vector.tensor_scalar(gdn[:, :], gup[:, :], -1.0, NU + 1.0, ALU.mult, ALU.add))
                for c in range(UC):
                    nc.vector.tensor_scalar(ov1[:, c, :], b125[:, :], mx[:, c:c + 1], None, ALU.is_le).then_inc(s_dch, 1)
                    ch.n += 1
                    ch.link(nc.vector.tensor_scalar(ov2[:, c, :], b125[:, :], mn[:, c:c + 1], None, ALU.is_ge))
                ch.link(nc.vector.tensor_tensor(ov1[:, :, :], ov1[:, :, :], ov2[:, :, :], ALU.mult))
                for c in range(UC):
                    nc.vector.tensor_scalar(hl[:, c, 0:NT], ov1[:, c, :], gup[:, c:c + 1], None, ALU.mult).then_inc(s_hl, 1)
                    nc.vector.tensor_scalar(hl[:, c, NT:2 * NT], ov1[:, c, :], gdn[:, c:c + 1], None, ALU.mult).then_inc(s_hl, 1)
                for n, (k, c) in enumerate((k, c) for k in order for c in range(UC)):
                    dve.wait_ge(s_tr, n + 1)
                    nc.vector.tensor_copy(target[k][:, c * UP:(c + 1) * UP, :].rearrange("p u j -> p j u"),
                                          ps[n % 2][0:TN, 0:UJ * UP].rearrange("p (j u) -> p j u", j=UJ)).then_inc(s_ev, 1)
                dve.wait_ge(s_hlt, 1)
                nc.vector.tensor_reduce(red[:, :], ps[2][0:2 * NT, 0:UC * UP], AX.X, ALU.max).then_inc(s_red, 1)
                dve.wait_ge(s_row, 1)
                ch.link(nc.vector.tensor_copy(row[:, :], ps[3][0:1, 0:2 * NT]))
                ch.link(nc.vector.tensor_scalar(m[:, 0, :], row[:, NT:2 * NT], -1.0, float(NU), ALU.mult, ALU.add))
                ch.link(nc.vector.tensor_scalar(m[:, 0, :], m[:, 0, :], NU - 1.0, None, ALU.min))
                ch.link(nc.vector.tensor_scalar(m[:, 3, :], m[:, 0, :], 1.0, None, ALU.add))
                ch.link(nc.vector.tensor_tensor(m[:, 1, :], row[:, 0:NT], m[:, 3, :], ALU.max))
                ch.link(nc.vector.tensor_tensor(m[:, 3, :], m[:, 1, :], m[:, 0, :], ALU.subtract))
                ch.link(nc.vector.tensor_tensor(more[:, :, :], npass[:, :].unsqueeze(1).to_broadcast([1, NT, NPASS]),
                                                m[:, 3, :].unsqueeze(2).to_broadcast([1, NT, NPASS]), ALU.is_lt))
                ch.link(nc.vector.tensor_reduce(m[:, 3, :], more[:, :, :], AX.X, ALU.add))
                ch.link(nc.vector.memset(m[:, 4, :], 0.0))
                for b in range(1, NT):
                    ch.link(nc.vector.tensor_tensor(m[:, 4, b:b + 1], m[:, 4, b - 1:b], m[:, 3, b - 1:b], ALU.add))
                ch.link(nc.vector.tensor_copy(s.meta[:, 0, :], m[:, 4, :]))
                ch.link(nc.vector.tensor_tensor(m[:, 3, :], m[:, 4, :], m[:, 3, :], ALU.add))
                ch.link(nc.vector.tensor_copy(s.meta[:, 1, :], m[:, 3, :]))
                ch.link(nc.vector.scalar_tensor_tensor(out=m[:, 2, :], in0=m[:, 4, :], scalar=-float(NB), in1=m[:, 0, :],
                                                       op0=ALU.mult, op1=ALU.add))
                ch.link(nc.vector.tensor_copy(s.meta[:, 2, :], m[:, 2, :]))

            @block.tensor
            def _(pe):
                pe.wait_ge(s_const, 2)
                for n, (k, c) in enumerate((k, c) for k in order for c in range(UC)):
                    pe.wait_ge(s_flt, order.index(k) + 1)
                    if n >= 2:
                        pe.wait_ge(s_ev, n - 1)
                    for j in range(UJ):
                        last = nc.tensor.transpose(ps[n % 2][0:TN, j * UP:(j + 1) * UP],
                                                   flt[k][:, c, :].rearrange("p (e j) -> p e j", j=UJ)[:, :, j],
                                                   s.ident[0:UP, 0:UP])
                    last.then_inc(s_tr, 1)
                pe.wait_ge(s_hl, 2 * UC)
                for c in range(UC):
                    last = nc.tensor.transpose(ps[2][0:2 * NT, c * UP:(c + 1) * UP], hl[:, c, :], s.ident[0:UP, 0:UP])
                last.then_inc(s_hlt, 1)
                pe.wait_ge(s_red, 1)
                nc.tensor.transpose(ps[3][0:1, 0:2 * NT], red[:, :], s.ident[0:2 * NT, 0:2 * NT]).then_inc(s_row, 1)


def stage_ln(nc, s, src, tag):
    with ExitStack() as ctx:
        st = ctx.enter_context(nc.sbuf_tensor(f"st_{tag}", [TN, NT, 6], F32))
        sd = ctx.enter_context(nc.sbuf_tensor(f"sd_{tag}", [TN, NT], F32))
        s_st, s_var, s_sd, s_mv = (s.new_sem(f"ln_{n}_{tag}") for n in ("st", "var", "sd", "mv"))
        with nc.Block() as block:
            @block.vector
            def _(dve):
                with dve.Fori(0, NT) as t:
                    nc.vector.bn_stats(st[:, bass.ds(t, 1), :], src[:, bass.ds(t, 1), :]).then_inc(s_st, 1)
                dve.wait_ge(s_st, NT)
                for t in range(NT):
                    nc.vector.bn_aggr(s.mv[:, t, :], st[:, t, :]).then_inc(s_mv, 1)
                dve.wait_ge(s_mv, NT)
                nc.vector.tensor_scalar(sd[:, :], s.mv[:, :, 1], EPS, None, ALU.add).then_inc(s_var, 1)
                dve.wait_ge(s_sd, 1)
                nc.vector.reciprocal(s.rstd[:, :], sd[:, :])

            @block.scalar
            def _(act):
                act.wait_ge(s_var, 1)
                nc.scalar.activation(sd[:, :], sd[:, :], ACT.Sqrt).then_inc(s_sd, 1)


def stage_project(nc, s, ins):
    W = 5 * D
    with ExitStack() as ctx:
        sb = lambda name, shape, dt=F32: ctx.enter_context(nc.sbuf_tensor(name, shape, dt))
        sem = lambda name: s.new_sem("a_" + name)
        pb = lambda name: ctx.enter_context(nc.psum_tensor(name, [P, 512], F32))
        w = sb("w_proj", [P, KD, W])
        bias = sb("b_proj", [TN, 2 * D])
        xs = [sb(f"xs{i}", [TN, D]) for i in range(2)]
        xT = [sb(f"xT{i}", [P, KD, TN]) for i in range(2)]
        kvs = [sb(f"kvs{i}", [TN, 2 * D]) for i in range(2)]
        qs = [sb(f"qs{i}", [TN, D]) for i in range(2)]
        km = [sb(f"km{i}", [TN, 2 * D]) for i in range(2)]
        psT = [pb(f"psT{i}") for i in range(2)]
        psKV, psQ, psM, psA = (pb(n) for n in ("psKV", "psQ", "psM", "psA"))
        s_w, s_b, s_xs, s_tr, s_xT, s_kv, s_q, s_m, s_kvs, s_qs, s_km, s_y, s_acc, s_a0 = (
            sem(n) for n in ("w", "b", "xs", "tr", "xT", "kv", "q", "m", "kvs", "qs", "km", "y", "acc", "a0"))
        s_xTo, s_kvo, s_qo = ([sem(f"{n}{i}") for i in range(2)] for n in ("xTo", "kvo", "qo"))
        with nc.Block() as block:
            @block.sync
            def _(sp):
                sp.dma_start(w[:, :, 0:D], ins["L0_gnn_Wk"].rearrange("(k p) n -> p k n", p=P)).then_inc(s_w, 16)
                sp.dma_start(w[:, :, D:2 * D], ins["L0_gnn_Wv"].rearrange("(k p) n -> p k n", p=P)).then_inc(s_w, 16)
                sp.dma_start(w[:, :, 2 * D:3 * D], ins["L0_gnn_Wq"].rearrange("(k p) n -> p k n", p=P)).then_inc(s_w, 16)
                sp.dma_start(w[:, :, 3 * D:5 * D],
                             ins["L0_mix_w_qkv"][:, D:3 * D].rearrange("(k p) n -> p k n", p=P)).then_inc(s_w, 16)
                sp.dma_start(bias[:, :], ins["L0_mix_b_qkv"][D:3 * D].partition_broadcast(TN)).then_inc(s_b, 16)

                def store(i, k):
                    t = 2 * i + k
                    sp.wait_ge(s_xT, t + 1)
                    sp.dma_start(s.xnT_d[bass.ds(t, 1)].rearrange("a p k n -> p (a k) n"), xT[k][:, :, :]).then_inc(s_xTo[k], 16)
                    sp.wait_ge(s_kvs, t + 1)
                    sp.dma_start(s.kv_d[bass.ds(t * TN, TN), :], kvs[k][:, :]).then_inc(s_kvo[k], 16)
                    sp.wait_ge(s_qs, t + 1)
                    sp.dma_start(s.q_d[bass.ds(t * TN, TN), :], qs[k][:, :]).then_inc(s_qo[k], 16)
                pairs(sp, store)
                for k in range(2):
                    for sm in (s_xTo[k], s_kvo[k], s_qo[k]):
                        sp.wait_ge(sm, 16 * (13 - k))

            @block.vector
            def _(dve):
                def norm(i, k):
                    t = 2 * i + k
                    after(dve, s_y, 2 * i + k - 1)
                    nc.vector.tensor_scalar(xs[k][:, :], s.x[:, bass.ds(t, 1), :].rearrange("p a d -> p (a d)"),
                                            s.mv[:, bass.ds(t, 1), 0], s.rstd[:, bass.ds(t, 1)],
                                            ALU.subtract, ALU.mult).then_inc(s_xs, 1)
                    dve.wait_ge(s_tr, t + 1)
                    after(dve, s_xTo[k], 16 * i)
                    nc.vector.tensor_copy(xT[k][:, :, :], psT[k][:, 0:KD * TN].rearrange("p (k n) -> p k n", k=KD)).then_inc(s_xT, 1)
                    dve.wait_ge(s_q, t + 1)
                    after(dve, s_qo[k], 16 * i)
                    nc.vector.tensor_copy(qs[k][:, :], psQ[0:TN, 0:D]).then_inc(s_qs, 1)
                    dve.wait_ge(s_b, 16)
                    dve.wait_ge(s_m, t + 1)
                    after(dve, s_acc, 2 * i + k - 1)
                    nc.vector.tensor_tensor(km[k][:, :], psM[0:TN, :], bias[:, :], ALU.add).then_inc(s_km, 1)
                pairs(dve, norm)
                dve.wait_ge(s_acc, NT + 1)
                nc.vector.tensor_copy(s.kvm[:, :], psA[:, 0:2 * P])

            @block.scalar
            def _(act):
                def evac(i, k):
                    t = 2 * i + k
                    act.wait_ge(s_xs, t + 1)
                    nc.scalar.activation(s.y[:, bass.ds(t, 1), :].rearrange("p a d -> p (a d)"), xs[k][:, :], ACT.Copy).then_inc(s_y, 1)
                    act.wait_ge(s_kv, t + 1)
                    after(act, s_kvo[k], 16 * i)
                    nc.scalar.activation(kvs[k][:, :], psKV[0:TN, :], ACT.Copy).then_inc(s_kvs, 1)
                pairs(act, evac)

            @block.tensor
            def _(pe):
                nc.tensor.matmul(psA[:, 0:2 * P], s.zero[0:TN, 0:P], s.zero[0:TN, 0:2 * P], start=True, stop=False)
                pe.wait_ge(s_w, 64)

                def tile(i, k):
                    t = 2 * i + k
                    pe.wait_ge(s_xs, t + 1)
                    for c in range(KD):
                        last = nc.tensor.transpose(psT[k][:, c * TN:(c + 1) * TN], xs[k][:, c * P:(c + 1) * P], s.ident[0:TN, 0:TN])
                    last.then_inc(s_tr, 1)
                    pe.wait_ge(s_xT, t + 1)
                    for ps, lo, hi, free, done in ((psKV, 0, 2 * D, s_kvs, s_kv), (psQ, 2 * D, 3 * D, s_qs, s_q), (psM, 3 * D, 5 * D, s_km, s_m)):
                        after(pe, free, t)
                        for c in range(KD):
                            last = nc.tensor.matmul(ps[0:TN, 0:hi - lo], xT[k][:, c, :], w[:, c, lo:hi], start=(c == 0), stop=(c == KD - 1))
                        last.then_inc(done, 1)
                    pe.wait_ge(s_km, t + 1)
                    for h in range(2):
                        last = nc.tensor.matmul(psA[:, h * P:(h + 1) * P], km[k][:, h * P:(h + 1) * P],
                                                km[k][:, D + h * P:D + (h + 1) * P], start=False, stop=False)
                    last.then_inc(s_acc, 1)
                pairs(pe, tile)
                nc.tensor.matmul(psA[:, 0:2 * P], s.zero[0:TN, 0:P], s.zero[0:TN, 0:2 * P], start=False, stop=True).then_inc(s_acc, 1)


def each_block(nc, eng, s, one_pass, start=None, middle=None, end=None, finish=None):
    def block(b):
        first = eng.value_load(s.meta[0:1, 0, bass.ds(b, 1)], min_val=0, max_val=NPASS * NT)
        stop = eng.value_load(s.meta[0:1, 1, bass.ds(b, 1)], min_val=1, max_val=NPASS * NT)
        shift = eng.value_load(s.meta[0:1, 2, bass.ds(b, 1)], min_val=-NB * NPASS * NT, max_val=NU - 1)

        def step(n, is_first):
            g = nc.s_assert_within(n * NB + shift, 0, NU - 1, skip_runtime_bounds_check_because=(
                "a pass starts below its block's last unit, and that is at most NU - 1"))
            one_pass(b, g, n, is_first)
        if start:
            start(b, first)
        if start or middle:
            step(first, True)
            if middle:
                middle(b)
            with eng.Fori(first + 1, stop) as n:
                step(n, False)
        else:
            with eng.Fori(first, stop) as n:
                step(n, False)
        if end:
            end(b)
    if start or middle or end:
        block(0)
        with eng.Fori(1, NT) as b:
            block(b)
    else:
        with eng.Fori(0, NT) as b:
            block(b)
    if finish:
        finish(eng.value_load(s.meta[0:1, 1, NT - 1:NT], min_val=1, max_val=NPASS * NT) - 1)


def stage_attention(nc, s, ins):
    CLIP = 5.0 * float(np.sqrt(DK))
    W = D + HG
    with ExitStack() as ctx:
        sb = lambda name, shape, dt=F32: ctx.enter_context(nc.sbuf_tensor(name, shape, dt))
        sem = lambda name: s.new_sem("g_" + name)
        q = sb("q_all", [TN, NT, D])
        nodes = sb("nodes", [TN, NT])
        units = []
        for a in range(NB):
            u = Shared()
            u.a = a
            u.drow = sb(f"drow{a}", [TN, UE], I32)
            u.idx = sb(f"idx{a}", [TN, UJ], I32)
            u.kv = sb(f"kv{a}", [TN, UJ, 2 * D])
            u.oT = sb(f"oT{a}", [TN, UJ, TN])
            u.oh = sb(f"oh{a}", [TN, UJ, TN])
            u.prod = sb(f"prod{a}", [TN, UJ, D])
            u.red = sb(f"red{a}", [TN, UJ, HG])
            u.wv = sb(f"wv{a}", [TN, UJ, W])
            u.s_kv = s.kv_gathered[a]
            u.s_row, u.s_idx, u.s_oT, u.s_g, u.s_clip, u.s_sc, u.s_wv, u.s_sct, u.s_ot, u.s_oh = (
                sem(f"{name}{a}") for name in ("row", "idx", "oT", "g", "clip", "sc", "wv", "sct", "ot", "oh"))
            units.append(u)
        zr = sb("zr", [TN, HG])
        gat = sb("gat", [TN, D])
        psG = [ctx.enter_context(nc.psum_tensor(f"psG{i}", [P, 1024], F32)) for i in range(2)]
        psH = [ctx.enter_context(nc.psum_tensor(f"g_psH{i}", [P, 512], F32)) for i in range(2)]
        psO = ctx.enter_context(nc.psum_tensor("psO", [P, 512], F32))
        s_q, s_blk, s_out, s_red, s_bch, s_go, s_prod, s_nodes, s_off, s_here = (
            sem(n) for n in ("q", "blk", "out", "red", "bch", "go", "prod", "nodes", "off", "here"))
        with nc.Block() as block:
            @block.sync
            def _(sp):
                sp.dma_start(q[:, :, :], s.q_d.rearrange("(t p) d -> p t d", p=TN)).then_inc(s_q, 16)

                def load(b, g, n, first):
                    for u in units:
                        sp.wait_ge(u.s_oT, n + 1)
                        sp.dma_start(u.drow[:, :], s.dst_d[bass.ds((g + u.a) * UE, UE)].partition_broadcast(TN)).then_inc(u.s_row, 16)
                each_block(nc, sp, s, load)

            @block.gpsimd
            def _(pool):
                nc.gpsimd.iota(nodes[:, :], pattern=[[-TN, NT]], base=0, channel_multiplier=-1,
                               allow_small_or_imprecise_dtypes=True).then_inc(s_nodes, 1)

                def gather(b, g, n, first):
                    for u in units:
                        pool.wait_ge(u.s_wv, n + 1)
                        nc.gpsimd.tensor_copy(u.idx[:, :], s.srci[:, bass.ds(g + u.a, 1), :]).then_inc(u.s_idx, 1)
                        pool.wait_ge(u.s_idx, n + 1)
                        pool.sem_inc(s_go, 1)
                        for j in range(UJ):
                            nc.gpsimd.indirect_dma_start(
                                out=u.kv[:, j, :], out_offset=None, in_=s.kv_d,
                                in_offset=bass.IndirectOffsetOnAxis(ap=u.idx[:, j:j + 1], axis=0)).then_inc(u.s_kv, 16)
                each_block(nc, pool, s, gather)

            @block.vector
            def _(dve):
                dve.sem_inc(s_prod, len(psG))
                for u in units:
                    dve.sem_inc(u.s_wv, 1)

                def scores(n, u, weigh_one):
                    turn = NB * n + u.a
                    dve.wait_ge(u.s_kv, 16 * UJ * n + 16 * UJ)
                    dve.wait_ge(u.s_g, n + 1)
                    nc.vector.tensor_tensor(u.prod[:, :, :], u.kv[:, :, 0:D],
                                            turn_of(psG, u.a)[0:TN, 0:UJ * D].rearrange("p (j d) -> p j d", d=D), ALU.mult).then_inc(s_prod, 1)
                    if weigh_one:
                        weigh(*weigh_one)
                    dve.wait_ge(s_prod, turn + 1 + len(psG))
                    nc.vector.tensor_reduce(u.red[:, :, :], u.prod[:, :, :].rearrange("p j (h d) -> p j h d", h=HG),
                                            AX.X, ALU.add).then_inc(s_red, 1)
                    dve.wait_ge(u.s_sct, n + 1)
                    dve.wait_ge(s_red, turn + 1)
                    nc.vector.tensor_scalar(u.red[:, :, :], u.red[:, :, :], -CLIP, CLIP, ALU.max, ALU.min).then_inc(u.s_clip, 1)

                def weigh(n, u):
                    dve.wait_ge(u.s_sc, n + 1)
                    nc.vector.tensor_tensor(u.wv[:, :, 0:D].rearrange("p j (h d) -> p j h d", h=HG),
                                            u.kv[:, :, D:2 * D].rearrange("p j (h d) -> p j h d", h=HG),
                                            u.wv[:, :, D:W].unsqueeze(3).to_broadcast([TN, UJ, HG, DK]),
                                            ALU.mult).then_inc(u.s_wv, 1)

                def close(b):
                    dve.wait_ge(s_blk, b + 1)
                    nc.vector.tensor_scalar(zr[:, :], psO[0:TN, D:W], 1e-9, None, ALU.add).then_inc(s_bch, 1)
                    dve.wait_ge(s_bch, 2 * b + 1)
                    nc.vector.reciprocal(zr[:, :], zr[:, :]).then_inc(s_bch, 1)
                    dve.wait_ge(s_bch, 2 * b + 2)
                    nc.vector.tensor_tensor(gat[:, :].rearrange("p (h d) -> p h d", h=HG),
                                            psO[0:TN, 0:D].rearrange("p (h d) -> p h d", h=HG),
                                            zr[:, :].unsqueeze(2).to_broadcast([TN, HG, DK]), ALU.mult).then_inc(s_out, 1)
                    dve.wait_ge(s_out, b + 1)
                    nc.vector.tensor_tensor(flat(s.x[:, bass.ds(b, 1), :]), flat(s.x[:, bass.ds(b, 1), :]), gat[:, :], ALU.add)

                def start(b, n):
                    if later(b):
                        weigh(n - 1, units[-1])
                        close(b - 1)

                def one_pass(b, g, n, first):
                    for u in units:
                        before = (n, units[u.a - 1]) if u.a else None if first else (n - 1, units[-1])
                        scores(n, u, before)

                def finish(n):
                    weigh(n, units[-1])
                    close(NT - 1)
                each_block(nc, dve, s, one_pass, start=start, finish=finish)

            @block.scalar
            def _(act):
                for u in units:
                    act.sem_inc(u.s_oh, 1)
                    act.sem_inc(u.s_oT, 1)
                act.wait_ge(s_nodes, 1)

                def offsets(b, n, u):
                    act.wait_ge(u.s_row, 16 * n + 16)
                    act.sem_inc(s_here, 1)
                    nc.scalar.activation(u.oT[:, :, :], u.drow[:, :].rearrange("p (e j) -> p j e", j=UJ), ACT.Abs,
                                         bias=nodes[:, bass.ds(b, 1)]).then_inc(s_off, 1)

                def onehots(n, u):
                    act.wait_ge(s_off, NB * n + u.a + 1)
                    nc.scalar.activation(u.oT[:, :, :], u.oT[:, :, :], ACT.Relu, bias=1.0, scale=-1.0).then_inc(u.s_oT, 1)

                def copy_turned(n, u):
                    act.wait_ge(u.s_sct, n + 1)
                    act.wait_ge(u.s_ot, n + 1)
                    nc.scalar.activation(u.oh[:, :, :], turn_of(psH, u.a)[0:TN, 0:UJ * TN].rearrange("p (j d) -> p j d", j=UJ),
                                         ACT.Copy).then_inc(u.s_oh, 1)

                def weights(n, u):
                    act.wait_ge(u.s_clip, n + 1)
                    nc.scalar.activation(u.wv[:, :, D:W], u.red[:, :, :], ACT.Exp, scale=1.0 / float(np.sqrt(DK))).then_inc(u.s_sc, 1)

                def step(b, n, u, n_old, old):
                    offsets(b, n, u)
                    if old:
                        copy_turned(n_old, old)
                    onehots(n, u)
                    if old:
                        weights(n_old, old)

                def start(b, n):
                    for k in range(2):
                        step(b, n, units[k], n - 1, units[k - 2] if later(b) else None)

                def one_pass(b, g, n, first):
                    if not first:
                        for k in range(2):
                            step(b, n, units[k], n - 1, units[k - 2])
                    for u in units[2:]:
                        step(b, n, u, n, units[u.a - 2])

                def finish(n):
                    for u in units[-2:]:
                        copy_turned(n, u)
                        weights(n, u)
                each_block(nc, act, s, one_pass, start=start, finish=finish)

            @block.tensor
            def _(pe):
                for u in units:
                    pe.sem_inc(u.s_sct, 1)
                pe.wait_ge(s_q, 16)

                def open_sums(b):
                    after(pe, s_out, b)
                    nc.tensor.matmul(psO[0:TN, 0:W], s.zero[0:TN, 0:TN], s.zero[0:TN, 0:W], start=True, stop=False)

                def close_sums():
                    nc.tensor.matmul(psO[0:TN, 0:W], s.zero[0:TN, 0:TN], s.zero[0:TN, 0:W], start=False, stop=True).then_inc(s_blk, 1)

                def spread(b, n, u):
                    pe.wait_ge(u.s_oT, n + 2)
                    pe.wait_ge(s_prod, NB * n + u.a + 1)
                    for j in range(UJ):
                        last = nc.tensor.matmul(turn_of(psG, u.a)[0:TN, j * D:(j + 1) * D], u.oT[:, j, :],
                                                flat(q[:, bass.ds(b, 1), :]), start=True, stop=True)
                    last.then_inc(u.s_g, 1)
                    if u.a >= len(psH):
                        pe.wait_ge(units[u.a - len(psH)].s_oh, n + 2)
                    else:
                        pe.wait_ge(units[u.a - len(psH)].s_oh, n + 1)
                    for j in range(UJ):
                        last = nc.tensor.transpose(turn_of(psH, u.a)[0:TN, j * TN:(j + 1) * TN], u.oT[:, j, :], s.ident[0:TN, 0:TN])
                    last.then_inc(u.s_ot, 1)

                def add_up(n, u):
                    pe.wait_ge(u.s_oh, n + 2)
                    pe.wait_ge(u.s_wv, n + 2)
                    for j in range(UJ):
                        last = nc.tensor.matmul(psO[0:TN, 0:W], u.oh[:, j, :], u.wv[:, j, :], start=False, stop=False)
                    last.then_inc(u.s_sct, 1)

                def start(b, n):
                    spread(b, n, units[0])
                    spread(b, n, units[1])
                    if later(b):
                        add_up(n - 1, units[-2])
                        add_up(n - 1, units[-1])
                        close_sums()
                    open_sums(b)

                def one_pass(b, g, n, first):
                    if not first:
                        spread(b, n, units[0])
                        add_up(n - 1, units[-2])
                        spread(b, n, units[1])
                        add_up(n - 1, units[-1])
                    for u in units[2:]:
                        spread(b, n, u)
                        add_up(n, units[u.a - 2])

                def finish(n):
                    add_up(n, units[-2])
                    add_up(n, units[-1])
                    close_sums()
                each_block(nc, pe, s, one_pass, start=start, finish=finish)


def turn_of(buffers, n):
    return buffers[n % len(buffers)]


def flat(ap):
    return ap.rearrange("p a d -> p (a d)")


def stage_fold(nc, s, ins):
    with ExitStack() as ctx:
        sb = lambda name, shape, dt=F32: ctx.enter_context(nc.sbuf_tensor(name, shape, dt))
        sem = lambda name: s.new_sem("f_" + name)
        pb = lambda name: ctx.enter_context(nc.psum_tensor(name, [P, 512], F32))
        wq = sb("wq_raw", [P, KD, D])
        wqT = sb("wqT", [P, 2, D])
        bq = sb("bq_col", [P, 2])
        bqw = sb("bq_wide", [P, 2, TN])
        a = sb("attn", [P, 2, DM])
        amx = sb("attn_max", [P, 2])
        bd = sb("attn_diag", [P, 2, P])
        bt = sb("attn_turned", [P, 2, P])
        psW, psB, psF, psb = (pb(n) for n in ("psW", "psB", "psF", "psb"))
        s_w, s_b, s_wt, s_wte, s_sub, s_exp, s_bd, s_bt, s_bte, s_f, s_dch = (
            sem(n) for n in ("w", "b", "wt", "wte", "sub", "exp", "bd", "bt", "bte", "f", "dch"))
        with nc.Block() as block:
            @block.sync
            def _(sp):
                sp.dma_start(wq[:, :, :], ins["L0_mix_w_qkv"][:, 0:D].rearrange("(k p) n -> p k n", p=P)).then_inc(s_w, 16)
                sp.dma_start(bq[:, :], ins["L0_mix_b_qkv"][0:D].rearrange("(c p) -> p c", p=P)).then_inc(s_b, 16)

            @block.vector
            def _(dve):
                ch = Chain(dve, s_dch, 100)
                ch.link(nc.vector.memset(bd[:, :, :], 0.0))
                kv = s.kvm[:, :].rearrange("p (c n) -> p c n", c=2)
                for h in range(2):
                    rows = slice(h * DM, (h + 1) * DM)
                    ch.link(nc.vector.tensor_copy(a[rows, :, :], kv[rows, :, h * DM:(h + 1) * DM]))
                ch.link(nc.vector.tensor_reduce(amx[:, :], a[:, :, :], AX.X, ALU.max))
                nc.vector.tensor_tensor(a[:, :, :], a[:, :, :], amx[:, :].unsqueeze(2).to_broadcast([P, 2, DM]),
                                        ALU.subtract).then_inc(s_sub, 1)
                dve.wait_ge(s_exp, 1)
                ch.link(nc.vector.tensor_reduce(amx[:, :], a[:, :, :], AX.X, ALU.add))
                ch.link(nc.vector.reciprocal(amx[:, :], amx[:, :]))
                for h in range(2):
                    rows = slice(h * DM, (h + 1) * DM)
                    nc.vector.tensor_tensor(bd[rows, :, h * DM:(h + 1) * DM], a[rows, :, :],
                                            amx[rows, :].unsqueeze(2).to_broadcast([DM, 2, DM]), ALU.mult).then_inc(s_bd, 1)
                dve.wait_ge(s_wt, 1)
                nc.vector.tensor_copy(wqT[:, :, :], psW[:, :].rearrange("p (c n) -> p c n", c=2)).then_inc(s_wte, 1)
                dve.wait_ge(s_b, 16)
                nc.vector.tensor_copy(bqw[:, :, :], bq[:, :].unsqueeze(2).to_broadcast([P, 2, TN])).then_inc(s_wte, 1)
                dve.wait_ge(s_bt, 1)
                nc.vector.tensor_copy(bt[:, :, :], psB[:, 0:2 * P].rearrange("p (c n) -> p c n", c=2)).then_inc(s_bte, 1)
                dve.wait_ge(s_f, 1)
                nc.vector.tensor_copy(s.wqf[:, :, :], psF[:, :].rearrange("p (k n) -> p k n", k=KD))
                nc.vector.tensor_copy(s.bqf[:, :], psb[0:TN, 0:D])

            @block.scalar
            def _(act):
                act.wait_ge(s_sub, 1)
                nc.scalar.activation(a[:, :, :], a[:, :, :], ACT.Exp, scale=float(DM) ** -0.5).then_inc(s_exp, 1)

            @block.tensor
            def _(pe):
                pe.wait_ge(s_w, 16)
                for c in range(2):
                    for k in range(KD):
                        last = nc.tensor.transpose(psW[:, c * D + k * P:c * D + (k + 1) * P], wq[:, k, c * P:(c + 1) * P], s.ident[:, :])
                last.then_inc(s_wt, 1)
                pe.wait_ge(s_bd, 2)
                for c in range(2):
                    last = nc.tensor.transpose(psB[:, c * P:(c + 1) * P], bd[:, c, :], s.ident[:, :])
                last.then_inc(s_bt, 1)
                pe.wait_ge(s_wte, 2)
                pe.wait_ge(s_bte, 1)
                for c in range(2):
                    for k in range(KD):
                        nc.tensor.matmul(psF[:, k * D + c * P:k * D + (c + 1) * P], wqT[:, c, k * P:(k + 1) * P], bt[:, c, :], start=True, stop=True)
                    last = nc.tensor.matmul(psb[0:TN, c * P:(c + 1) * P], bqw[:, c, :], bt[:, c, :], start=True, stop=True)
                last.then_inc(s_f, 1)


def stage_mix_attend(nc, s, ins):
    with ExitStack() as ctx:
        sb = lambda name, shape, dt=F32: ctx.enter_context(nc.sbuf_tensor(name, shape, dt))
        sem = lambda name: s.new_sem("m_" + name)
        xT = [sb(f"mxT{i}", [P, KD, TN]) for i in range(2)]
        att = [sb(f"att{i}", [TN, D]) for i in range(2)]
        psF = [ctx.enter_context(nc.psum_tensor(f"mpsF{i}", [P, 512], F32)) for i in range(2)]
        s_f, s_att, s_y = (sem(n) for n in ("f", "att", "y"))
        s_xT = [sem(f"xT{i}") for i in range(2)]
        with nc.Block() as block:
            @block.sync
            def _(sp):
                def load(i, k):
                    t = 2 * i + k
                    after(sp, s_f, 2 * i + k - 1)
                    sp.dma_start(xT[k][:, :, :], s.xnT_d[bass.ds(t, 1)].rearrange("a p k n -> p (a k) n")).then_inc(s_xT[k], 16)
                pairs(sp, load)

            @block.tensor
            def _(pe):
                def tile(i, k):
                    t = 2 * i + k
                    pe.wait_ge(s_xT[k], 16 * i + 16)
                    after(pe, s_att, 2 * i + k - 1)
                    for c in range(KD):
                        last = nc.tensor.matmul(psF[k][0:TN, 0:D], xT[k][:, c, :], s.wqf[:, c, :], start=(c == 0), stop=(c == KD - 1))
                    last.then_inc(s_f, 1)
                pairs(pe, tile)

            @block.vector
            def _(dve):
                def tile(i, k):
                    t = 2 * i + k
                    dve.wait_ge(s_f, t + 1)
                    nc.vector.tensor_tensor(att[k][:, :], psF[k][0:TN, 0:D], s.bqf[:, :], ALU.add).then_inc(s_att, 1)
                    dve.wait_ge(s_att, t + 1)
                    nc.vector.tensor_tensor(flat(s.y[:, bass.ds(t, 1), :]), flat(s.y[:, bass.ds(t, 1), :]), att[k][:, :], ALU.add)
                pairs(dve, tile)


def stage_mix_mlp(nc, s, ins):
    with ExitStack() as ctx:
        sb = lambda name, shape, dt=F32: ctx.enter_context(nc.sbuf_tensor(name, shape, dt))
        sem = lambda name: s.new_sem("n_" + name)
        pb = lambda name: ctx.enter_context(nc.psum_tensor("n_" + name, [P, 512], F32))
        w1 = sb("w_fc1", [P, KD, FM])
        w2 = sb("w_fc2", [P, CM, D])
        b1 = sb("b_fc1", [P, CM])
        b2 = sb("b_fc2", [TN, D])
        g = sb("norm_g", [P, KD])
        b = sb("norm_b", [P, KD])
        xs = [sb(f"n_xs{i}", [TN, D]) for i in range(2)]
        xT = [sb(f"n_xT{i}", [P, KD, TN]) for i in range(2)]
        hT = [sb(f"n_hT{i}", [P, CM, TN]) for i in range(2)]
        o = [sb(f"n_o{i}", [TN, D]) for i in range(2)]
        psT = [pb(f"psT{i}") for i in range(2)]
        psH = [[pb(f"psH{i}{j}") for j in range(2)] for i in range(2)]
        psY = [pb(f"psY{i}") for i in range(2)]
        s_w, s_xs, s_tr, s_xT, s_h, s_hT, s_y, s_o, s_dch = (sem(n) for n in ("w", "xs", "tr", "xT", "h", "hT", "y", "o", "dch"))
        HB = CM // 2
        with nc.Block() as block:
            @block.sync
            def _(sp):
                sp.dma_start(w1[:, :, :], ins["L0_mix_w_fc1"].rearrange("(k p) n -> p k n", p=P)).then_inc(s_w, 16)
                sp.dma_start(w2[:, :, :], ins["L0_mix_w_fc2"].rearrange("(c p) n -> p c n", p=P)).then_inc(s_w, 16)
                sp.dma_start(b1[:, :], ins["L0_mix_b_fc1"].rearrange("(c p) -> p c", p=P)).then_inc(s_w, 16)
                sp.dma_start(g[:, :], ins["L0_mix_norm_g"].rearrange("(c p) -> p c", p=P)).then_inc(s_w, 16)
                sp.dma_start(b[:, :], ins["L0_mix_norm_b"].rearrange("(c p) -> p c", p=P)).then_inc(s_w, 16)
                sp.dma_start(b2[:, :], ins["L0_mix_b_fc2"].partition_broadcast(TN)).then_inc(s_w, 16)

            @block.vector
            def _(dve):
                ch = Chain(dve, s_dch, 2)
                dve.wait_ge(s_w, 96)

                def norm(i, slots):
                    for k in slots:
                        t = 2 * i + k
                        after(dve, s_tr, 2 * i)
                        nc.vector.tensor_scalar(xs[k][:, :], flat(s.y[:, bass.ds(t, 1), :]), s.mv[:, bass.ds(t, 1), 0],
                                                s.rstd[:, bass.ds(t, 1)], ALU.subtract, ALU.mult).then_inc(s_xs, 1)

                def add(i, slots):
                    for k in slots:
                        t = 2 * i + k
                        ch.at(t)
                        dve.wait_ge(s_y, t + 1)
                        ch.link(nc.vector.tensor_tensor(o[k][:, :], psY[k][0:TN, 0:D], b2[:, :], ALU.add))
                        ch.link(nc.vector.tensor_tensor(o[k][:, :], o[k][:, :], flat(s.y[:, bass.ds(t, 1), :]), ALU.add))
                        nc.vector.tensor_tensor(flat(s.x[:, bass.ds(t, 1), :]), flat(s.x[:, bass.ds(t, 1), :]), o[k][:, :],
                                                ALU.add).then_inc(s_o, 1)
                duos(dve, NT, (0, norm), (1, add))

            @block.scalar
            def _(act):
                act.wait_ge(s_w, 96)

                def scale(i, slots):
                    for k in slots:
                        act.wait_ge(s_tr, 2 * i + k + 1)
                        for c in range(KD):
                            nc.scalar.activation(xT[k][:, c, :], psT[k][:, c * TN:(c + 1) * TN], ACT.Identity,
                                                 bias=b[:, c:c + 1], scale=g[:, c:c + 1]).then_inc(s_xT, 1)

                def gelu(i, slots):
                    for k in slots:
                        t = 2 * i + k
                        for c in range(CM):
                            if c % HB == 0:
                                act.wait_ge(s_h, 2 * t + 1 + c // HB)
                            nc.scalar.activation(hT[k][:, c, :], psH[k][c // HB][:, (c % HB) * TN:(c % HB + 1) * TN], ACT.Gelu,
                                                 bias=b1[:, c:c + 1]).then_inc(s_hT, 1)
                duos(act, NT, (0, scale), (0, gelu))

            @block.tensor
            def _(pe):
                pe.wait_ge(s_w, 96)

                def turn(i, slots):
                    for k in slots:
                        pe.wait_ge(s_xs, 2 * i + k + 1)
                        for c in range(KD):
                            last = nc.tensor.transpose(psT[k][:, c * TN:(c + 1) * TN], xs[k][:, c * P:(c + 1) * P], s.ident[0:TN, 0:TN])
                        last.then_inc(s_tr, 1)

                def up(i, slots):
                    for k in slots:
                        t = 2 * i + k
                        pe.wait_ge(s_xT, KD * t + KD)
                        for m in range(CM):
                            for c in range(KD):
                                last = nc.tensor.matmul(psH[k][m // HB][:, (m % HB) * TN:(m % HB + 1) * TN], w1[:, c, m * P:(m + 1) * P], xT[k][:, c, :],
                                                        start=(c == 0), stop=(c == KD - 1))
                            if m % HB == HB - 1:
                                last.then_inc(s_h, 1)

                def down(i, slots):
                    for k in slots:
                        t = 2 * i + k
                        after(pe, s_o, 2 * i)
                        for m in range(CM):
                            if m % HB == 0:
                                pe.wait_ge(s_hT, CM * t + m + HB)
                            last = nc.tensor.matmul(psY[k][0:TN, 0:D], hT[k][:, m, :], w2[:, m, :], start=(m == 0), stop=(m == CM - 1))
                        last.then_inc(s_y, 1)
                duos(pe, NT, (0, turn), (1, down), (0, up))


def expert_of(r, eng, t):
    return eng.value_load(r.expert[0:1, bass.ds(t, 1)], min_val=0, max_val=X0 - 1)


def stage_route(nc, s, r, tag):
    K = r.K
    LAST = X0 - 1.0
    with ExitStack() as ctx:
        sb = lambda name, shape, dt=F32: ctx.enter_context(nc.sbuf_tensor(tag + name, shape, dt))
        sem = lambda name: s.new_sem(tag + name)
        lower = sb("lower", [TN, X0, X0])
        tri, one = sb("tri", [TN, TN]), sb("one", [TN, TN])
        steps, tiles = sb("steps", [TN, NT]), sb("tiles", [1, r.tiles])
        m1, sm = sb("m1", [TN, NT]), sb("sm", [TN, NT])
        ex, sc, rank, chosen, place = (sb(n, [TN, NT, X0]) for n in ("ex", "sc", "rank", "chosen", "place"))
        total, before = sb("total", [TN, NT, X0]), [sb(f"before{i}", [TN, NT, X0]) for i in range(2)]
        cmp_, eq = sb("cmp", [TN, NT, X0, X0]), sb("eq", [TN, NT, X0, X0])
        need, used, end, start = sb("need", [TN, X0, NT]), sb("used", [TN, X0]), sb("end", [TN, X0]), sb("start", [TN, X0])
        sel, val = sb("sel", [TN, NT, X0]), sb("val", [TN, NT])
        past, own_tile = sb("past", [1, r.tiles, X0]), sb("own_tile", [1, r.tiles])
        ps = ctx.enter_context(nc.psum_tensor(tag + "ps", [P, 512], F32))
        s_const, s_ex, s_exd, s_ch, s_cnt, s_dch = (sem(n) for n in ("const", "ex", "exd", "ch", "cnt", "dch"))
        W = NT * X0
        flat3 = lambda ap: ap.rearrange("p t e -> p (t e)")
        wide = lambda ap: ap.unsqueeze(2).to_broadcast([TN, NT, X0])
        with nc.Block() as block:
            @block.gpsimd
            def _(pool):
                nc.gpsimd.iota(steps[:, :], pattern=[[TN, NT]], base=0, channel_multiplier=0,
                               allow_small_or_imprecise_dtypes=True).then_inc(s_const, 1)
                nc.gpsimd.iota(tiles[:, :], pattern=[[1, r.tiles]], base=0, channel_multiplier=0,
                               allow_small_or_imprecise_dtypes=True).then_inc(s_const, 1)
                nc.gpsimd.memset(one[:, :], 1.0).then_inc(s_const, 1)
                nc.gpsimd.memset(lower[:, :, :], 1.0).then_inc(s_const, 1)
                pool.wait_ge(s_const, 4)
                nc.gpsimd.affine_select(out=lower[:, :, :], in_=lower[:, :, :], compare_op=ALU.is_gt, fill=0.0, base=0,
                                        pattern=[[1, X0], [-1, X0]], channel_multiplier=0).then_inc(s_const, 1)

            @block.vector
            def _(dve):
                ch = Chain(dve, s_dch, 100)
                do = nc.vector
                ch.link(do.tensor_reduce(m1[:, :], r.lg[:, :, :], AX.X, ALU.max))
                do.tensor_tensor(ex[:, :, :], r.lg[:, :, :], wide(m1[:, :]), ALU.subtract).then_inc(s_ex, 1)
                do.tensor_scalar(tri[:, :], s.iota_f[:, :], s.iota_p[:, 0:1], None, ALU.is_gt).then_inc(s_ch, 1)

                def gates():
                    ch.link(do.tensor_reduce(sm[:, :], ex[:, :, :], AX.X, ALU.add))
                    ch.link(do.reciprocal(sm[:, :], sm[:, :]))
                    ch.link(do.tensor_tensor(sc[:, :, :], ex[:, :, :], wide(sm[:, :]), ALU.mult))
                dve.wait_ge(s_exd, 1)
                if K == 1:
                    gates()
                key = sc if K == 1 else r.lg
                dve.wait_ge(s_const, 5)
                others = key[:, :, :].unsqueeze(2).to_broadcast([TN, NT, X0, X0])
                own = key[:, :, :].unsqueeze(3).to_broadcast([TN, NT, X0, X0])
                ch.link(do.tensor_tensor(eq[:, :, :, :], others, own, ALU.is_equal))
                ch.link(do.tensor_tensor(eq[:, :, :, :], eq[:, :, :, :], lower[:, :, :].unsqueeze(1).to_broadcast([TN, NT, X0, X0]), ALU.mult))
                ch.link(do.tensor_tensor(cmp_[:, :, :, :], others, own, ALU.is_gt))
                ch.link(do.tensor_tensor(cmp_[:, :, :, :], cmp_[:, :, :, :], eq[:, :, :, :], ALU.add))
                ch.link(do.tensor_reduce(rank[:, :, :], cmp_[:, :, :, :], AX.X, ALU.add))
                do.tensor_scalar(chosen[:, :, :], rank[:, :, :], float(K), None, ALU.is_lt).then_inc(s_ch, 1)
                if K == 2:
                    dve.wait_ge(s_ch, 2)
                    ch.link(do.tensor_tensor(ex[:, :, :], ex[:, :, :], chosen[:, :, :], ALU.mult))
                    gates()
                dve.wait_ge(s_cnt, 1)
                ch.link(do.tensor_copy(flat3(total[:, :, :]), ps[0:TN, 256:256 + W]))
                ch.link(do.tensor_copy(flat3(before[0][:, :, :]), ps[0:TN, 256:256 + W]))
                shift, n = 1, 0
                while shift < NT:
                    a, b = before[n % 2], before[(n + 1) % 2]
                    ch.link(do.tensor_copy(b[:, 0:shift, :], a[:, 0:shift, :]))
                    ch.link(do.tensor_tensor(b[:, shift:, :], a[:, shift:, :], a[:, 0:NT - shift, :], ALU.add))
                    shift, n = 2 * shift, n + 1
                sums, free = before[n % 2], before[(n + 1) % 2]
                ch.link(do.tensor_tensor(need[:, :, :], steps[:, :].unsqueeze(1).to_broadcast([TN, X0, NT]),
                                         sums[:, NT - 1, :].unsqueeze(2).to_broadcast([TN, X0, NT]), ALU.is_lt))
                ch.link(do.tensor_reduce(used[:, :], need[:, :, :], AX.X, ALU.add))
                ch.link(do.tensor_copy(end[:, :], used[:, :]))
                for e in range(1, X0):
                    ch.link(do.tensor_tensor(end[:, e:e + 1], end[:, e:e + 1], end[:, e - 1:e], ALU.add))
                ch.link(do.tensor_tensor(start[:, :], end[:, :], used[:, :], ALU.subtract))
                ch.link(do.tensor_tensor(free[:, :, :], sums[:, :, :], total[:, :, :], ALU.subtract))
                ch.link(do.tensor_tensor(flat3(place[:, :, :]), flat3(free[:, :, :]), ps[0:TN, 0:W], ALU.add))
                ch.link(do.scalar_tensor_tensor(out=place[:, :, :], in0=start[:, :].unsqueeze(1).to_broadcast([TN, NT, X0]),
                                                scalar=float(TN), in1=place[:, :, :], op0=ALU.mult, op1=ALU.add))
                for k in range(K):
                    for what, to in ((place, r.pos), (sc, r.gate)):
                        ch.link(do.scalar_tensor_tensor(out=sel[:, :, :], in0=rank[:, :, :], scalar=float(k), in1=what[:, :, :],
                                                        op0=ALU.is_equal, op1=ALU.mult))
                        ch.link(do.tensor_reduce(val[:, :], sel[:, :, :], AX.X, ALU.add))
                        ch.link(do.tensor_copy(to[:, :, k], val[:, :]))
                ch.link(do.tensor_tensor(past[:, :, :], end[0:1, :].unsqueeze(1).to_broadcast([1, r.tiles, X0]),
                                         tiles[:, :].unsqueeze(2).to_broadcast([1, r.tiles, X0]), ALU.is_le))
                ch.link(do.tensor_reduce(own_tile[:, :], past[:, :, :], AX.X, ALU.add))
                ch.link(do.tensor_scalar(own_tile[:, :], own_tile[:, :], LAST, None, ALU.min))
                ch.link(do.tensor_copy(r.expert[:, :], own_tile[:, :]))

            @block.scalar
            def _(act):
                act.wait_ge(s_ex, 1)
                nc.scalar.activation(ex[:, :, :], ex[:, :, :], ACT.Exp).then_inc(s_exd, 1)

            @block.tensor
            def _(pe):
                pe.wait_ge(s_const, 5)
                pe.wait_ge(s_ch, 2)
                nc.tensor.matmul(ps[0:TN, 0:W], tri[:, :], flat3(chosen[:, :, :]), start=True, stop=True)
                nc.tensor.matmul(ps[0:TN, 256:256 + W], one[:, :], flat3(chosen[:, :, :]), start=True, stop=True).then_inc(s_cnt, 1)


def stage_dispatch(nc, s, r, tag):
    K = r.K
    with ExitStack() as ctx:
        sb = lambda name, shape, dt=F32: ctx.enter_context(nc.sbuf_tensor(tag + name, shape, dt))
        sem = lambda name: s.new_sem(tag + name)
        row = [sb(f"row{i}", [TN, D]) for i in range(2)]
        idx = [sb(f"idx{i}", [TN, K], I32) for i in range(2)]
        s_row, s_idx, s_go = (sem(n) for n in ("row", "idx", "go"))
        with nc.Block() as block:
            @block.scalar
            def _(act):
                def tile(i, k):
                    t = 2 * i + k
                    after(act, s.scattered[k], 16 * K * i + s.scattered_n[k])
                    nc.scalar.activation(row[k][:, :], flat(s.y[:, bass.ds(t, 1), :]), ACT.Copy).then_inc(s_row, 1)
                pairs(act, tile)

            @block.gpsimd
            def _(pool):
                def tile(i, k):
                    t = 2 * i + k
                    after(pool, s.scattered[k], 16 * K * i + s.scattered_n[k])
                    nc.gpsimd.tensor_copy(idx[k][:, :], flat(r.pos[:, bass.ds(t, 1), :])).then_inc(s_idx, 1)
                    pool.wait_ge(s_idx, t + 1)
                    pool.wait_ge(s_row, t + 1)
                    pool.sem_inc(s_go, 1)
                    for c in range(K):
                        nc.gpsimd.indirect_dma_start(out=s.sorted_d[0:r.tiles * TN, :], out_offset=bass.IndirectOffsetOnAxis(ap=idx[k][:, c:c + 1], axis=0),
                                                     in_=row[k][:, :], in_offset=None).then_inc(s.scattered[k], 16)
                pairs(pool, tile)
                pool.wait_ge(s.scattered[0], 16 * K * 13 + s.scattered_n[0])
                pool.wait_ge(s.scattered[1], 16 * K * 12 + s.scattered_n[1])
    s.scattered_n = [n + 16 * K * len(range(k, NT, 2)) for k, n in enumerate(s.scattered_n)]


def stage_combine(nc, s, r, out, tag):
    K = r.K
    with ExitStack() as ctx:
        sb = lambda name, shape, dt=F32: ctx.enter_context(nc.sbuf_tensor(tag + name, shape, dt))
        sem = lambda name: s.new_sem(tag + name)
        BUFS = 4
        row = [sb(f"row{i}", [TN, K, D]) for i in range(BUFS)]
        idx = [sb(f"idx{i}", [TN, K], I32) for i in range(BUFS)]
        acc = [sb(f"acc{i}", [TN, D]) for i in range(BUFS)]
        s_idx, s_go, s_acc, s_part, s_fin = (sem(n) for n in ("idx", "go", "acc", "part", "fin"))
        s_out = [sem(f"out{i}") for i in range(BUFS)]

        def tiles(eng, body):
            for k in range(BUFS):
                body(0, k)
            with eng.Fori(1, NT // BUFS) as i:
                for k in range(BUFS):
                    body(i, k)
            for k in range(NT % BUFS):
                body(NT // BUFS, k)
        with nc.Block() as block:
            @block.gpsimd
            def _(pool):
                def tile(i, k):
                    t = BUFS * i + k
                    after(pool, s_acc, BUFS * (i - 1) + k + 1 if not isinstance(i, int) or i > 0 else 0)
                    nc.gpsimd.tensor_copy(idx[k][:, :], flat(r.pos[:, bass.ds(t, 1), :])).then_inc(s_idx, 1)
                    pool.wait_ge(s_idx, t + 1)
                    pool.sem_inc(s_go, 1)
                    for c in range(K):
                        nc.gpsimd.indirect_dma_start(out=row[k][:, c, :], out_offset=None, in_=s.done_d[0:r.tiles * TN, :],
                                                     in_offset=bass.IndirectOffsetOnAxis(ap=idx[k][:, c:c + 1], axis=0)).then_inc(s.gathered[k], 16)
                tiles(pool, tile)

            @block.vector
            def _(dve):
                def tile(i, k):
                    t = BUFS * i + k
                    dve.wait_ge(s.gathered[k], 16 * K * i + 16 * K + s.gathered_n[k])
                    if out is not None:
                        after(dve, s_out[k], 16 * i)
                    here = flat(s.x[:, bass.ds(t, 1), :])
                    end = here if out is None else acc[k][:, :]
                    if K == 2:
                        nc.vector.scalar_tensor_tensor(out=acc[k][:, :], in0=row[k][:, 0, :], scalar=flat(r.gate[:, bass.ds(t, 1), 0:1]),
                                                       in1=here, op0=ALU.mult, op1=ALU.add).then_inc(s_part, 1)
                        dve.wait_ge(s_part, t + 1)
                        nc.vector.scalar_tensor_tensor(out=end, in0=row[k][:, 1, :], scalar=flat(r.gate[:, bass.ds(t, 1), 1:2]),
                                                       in1=acc[k][:, :], op0=ALU.mult, op1=ALU.add).then_inc(s_acc, 1)
                    else:
                        nc.vector.scalar_tensor_tensor(out=end, in0=row[k][:, 0, :], scalar=flat(r.gate[:, bass.ds(t, 1), 0:1]),
                                                       in1=here, op0=ALU.mult, op1=ALU.add).then_inc(s_acc, 1)
                tiles(dve, tile)

            if out is not None:
                @block.sync
                def _(sp):
                    def tile(i, k):
                        t = BUFS * i + k
                        sp.wait_ge(s_acc, t + 1)
                        sp.dma_start(out[bass.ds(t * TN, TN), :], acc[k][:, :]).then_inc(s_out[k], 16)
                    tiles(sp, tile)
                    for k in range(BUFS):
                        sp.wait_ge(s_out[k], 16 * len(range(k, NT, BUFS)))
    s.gathered_n = [n + 16 * K * len(range(k, NT, BUFS)) for k, n in enumerate(s.gathered_n)]


def stage_experts0(nc, s, ins):
    r = Shared()
    r.K, r.tiles = 1, TILES0
    with ExitStack() as own:
        sb = lambda name, shape, dt=F32: own.enter_context(nc.sbuf_tensor("e_" + name, shape, dt))
        r.lg, r.pos, r.gate = sb("lg", [TN, NT, X0]), sb("pos", [TN, NT, 1], I32), sb("gate", [TN, NT, 1])
        r.expert = sb("expert", [1, r.tiles], I32)
        w1 = sb("w1", [P, KD, F0])
        b1 = sb("b1", [P, C0])
        wg = sb("wg", [P, C0, X0])
        bg = sb("bg", [TN, X0])
        wd = sb("wd", [P, X0, C0, D])
        bd = sb("bd", [TN, X0, D])
        xs = [sb(f"xs{i}", [TN, D]) for i in range(2)]
        xT = [sb(f"xT{i}", [P, KD, TN]) for i in range(2)]
        hT = [sb(f"hT{i}", [P, C0, TN]) for i in range(2)]
        o = [sb(f"o{i}", [TN, D]) for i in range(2)]
        s_w1, s_w = s.new_sem("e_w1"), s.new_sem("e_w")

        for routing in (True, False):
            tiles = NT if routing else r.tiles
            with ExitStack() as ctx:
                tag = "er_" if routing else "ex_"
                psT, psY, psH0, psH1 = ([ctx.enter_context(nc.psum_tensor(f"{tag}{n}{i}", [P, 512], F32)) for i in range(2)]
                                        for n in ("psT", "psY", "psH0", "psH1"))
                psH = [psH0, psH1]
                s_xs, s_st = ([s.new_sem(f"{tag}{n}{i}") for i in range(2)] for n in ("xs", "st"))
                s_xse, s_tr, s_xT, s_h, s_hT, s_p, s_out = (s.new_sem(tag + n) for n in ("xse", "tr", "xT", "h", "hT", "p", "out"))
                with nc.Block() as block:
                    @block.sync
                    def _(sp):
                        if routing:
                            sp.dma_start(w1[:, :, :], ins["L0_ffn_W1"].rearrange("(k p) n -> p k n", p=P)).then_inc(s_w1, 16)
                            sp.dma_start(b1[:, :], ins["L0_ffn_b1"].rearrange("(c p) -> p c", p=P)).then_inc(s_w1, 16)
                            sp.dma_start(wg[:, :, :], ins["L0_ffn_Wg"].rearrange("(c p) e -> p c e", p=P)).then_inc(s_w1, 16)
                            sp.dma_start(bg[:, :], ins["L0_ffn_bg"].partition_broadcast(TN)).then_inc(s_w1, 16)
                            sp.dma_start(bd[:, :, :].rearrange("p e n -> p (e n)"), ins["L0_ffn_bd"].rearrange("e n -> (e n)").partition_broadcast(TN)).then_inc(s_w, 16)
                            for e in range(X0):
                                sp.dma_start(wd[:, e, :, :], ins["L0_ffn_Wd"][e].rearrange("(c p) n -> p c n", p=P)).then_inc(s_w, 16)
                        else:
                            def store(i, slots):
                                for k in slots:
                                    t = 2 * i + k
                                    sp.wait_ge(s_out, t + 1)
                                    sp.dma_start(s.done_d[bass.ds(t * TN, TN), :], o[k][:, :]).then_inc(s_st[k], 16)

                            def duo(i, slots):
                                for k in slots:
                                    t = 2 * i + k
                                    after(sp, s_tr, 2 * i)
                                    sp.dma_start(xs[k][:, :], s.sorted_d[bass.ds(t * TN, TN), :]).then_inc(s_xs[k], 16)
                            duos(sp, tiles, (0, duo), (1, store))
                            for k in range(2):
                                sp.wait_ge(s_st[k], 16 * len(range(k, tiles, 2)))

                    @block.vector
                    def _(dve):
                        dve.wait_ge(s_w1, 64)
                        if not routing:
                            dve.wait_ge(s_w, 16 * (X0 + 1))

                        def duo(i, slots):
                            if routing:
                                for k in slots:
                                    t = 2 * i + k
                                    after(dve, s_xse, 2 * i)
                                    nc.vector.tensor_scalar(xs[k][:, :], flat(s.x[:, bass.ds(t, 1), :]), s.mv[:, bass.ds(t, 1), 0],
                                                            s.rstd[:, bass.ds(t, 1)], ALU.subtract, ALU.mult).then_inc(s_xs[k], 16)
                            for k in slots:
                                t = 2 * i + k
                                dve.wait_ge(s_tr, t + 1)
                                nc.vector.tensor_copy(xT[k][:, :, :], psT[k][:, 0:KD * TN].rearrange("p (k n) -> p k n", k=KD)).then_inc(s_xT, 1)
                                if routing:
                                    nc.vector.tensor_scalar(flat(s.y[:, bass.ds(t, 1), :]), xs[k][:, :], 1.0, None, ALU.mult).then_inc(s_xse, 1)

                        def finish(i, slots):
                            for k in slots:
                                t = 2 * i + k
                                if routing:
                                    dve.wait_ge(s_p, t + 1)
                                    nc.vector.tensor_tensor(flat(r.lg[:, bass.ds(t, 1), :]), psY[k][0:TN, 0:X0], bg[:, :], ALU.add).then_inc(s_out, 1)
                                else:
                                    e = expert_of(r, dve, t)
                                    dve.wait_ge(s_p, t + 1)
                                    after(dve, s_st[k], 16 * i)
                                    nc.vector.tensor_tensor(o[k][:, :], psY[k][0:TN, 0:D], flat(bd[:, bass.ds(e, 1), :]), ALU.add).then_inc(s_out, 1)
                        duos(dve, tiles, (0, duo), (1, finish))

                    @block.scalar
                    def _(act):
                        act.wait_ge(s_w1, 64)

                        def duo(i, slots):
                            for k in slots:
                                t = 2 * i + k
                                for c in range(C0):
                                    if c % 4 == 0:
                                        act.wait_ge(s_h, 2 * t + 1 + c // 4)
                                    nc.scalar.activation(hT[k][:, c, :], psH[k][c // 4][:, (c % 4) * TN:(c % 4 + 1) * TN], ACT.Gelu,
                                                         bias=b1[:, c:c + 1]).then_inc(s_hT, 1)
                        duos(act, tiles, (0, duo))

                    @block.tensor
                    def _(pe):
                        pe.wait_ge(s_w1, 64)
                        if not routing:
                            pe.wait_ge(s_w, 16 * (X0 + 1))

                        def turn(i, slots):
                            for k in slots:
                                pe.wait_ge(s_xs[k], 16 * i + 16)
                                for c in range(KD):
                                    last = nc.tensor.transpose(psT[k][:, c * TN:(c + 1) * TN], xs[k][:, c * P:(c + 1) * P], s.ident[0:TN, 0:TN])
                                last.then_inc(s_tr, 1)

                        def up(i, slots):
                            for k in slots:
                                t = 2 * i + k
                                pe.wait_ge(s_xT, t + 1)
                                for m in range(C0):
                                    for c in range(KD):
                                        last = nc.tensor.matmul(psH[k][m // 4][:, (m % 4) * TN:(m % 4 + 1) * TN], w1[:, c, m * P:(m + 1) * P], xT[k][:, c, :],
                                                                start=(c == 0), stop=(c == KD - 1))
                                    if m % 4 == 3:
                                        last.then_inc(s_h, 1)

                        def down(i, slots):
                            for k in slots:
                                t = 2 * i + k
                                if not routing:
                                    e = expert_of(r, pe, t)
                                after(pe, s_out, 2 * i)
                                for m in range(C0):
                                    if m % 4 == 0:
                                        pe.wait_ge(s_hT, C0 * t + m + 4)
                                    if routing:
                                        last = nc.tensor.matmul(psY[k][0:TN, 0:X0], hT[k][:, m, :], wg[:, m, :], start=(m == 0), stop=(m == C0 - 1))
                                    else:
                                        last = nc.tensor.matmul(psY[k][0:TN, 0:D], hT[k][:, m, :], wd[:, bass.ds(e, 1), m, :].rearrange("p a n -> p (a n)"),
                                                                start=(m == 0), stop=(m == C0 - 1))
                                last.then_inc(s_p, 1)
                        duos(pe, tiles, (0, turn), (1, down), (0, up))
            if routing:
                stage_route(nc, s, r, "et_")
                stage_dispatch(nc, s, r, "ed_")
        stage_combine(nc, s, r, None, "ec_")


def rotations(dbl, h0):
    base = dbl[:, h0:h0 + HH, 0:DK]
    rows, heads, cols = base.ap
    return bass.AP(base.tensor, base.offset, [rows, [cols[0], NS], heads, cols])


def build_layer1(nc, s, ctx):
    sb = lambda name, shape: ctx.enter_context(nc.sbuf_tensor(name, shape, F32))
    s.q1 = sb("q1", [TN, NT + 1, D])


def build_keys(nc, s, ctx):
    sb = lambda name, shape: ctx.enter_context(nc.sbuf_tensor(name, shape, F32))
    s.k1 = s.y
    s.v1 = sb("v1", [TN, NT, D])


def build_moments(nc, s, ctx):
    s.mom = [ctx.enter_context(nc.sbuf_tensor(f"mom{g}", [P, NS + 1, HH * VE], F32)) for g in range(2)]
    s.mom0 = ctx.enter_context(nc.sbuf_tensor("mom_const", [TN, 2, HH * VE], F32))


def stage_project1(nc, s, ins):
    SC = float(DK) ** 0.25
    with ExitStack() as ctx:
        sb = lambda name, shape, dt=F32: ctx.enter_context(nc.sbuf_tensor("b_" + name, shape, dt))
        sem = lambda name: s.new_sem("b_" + name)
        pb = lambda name: ctx.enter_context(nc.psum_tensor("b_" + name, [P, 512], F32))
        NR = R * D // 512
        wr = sb("wr", [P, KD, R, D])
        wraw = sb("wraw", [P, 3 * KD, D])
        wT = sb("wT", [P, KD, 3 * D])
        bias = sb("bias", [TN, 3 * D])
        fac = sb("fac", [TN, 2 * HG])
        xs = [sb(f"xs{i}", [TN, D]) for i in range(2)]
        xT = [sb(f"xT{i}", [P, KD, TN]) for i in range(2)]
        hs = [sb(f"hs{i}", [TN, R * D]) for i in range(2)]
        qk = sb("qk", [TN, 2 * D])
        sq = sb("sq", [TN, 2 * D])
        nrm = sb("nrm", [TN, 2 * HG])
        psT = [pb(f"psT{i}") for i in range(2)]
        psR = [pb(f"psR{i}") for i in range(3)]
        psQ, psV = pb("psQ"), pb("psV")
        s_raw, s_w, s_b, s_wt, s_wte, s_fac, s_xs, s_tr, s_xT, s_r, s_hs, s_q, s_v, s_ss, s_sqrt, s_vo, s_qke, s_kept, s_dch = (
            sem(n) for n in ("raw", "w", "b", "wt", "wte", "fac", "xs", "tr", "xT", "r", "hs", "q", "v", "ss", "sqrt", "vo", "qke", "kept", "dch"))
        s_ho = [sem(f"ho{i}") for i in range(2)]
        with nc.Block() as block:
            @block.sync
            def _(sp):
                sp.dma_start(wraw[:, :, :], ins["L1_mix_Wqkv"].rearrange("(c p) n -> p c n", p=P)).then_inc(s_raw, 16)
                for r in range(R):
                    sp.dma_start(wr[:, :, r, :], ins["L1_gnn_weight"][r].rearrange("(k p) n -> p k n", p=P)).then_inc(s_w, 16)
                sp.dma_start(bias[:, :], ins["L1_mix_bqkv"].partition_broadcast(TN)).then_inc(s_b, 16)
                sp.dma_start(fac[:, 0:HG], ins["L1_mix_temperature"].rearrange("a h b c -> (a h b c)").partition_broadcast(TN)).then_inc(s_b, 16)

                def store(i, k):
                    t = 2 * i + k
                    sp.wait_ge(s_hs, NR * t + NR)
                    sp.dma_start(s.h_d.rearrange("(n r) d -> n (r d)", r=R)[bass.ds(t * TN, TN), :], hs[k][:, :]).then_inc(s_ho[k], 16)
                pairs(sp, store)
                sp.wait_ge(s_ho[0], 16 * 13)
                sp.wait_ge(s_ho[1], 16 * 12)

            @block.vector
            def _(dve):
                ch = Chain(dve, s_dch, 5)
                for n in range(3):
                    dve.wait_ge(s_wt, n + 1)
                    nc.vector.tensor_copy(wT[:, :, n * D:(n + 1) * D].rearrange("p k (c n) -> p c k n", c=2),
                                          psR[n][:, :].rearrange("p (c k n) -> p c k n", c=2, k=KD)).then_inc(s_wte, 1)
                dve.wait_ge(s_b, 32)
                nc.vector.tensor_scalar(fac[:, 0:HG], fac[:, 0:HG], SC * SC, None, ALU.mult).then_inc(s_fac, 1)
                nc.vector.memset(fac[:, HG:2 * HG], SC).then_inc(s_fac, 1)
                nc.vector.memset(s.q1[:, NT, :], 0.0)
                dve.wait_ge(s_fac, 2)

                def norm(i, slots):
                    for k in slots:
                        t = 2 * i + k
                        after(dve, s_tr, 2 * i)
                        nc.vector.tensor_scalar(xs[k][:, :], flat(s.x[:, bass.ds(t, 1), :]), s.mv[:, bass.ds(t, 1), 0],
                                                s.rstd[:, bass.ds(t, 1)], ALU.subtract, ALU.mult).then_inc(s_xs, 1)

                def keep_turned(i, k):
                    dve.wait_ge(s_tr, 2 * i + k + 1)
                    after(dve, s_r, NR * (2 * i + k - 1) if later(i) else 0)
                    nc.vector.tensor_copy(xT[k][:, :, :], psT[k][:, 0:KD * TN].rearrange("p (k n) -> p k n", k=KD)).then_inc(s_xT, 1)

                def tile(i, k):
                    t = 2 * i + k
                    ch.at(t)
                    dve.wait_ge(s_q, t + 1)
                    after(dve, s_kept, 2 * t)
                    ch.link(nc.vector.tensor_tensor(qk[:, :], psQ[0:TN, :], bias[:, 0:2 * D], ALU.add))
                    dve.sem_inc(s_qke, 1)
                    ch.link(nc.vector.tensor_tensor(sq[:, :], qk[:, :], qk[:, :], ALU.mult))
                    nc.vector.tensor_reduce(nrm[:, :], sq[:, :].rearrange("p (h d) -> p h d", d=DK), AX.X, ALU.add).then_inc(s_ss, 1)
                    dve.wait_ge(s_v, t + 1)
                    nc.vector.tensor_tensor(flat(s.v1[:, bass.ds(t, 1), :]), psV[0:TN, 0:D], bias[:, 2 * D:3 * D], ALU.add).then_inc(s_vo, 1)
                    dve.wait_ge(s_sqrt, t + 1)
                    ch.link(nc.vector.tensor_scalar(nrm[:, 0:HG], nrm[:, 0:HG], SC, 1e-12, ALU.mult, ALU.max))
                    nc.vector.tensor_scalar(nrm[:, HG:2 * HG], nrm[:, HG:2 * HG], 1e-12, None, ALU.max).then_inc(s_fac, 1)
                    dve.wait_ge(s_fac, t + 3)
                    ch.link(nc.vector.reciprocal(nrm[:, :], nrm[:, :]))
                    ch.link(nc.vector.tensor_tensor(nrm[:, :], nrm[:, :], fac[:, :], ALU.mult))
                    for n, to in enumerate((s.q1, s.k1)):
                        nc.vector.tensor_tensor(flat(to[:, bass.ds(t, 1), :]).rearrange("p (h d) -> p h d", d=DK),
                                                qk[:, n * D:(n + 1) * D].rearrange("p (h d) -> p h d", d=DK),
                                                nrm[:, n * HG:(n + 1) * HG].unsqueeze(2).to_broadcast([TN, HG, DK]), ALU.mult).then_inc(s_kept, 1)

                def both(i, slots):
                    for k in range(2):
                        if later(i):
                            tile(i - 1, k)
                        if k in slots:
                            keep_turned(i, k)
                duos(dve, NT, (0, norm), (0, both))
                tile(NT // 2, 0)

            @block.scalar
            def _(act):
                def tile(i, k):
                    t = 2 * i + k
                    after(act, s_ho[k], 16 * i)
                    for n in range(NR):
                        act.wait_ge(s_r, NR * t + n + 1)
                        nc.scalar.activation(hs[k][:, n * 512:(n + 1) * 512], turn_of(psR, n)[0:TN, :], ACT.Copy).then_inc(s_hs, 1)
                    act.wait_ge(s_ss, t + 1)
                    nc.scalar.activation(nrm[:, :], nrm[:, :], ACT.Sqrt).then_inc(s_sqrt, 1)
                pairs(act, tile)

            @block.tensor
            def _(pe):
                pe.wait_ge(s_raw, 16)
                for n in range(3):
                    for c in range(2):
                        for k in range(KD):
                            last = nc.tensor.transpose(psR[n][:, c * D + k * P:c * D + (k + 1) * P], wraw[:, 2 * n + c, k * P:(k + 1) * P], s.ident[:, :])
                    last.then_inc(s_wt, 1)
                pe.wait_ge(s_wte, 3)
                pe.wait_ge(s_w, 16 * R)

                def turn(i, slots):
                    for k in slots:
                        pe.wait_ge(s_xs, 2 * i + k + 1)
                        after(pe, s_xT, 2 * i + k - 1 if later(i) else 0)
                        for c in range(KD):
                            last = nc.tensor.transpose(psT[k][:, c * TN:(c + 1) * TN], xs[k][:, c * P:(c + 1) * P], s.ident[0:TN, 0:TN])
                        last.then_inc(s_tr, 1)

                def tile(i, k):
                    t = 2 * i + k
                    pe.wait_ge(s_xT, t + 1)
                    after(pe, s_qke, t)
                    for c in range(KD):
                        last = nc.tensor.matmul(psQ[0:TN, :], xT[k][:, c, :], wT[:, c, 0:2 * D], start=(c == 0), stop=(c == KD - 1))
                    last.then_inc(s_q, 1)
                    after(pe, s_vo, t)
                    for c in range(KD):
                        last = nc.tensor.matmul(psV[0:TN, 0:D], xT[k][:, c, :], wT[:, c, 2 * D:3 * D], start=(c == 0), stop=(c == KD - 1))
                    last.then_inc(s_v, 1)
                    for n in range(NR):
                        after(pe, s_hs, NR * t + max(n - len(psR) + 1, 0))
                        for c in range(KD):
                            last = nc.tensor.matmul(turn_of(psR, n)[0:TN, :], xT[k][:, c, :],
                                                    wr[:, c, 2 * n:2 * n + 2, :].rearrange("p r d -> p (r d)"), start=(c == 0), stop=(c == KD - 1))
                        last.then_inc(s_r, 1)

                def products(i, slots):
                    for k in slots:
                        tile(i, k)
                duos(pe, NT, (0, turn), (1, products))


def stage_moments(nc, s, half):
    SC = float(DK) ** 0.25
    A, B, C = 0.5, 1.0, 1.0
    W = HH * VE
    PER = 3
    h0 = half * HH
    with ExitStack() as ctx:
        tag = f"k{half}_"
        sb = lambda name, shape, dt=F32: ctx.enter_context(nc.sbuf_tensor(tag + name, shape, dt))
        sem = lambda name: s.new_sem(tag + name)
        dbl = [sb(f"dbl{i}", [TN, HH, 2 * DK]) for i in range(2)]
        kk = [sb(f"kk{i}", [TN, NS + 1, P]) for i in range(2)]
        v1 = [sb(f"v1{i}", [TN, HH, VE]) for i in range(2)]
        wt = sb("wt", [P, NS + 1])
        one = sb("one", [TN, TN])
        ps = [ctx.enter_context(nc.psum_tensor(f"{tag}ps{i}", [P, 512], F32)) for i in range((NS + 1) // PER)]
        psC = ctx.enter_context(nc.psum_tensor(tag + "psC", [P, 512], F32))
        s_init, s_dbl, s_v, s_kk, s_m, s_end = (sem(n) for n in ("init", "dbl", "v", "kk", "m", "end"))
        with nc.Block() as block:
            @block.scalar
            def _(act):
                act.wait_ge(s_init, 8)

                def tile(i, k):
                    t = 2 * i + k
                    after(act, s_m, 2 * i + k - 1)
                    keys = flat(s.k1[:, bass.ds(t, 1), h0 * DK:(h0 + HH) * DK]).rearrange("p (h d) -> p h d", d=DK)
                    for c in range(2):
                        nc.scalar.activation(dbl[k][:, :, c * DK:(c + 1) * DK], keys, ACT.Copy).then_inc(s_dbl, 1)
                    nc.scalar.activation(kk[k][:, NS, :].rearrange("p (h d) -> p h d", d=DK), keys, ACT.Copy).then_inc(s_dbl, 1)
                    nc.scalar.activation(v1[k][:, :, 1:VE], flat(s.v1[:, bass.ds(t, 1), h0 * DK:(h0 + HH) * DK]).rearrange("p (h d) -> p h d", d=DK),
                                         ACT.Copy).then_inc(s_v, 1)
                pairs(act, tile)

            @block.vector
            def _(dve):
                nc.vector.memset(one[:, :], 1.0).then_inc(s_init, 1)
                for k in range(2):
                    nc.vector.memset(v1[k][:, :, :], 1.0).then_inc(s_init, 1)
                nc.vector.memset(wt[:, 0:1], A / N).then_inc(s_init, 1)
                nc.vector.memset(wt[:, 1:NS - 1], 2 * A / N).then_inc(s_init, 1)
                nc.vector.memset(wt[:, NS - 1:NS], A / N).then_inc(s_init, 1)
                nc.vector.memset(wt[:, NS:NS + 1], SC ** 2 * B / N).then_inc(s_init, 1)
                nc.vector.memset(s.mom[half][:, :, :], 0.0).then_inc(s_init, 1)

                def tile(i, k):
                    t = 2 * i + k
                    dve.wait_ge(s_dbl, 3 * t + 3)
                    after(dve, s_m, 2 * i + k - 1)
                    nc.vector.tensor_tensor(kk[k][:, 0:NS, :].rearrange("p r (h d) -> p r h d", d=DK), rotations(dbl[k], 0),
                                            dbl[k][:, :, 0:DK].unsqueeze(1).to_broadcast([TN, NS, HH, DK]), ALU.mult).then_inc(s_kk, 1)
                pairs(dve, tile)
                dve.wait_ge(s_end, 1)
                dve.wait_ge(s_init, 8)
                for h in range(HH):
                    rows, cols = slice(h * DK, (h + 1) * DK), slice(h * VE, (h + 1) * VE)
                    for n, bank in enumerate(ps):
                        nc.vector.tensor_tensor(s.mom[half][rows, n * PER:(n + 1) * PER, cols],
                                                bank[rows, 0:PER * W].rearrange("p (r c) -> p r c", r=PER)[:, :, cols],
                                                wt[rows, n * PER:(n + 1) * PER].unsqueeze(2).to_broadcast([DK, PER, VE]), ALU.mult)
                nc.vector.tensor_scalar(s.mom0[:, half, :], psC[0:TN, 0:W], SC ** 4 * C / N, None, ALU.mult)

            @block.tensor
            def _(pe):
                for bank in (*ps, psC):
                    nc.tensor.matmul(bank[:, 0:PER * W], s.zero[:, 0:P], s.zero[:, 0:PER * W], start=True, stop=False)
                pe.wait_ge(s_init, 8)

                def tile(i, k):
                    t = 2 * i + k
                    pe.wait_ge(s_v, t + 1)
                    values = v1[k][:, :, :].rearrange("p h d -> p (h d)")
                    nc.tensor.matmul(psC[0:TN, 0:W], one[:, :], values, start=False, stop=False)
                    pe.wait_ge(s_kk, t + 1)
                    for r in range(NS + 1):
                        last = nc.tensor.matmul(ps[r // PER][:, r % PER * W:(r % PER + 1) * W], kk[k][:, r, :], values, start=False, stop=False)
                    last.then_inc(s_m, 1)
                pairs(pe, tile)
                for bank in (*ps, psC):
                    last = nc.tensor.matmul(bank[:, 0:PER * W], s.zero[:, 0:P], s.zero[:, 0:PER * W], start=False, stop=True)
                last.then_inc(s_end, 1)


def stage_batchnorm(nc, s, ins):
    with ExitStack() as ctx:
        sb = lambda name, shape, dt=F32: ctx.enter_context(nc.sbuf_tensor("v_" + name, shape, dt))
        sem = lambda name: s.new_sem("v_" + name)
        one = sb("one", [TN, TN])
        mean = sb("mean", [TN, D])
        var = sb("var", [TN, D])
        scale = sb("scale", [TN, D])
        sq = [sb(f"sq{i}", [TN, D]) for i in range(2)]
        psM, psV = (ctx.enter_context(nc.psum_tensor("v_" + n, [P, 512], F32)) for n in ("psM", "psV"))
        s_in, s_one, s_sum, s_mean, s_c, s_sq, s_v, s_var, s_sd, s_dch = (
            sem(n) for n in ("in", "one", "sum", "mean", "c", "sq", "v", "var", "sd", "dch"))
        with nc.Block() as block:
            @block.sync
            def _(sp):
                sp.dma_start(scale[:, :], ins["L1_gnn_gamma"].partition_broadcast(TN)).then_inc(s_in, 16)

            @block.vector
            def _(dve):
                nc.vector.memset(one[:, :], 1.0).then_inc(s_one, 1)
                dve.wait_ge(s_sum, 1)
                nc.vector.tensor_scalar(mean[:, :], psM[0:TN, 0:D], 1.0 / N, None, ALU.mult).then_inc(s_mean, 1)
                dve.wait_ge(s_mean, 1)

                def tile(i, k):
                    t = 2 * i + k
                    row = flat(s.y[:, bass.ds(t, 1), :])
                    nc.vector.tensor_tensor(row, row, mean[:, :], ALU.subtract).then_inc(s_c, 1)
                    dve.wait_ge(s_c, t + 1)
                    after(dve, s_v, 2 * i + k - 1)
                    nc.vector.tensor_tensor(sq[k][:, :], row, row, ALU.mult).then_inc(s_sq, 1)
                pairs(dve, tile)
                dve.wait_ge(s_v, NT + 1)
                nc.vector.tensor_scalar(var[:, :], psV[0:TN, 0:D], 1.0 / N, EPS, ALU.mult, ALU.add).then_inc(s_var, 1)
                dve.wait_ge(s_sd, 1)
                nc.vector.reciprocal(var[:, :], var[:, :]).then_inc(s_dch, 1)
                dve.wait_ge(s_dch, 1)
                dve.wait_ge(s_in, 16)
                nc.vector.tensor_tensor(scale[:, :], scale[:, :], var[:, :], ALU.mult).then_inc(s_dch, 1)
                dve.wait_ge(s_dch, 2)
                with dve.Fori(0, NT) as t:
                    row, out = flat(s.y[:, bass.ds(t, 1), :]), flat(s.x[:, bass.ds(t, 1), :])
                    nc.vector.tensor_tensor(row, row, scale[:, :], ALU.mult).then_inc(s_dch, 1)
                    dve.wait_ge(s_dch, t + 3)
                    nc.vector.tensor_tensor(out, out, row, ALU.add)

            @block.scalar
            def _(act):
                act.wait_ge(s_var, 1)
                nc.scalar.activation(var[:, :], var[:, :], ACT.Sqrt).then_inc(s_sd, 1)

            @block.tensor
            def _(pe):
                pe.wait_ge(s_one, 1)
                for t in range(NT):
                    last = nc.tensor.matmul(psM[0:TN, 0:D], one[:, :], s.y[:, t, :], start=(t == 0), stop=(t == NT - 1))
                last.then_inc(s_sum, 1)
                nc.tensor.matmul(psV[0:TN, 0:D], s.zero[0:TN, 0:TN], s.zero[0:TN, 0:D], start=True, stop=False)

                def tile(i, k):
                    pe.wait_ge(s_sq, 2 * i + k + 1)
                    nc.tensor.matmul(psV[0:TN, 0:D], one[:, :], sq[k][:, :], start=False, stop=False).then_inc(s_v, 1)
                pairs(pe, tile)
                nc.tensor.matmul(psV[0:TN, 0:D], s.zero[0:TN, 0:TN], s.zero[0:TN, 0:D], start=False, stop=True).then_inc(s_v, 1)


def stage_relations_mix1(nc, s, ins):
    SLOTS = [(a, j) for a in range(NB) for j in range(UJ)]
    W = HH * VE
    BK = 4
    GROUPS = [(a, min(a + BK, NS + 1)) for a in range(0, NS + 1, BK)]
    NG = len(GROUPS)
    with ExitStack() as ctx:
        sb = lambda name, shape, dt=F32: ctx.enter_context(nc.sbuf_tensor("q_" + name, shape, dt))
        sem = lambda name: s.new_sem("q_" + name)
        pb = lambda name: ctx.enter_context(nc.psum_tensor("q_" + name, [P, 512], F32))
        wraw = sb("wraw", [P, 2, D])
        wT = sb("wT", [P, KD, D])
        bias = sb("bias", [TN, D])
        dbl = sb("dbl", [TN, HG, 2 * DK])
        qq = [sb(f"qq{g}", [TN, NS + 1, P]) for g in range(2)]
        qT = [sb(f"qT{g}", [P, NS + 1, TN]) for g in range(2)]
        y1 = [sb(f"y1{g}", [TN, HH, VE]) for g in range(2)]
        rc = [sb(f"rc{g}", [TN, HH]) for g in range(2)]
        o = sb("o", [TN, D])
        oT = sb("oT", [P, KD, TN])
        res = sb("res", [TN, D])
        psT = [pb(f"psT{i}") for i in range(3)]
        psY = [pb(f"psY{i}") for i in range(2)]
        psO, psP = pb("psO"), pb("psP")
        shift = sb("shift", [TN, D])
        iota_b = sb("iota_b", [TN, TN])
        idx = [sb(f"idx{a}", [TN, UJ], I32) for a in range(NB)]
        rows = [sb(f"rows{a}_{j}", [TN, D]) for a, j in SLOTS]
        oh = [sb(f"oh{a}_{j}", [TN, TN]) for a, j in SLOTS]
        psR = pb("psR")
        s_blk, s_bch, s_go = (sem(n) for n in ("blk", "bch", "go"))
        s_sct, s_oh, s_idx = ([sem(f"{n}{a}") for a in range(NB)] for n in ("sct", "oh", "idx"))
        s_rows = s.rows_gathered
        s_raw, s_b, s_wt, s_wte, s_dbl, s_qq, s_tr, s_ev, s_y, s_y1, s_o, s_ot, s_oT, s_p, s_res, s_dch = (
            sem(n) for n in ("raw", "b", "wt", "wte", "dbl", "qq", "tr", "ev", "y", "y1", "o", "ot", "oT", "p", "res", "dch"))
        with nc.Block() as block:
            @block.sync
            def _(sp):
                sp.dma_start(wraw[:, :, :], ins["L1_mix_Wproj"].rearrange("(c p) n -> p c n", p=P)).then_inc(s_raw, 16)
                sp.dma_start(bias[:, :], ins["L1_mix_bproj"].partition_broadcast(TN)).then_inc(s_b, 16)
                sp.dma_start(shift[:, :], ins["L1_gnn_beta"].partition_broadcast(TN)).then_inc(s_b, 16)

            @block.gpsimd
            def _(pool):
                def gather(b, g, n, first):
                    for a in range(NB):
                        pool.wait_ge(s_sct[a], n + 1)
                        nc.gpsimd.tensor_copy(idx[a][:, :], s.reli[:, bass.ds(g + a, 1), :]).then_inc(s_idx[a], 1)
                        pool.wait_ge(s_idx[a], n + 1)
                        pool.sem_inc(s_go, 1)
                        for j in range(UJ):
                            nc.gpsimd.indirect_dma_start(out=rows[a * UJ + j][:, :], out_offset=None, in_=s.h_d,
                                                         in_offset=bass.IndirectOffsetOnAxis(ap=idx[a][:, j:j + 1], axis=0)).then_inc(s_rows[a], 16)
                each_block(nc, pool, s, gather)

            @block.vector
            def _(dve):
                ch = Chain(dve, s_dch, 2)
                dve.wait_ge(s_wt, 1)
                nc.vector.tensor_copy(wT[:, :, :].rearrange("p k (c n) -> p c k n", c=2),
                                      psO[:, :].rearrange("p (c k n) -> p c k n", c=2, k=KD)).then_inc(s_wte, 1)
                dve.wait_ge(s_b, 32)
                nc.vector.tensor_tensor(bias[:, :], bias[:, :], shift[:, :], ALU.add).then_inc(s_wte, 1)
                dve.wait_ge(s_wte, 2)
                nc.vector.tensor_copy(iota_b[:, :], s.iota_f[:, :]).then_inc(s_bch, 1)
                dve.wait_ge(s_bch, 1)

                def one_pass(b, g, n, first):
                    for a in range(NB):
                        dve.wait_ge(s_sct[a], n + 1)
                        for j in range(UJ):
                            last = nc.vector.tensor_scalar(oh[a * UJ + j][:, :], iota_b[:, :], s.dstf[:, bass.ds(g + a, 1), j], None, ALU.is_equal)
                        last.then_inc(s_oh[a], 1)

                def square(t):
                    queries = flat(s.q1[:, bass.ds(t, 1), :]).rearrange("p (h d) -> p h d", d=DK)
                    for c in range(2):
                        nc.vector.tensor_scalar(dbl[:, :, c * DK:(c + 1) * DK], queries, 1.0, None, ALU.mult).then_inc(s_dbl, 1)
                    dve.wait_ge(s_dbl, 2 * t + 2)
                    for g in range(2):
                        nc.vector.tensor_copy(qq[g][:, NS, :].rearrange("p (h d) -> p h d", d=DK), dbl[:, g * HH:(g + 1) * HH, 0:DK])
                        nc.vector.tensor_tensor(qq[g][:, 0:NS, :].rearrange("p r (h d) -> p r h d", d=DK), rotations(dbl, g * HH),
                                                dbl[:, g * HH:(g + 1) * HH, 0:DK].unsqueeze(1).to_broadcast([TN, NS, HH, DK]), ALU.mult).then_inc(s_qq, 1)

                def project(t):
                    out = flat(s.x[:, bass.ds(t, 1), :])
                    dve.wait_ge(s_ot, t + 1)
                    nc.vector.tensor_copy(oT[:, :, :], psO[:, 0:KD * TN].rearrange("p (k n) -> p k n", k=KD)).then_inc(s_oT, 1)
                    dve.wait_ge(s_p, t + 1)
                    nc.vector.tensor_tensor(res[:, :], psP[0:TN, 0:D], bias[:, :], ALU.add).then_inc(s_res, 1)
                    dve.wait_ge(s_res, t + 1)
                    nc.vector.tensor_tensor(out, out, res[:, :], ALU.add)

                def middle(b):
                    if later(b):
                        project(b - 1)
                    dve.wait_ge(s_tr, 2 * NG * b + 2 * NG)
                    square(b + 1)

                def end(t):
                    ch.at(t)
                    dve.wait_ge(s_blk, t + 1)
                    nc.vector.tensor_scalar(flat(s.y[:, bass.ds(t, 1), :]), psR[0:TN, 0:D], 1.0, None, ALU.mult).then_inc(s_bch, 1)
                    nc.vector.tensor_scalar(iota_b[:, :], iota_b[:, :], float(TN), None, ALU.add).then_inc(s_bch, 1)
                    for g in range(2):
                        dve.wait_ge(s_y, 2 * t + g + 1)
                        nc.vector.tensor_tensor(y1[g][:, :, :].rearrange("p h d -> p (h d)"), psY[g][0:TN, 0:W], s.mom0[:, g, :], ALU.add).then_inc(s_y1, 1)
                        dve.wait_ge(s_y1, 2 * t + g + 1)
                        ch.link(nc.vector.reciprocal(rc[g][:, :].unsqueeze(2), y1[g][:, :, 0:1]))
                        nc.vector.tensor_tensor(o[:, g * P:(g + 1) * P].rearrange("p (h d) -> p h d", d=DK), y1[g][:, :, 1:VE],
                                                rc[g][:, :].unsqueeze(2).to_broadcast([TN, HH, DK]), ALU.mult).then_inc(s_o, 1)
                    dve.wait_ge(s_bch, 2 * t + 3)
                square(0)
                each_block(nc, dve, s, one_pass, middle=middle, end=end, finish=lambda n: project(NT - 1))

            @block.scalar
            def _(act):
                def tile(i, k):
                    t = 2 * i + k
                    for g in range(2):
                        for n, (a, b) in enumerate(GROUPS):
                            act.wait_ge(s_tr, 2 * NG * t + g * NG + n + 1)
                            if n == 0:
                                after(act, s_y, 2 * t + g - 1)
                            nc.scalar.activation(qT[g][:, a:b, :], turn_of(psT, g * NG + n)[:, 0:(b - a) * TN].rearrange("p (r n) -> p r n", r=b - a),
                                                 ACT.Copy).then_inc(s_ev, 1)
                pairs(act, tile)

            @block.tensor
            def _(pe):
                pe.wait_ge(s_raw, 16)
                for c in range(2):
                    for k in range(KD):
                        last = nc.tensor.transpose(psO[:, c * D + k * P:c * D + (k + 1) * P], wraw[:, c, k * P:(k + 1) * P], s.ident[:, :])
                last.then_inc(s_wt, 1)
                pe.wait_ge(s_wte, 2)

                for a in range(NB):
                    pe.sem_inc(s_sct[a], 1)

                def turn(t, g):
                    pe.wait_ge(s_qq, 2 * t + g + 1)
                    for n, (a, b) in enumerate(GROUPS):
                        at = g * NG + n
                        if at < 3:
                            after(pe, s_ev, 2 * NG * t)
                        else:
                            pe.wait_ge(s_ev, 2 * NG * t + at - 2)
                        for r in range(a, b):
                            last = nc.tensor.transpose(turn_of(psT, at)[:, (r - a) * TN:(r - a + 1) * TN], qq[g][:, r, :], s.ident[0:TN, 0:TN])
                        last.then_inc(s_tr, 1)

                def contract(t, g):
                    after(pe, s_y1, 2 * t)
                    for n, (a, b) in enumerate(GROUPS):
                        pe.wait_ge(s_ev, 2 * NG * t + g * NG + n + 1)
                        for r in range(a, b):
                            last = nc.tensor.matmul(psY[g][0:TN, 0:W], qT[g][:, r, :], s.mom[g][:, r, :], start=(r == 0), stop=(r == NS))
                    last.then_inc(s_y, 1)

                def start(t, n):
                    pe.wait_ge(s_bch, 2 * t + 1)
                    nc.tensor.matmul(psR[0:TN, 0:D], s.zero[0:TN, 0:TN], s.zero[0:TN, 0:D], start=True, stop=False)
                    turn(t, 0)

                def one_pass(b, g, n, first):
                    for a in range(NB):
                        pe.wait_ge(s_oh[a], n + 1)
                        pe.wait_ge(s_rows[a], 16 * UJ * n + 16 * UJ)
                        for j in range(UJ):
                            last = nc.tensor.matmul(psR[0:TN, 0:D], oh[a * UJ + j][:, :], rows[a * UJ + j][:, :], start=False, stop=False)
                        last.then_inc(s_sct[a], 1)

                def turn_out(t):
                    pe.wait_ge(s_o, 2 * t + 2)
                    for c in range(KD):
                        last = nc.tensor.transpose(psO[:, c * TN:(c + 1) * TN], o[:, c * P:(c + 1) * P], s.ident[0:TN, 0:TN])
                    last.then_inc(s_ot, 1)

                def project(t):
                    pe.wait_ge(s_oT, t + 1)
                    for c in range(KD):
                        last = nc.tensor.matmul(psP[0:TN, 0:D], oT[:, c, :], wT[:, c, :], start=(c == 0), stop=(c == KD - 1))
                    last.then_inc(s_p, 1)

                def middle(t):
                    if later(t):
                        turn_out(t - 1)
                    turn(t, 1)
                    if later(t):
                        project(t - 1)
                    contract(t, 0)

                def end(t):
                    nc.tensor.matmul(psR[0:TN, 0:D], s.zero[0:TN, 0:TN], s.zero[0:TN, 0:D], start=False, stop=True).then_inc(s_blk, 1)
                    contract(t, 1)

                def finish(n):
                    turn_out(NT - 1)
                    project(NT - 1)
                each_block(nc, pe, s, one_pass, start=start, middle=middle, end=end, finish=finish)


def stage_normalise(nc, s):
    with nc.Block() as block:
        @block.vector
        def _(dve):
            with dve.Fori(0, NT) as t:
                nc.vector.tensor_scalar(flat(s.y[:, bass.ds(t, 1), :]), flat(s.x[:, bass.ds(t, 1), :]), s.mv[:, bass.ds(t, 1), 0],
                                        s.rstd[:, bass.ds(t, 1)], ALU.subtract, ALU.mult)


def stage_experts1(nc, s, ins, out):
    r = Shared()
    r.K, r.tiles = 2, TILES1
    with ExitStack() as own:
        sb = lambda name, shape, dt=F32: own.enter_context(nc.sbuf_tensor("z_" + name, shape, dt))
        sem = lambda name: s.new_sem("z_" + name)
        r.lg, r.pos, r.gate = sb("lg", [TN, NT, X0]), sb("pos", [TN, NT, 2], I32), sb("gate", [TN, NT, 2])
        r.expert = sb("expert", [1, r.tiles], I32)
        w1 = sb("w1", [P, X0, KD, F1])
        w2 = sb("w2", [P, X0, C1, D])
        b1 = sb("b1", [TN, X0, F1])
        b2 = sb("b2", [TN, X0, D])
        ga = sb("ga", [P, KD])
        be = sb("be", [P, KD])
        s_w1, s_w = sem("w1"), sem("w")
        with ExitStack() as ctx:
            sb = lambda name, shape, dt=F32: ctx.enter_context(nc.sbuf_tensor("zr_" + name, shape, dt))
            wr = sb("wr", [P, KD, X0])
            br = sb("br", [TN, X0])
            xs = [sb(f"xs{i}", [TN, D]) for i in range(2)]
            xT = [sb(f"xT{i}", [P, KD, TN]) for i in range(2)]
            psT, psL = ([ctx.enter_context(nc.psum_tensor(f"zr_{n}{i}", [P, 512], F32)) for i in range(2)] for n in ("psT", "psL"))
            s_xs, s_y, s_tr, s_xT, s_l, s_lg = (sem("r" + n) for n in ("xs", "y", "tr", "xT", "l", "lg"))
            with nc.Block() as block:
                @block.sync
                def _(sp):
                    sp.dma_start(ga[:, :], ins["L1_ffn_gamma"].rearrange("(c p) -> p c", p=P)).then_inc(s_w1, 16)
                    sp.dma_start(be[:, :], ins["L1_ffn_beta"].rearrange("(c p) -> p c", p=P)).then_inc(s_w1, 16)
                    sp.dma_start(wr[:, :, :], ins["L1_ffn_Wr"].rearrange("(k p) e -> p k e", p=P)).then_inc(s_w1, 16)
                    sp.dma_start(br[:, :], ins["L1_ffn_br"].partition_broadcast(TN)).then_inc(s_w1, 16)
                    sp.dma_start(b1[:, :, :].rearrange("p e n -> p (e n)"), ins["L1_ffn_b1"].rearrange("e n -> (e n)").partition_broadcast(TN)).then_inc(s_w, 16)
                    sp.dma_start(b2[:, :, :].rearrange("p e n -> p (e n)"), ins["L1_ffn_b2"].rearrange("e n -> (e n)").partition_broadcast(TN)).then_inc(s_w, 16)
                    for e in range(X0):
                        sp.dma_start(w1[:, e, :, :], ins["L1_ffn_W1"][e].rearrange("(k p) n -> p k n", p=P)).then_inc(s_w, 16)
                        sp.dma_start(w2[:, e, :, :], ins["L1_ffn_W2"][e].rearrange("(c p) n -> p c n", p=P)).then_inc(s_w, 16)

                @block.vector
                def _(dve):
                    dve.wait_ge(s_w1, 64)

                    def duo(i, slots):
                        for k in slots:
                            t = 2 * i + k
                            after(dve, s_y, 2 * i)
                            nc.vector.tensor_scalar(xs[k][:, :], flat(s.y[:, bass.ds(t, 1), :]), s.mv[:, bass.ds(t, 1), 0],
                                                    s.rstd[:, bass.ds(t, 1)], ALU.subtract, ALU.mult).then_inc(s_xs, 1)

                    def logits(i, slots):
                        for k in slots:
                            t = 2 * i + k
                            dve.wait_ge(s_l, t + 1)
                            nc.vector.tensor_tensor(flat(r.lg[:, bass.ds(t, 1), :]), psL[k][0:TN, 0:X0], br[:, :], ALU.add).then_inc(s_lg, 1)
                    duos(dve, NT, (0, duo), (1, logits))

                @block.scalar
                def _(act):
                    act.wait_ge(s_w1, 64)

                    def duo(i, slots):
                        for k in slots:
                            t = 2 * i + k
                            act.wait_ge(s_tr, t + 1)
                            for c in range(KD):
                                nc.scalar.activation(xT[k][:, c, :], psT[k][:, c * TN:(c + 1) * TN], ACT.Identity,
                                                     bias=be[:, c:c + 1], scale=ga[:, c:c + 1]).then_inc(s_xT, 1)
                        for k in slots:
                            t = 2 * i + k
                            nc.scalar.activation(flat(s.y[:, bass.ds(t, 1), :]), xs[k][:, :], ACT.Copy).then_inc(s_y, 1)
                    duos(act, NT, (0, duo))

                @block.tensor
                def _(pe):
                    pe.wait_ge(s_w1, 64)

                    def duo(i, slots):
                        for k in slots:
                            t = 2 * i + k
                            pe.wait_ge(s_xs, t + 1)
                            for c in range(KD):
                                last = nc.tensor.transpose(psT[k][:, c * TN:(c + 1) * TN], xs[k][:, c * P:(c + 1) * P], s.ident[0:TN, 0:TN])
                            last.then_inc(s_tr, 1)

                    def logits(i, slots):
                        for k in slots:
                            t = 2 * i + k
                            pe.wait_ge(s_xT, KD * t + KD)
                            after(pe, s_lg, 2 * i)
                            for c in range(KD):
                                last = nc.tensor.matmul(psL[k][0:TN, 0:X0], xT[k][:, c, :], wr[:, c, :], start=(c == 0), stop=(c == KD - 1))
                            last.then_inc(s_l, 1)
                    duos(pe, NT, (0, duo), (0, logits))
        stage_route(nc, s, r, "zt_")
        stage_dispatch(nc, s, r, "zd_")
        with ExitStack() as ctx:
            sb = lambda name, shape, dt=F32: ctx.enter_context(nc.sbuf_tensor("ze_" + name, shape, dt))
            pb = lambda name: ctx.enter_context(nc.psum_tensor("ze_" + name, [P, 512], F32))
            xs = [sb(f"xs{i}", [TN, D]) for i in range(2)]
            xT = [sb(f"xT{i}", [P, KD, TN]) for i in range(2)]
            h = [sb(f"h{i}", [TN, F1]) for i in range(2)]
            hT = [sb(f"hT{i}", [P, C1, TN]) for i in range(2)]
            o = [sb(f"o{i}", [TN, D]) for i in range(2)]
            psT, psH, psU = ([pb(f"{n}{i}") for i in range(2)] for n in ("psT", "psH", "psU"))
            psY = [pb("psY0"), pb("psY1")]
            s_tr, s_xT, s_h, s_hb, s_hg, s_u, s_hT, s_yy, s_o = (sem("e" + n) for n in ("tr", "xT", "h", "hb", "hg", "u", "hT", "yy", "o"))
            s_xs, s_out = ([sem(f"{n}{i}") for i in range(2)] for n in ("exs", "eout"))
            with nc.Block() as block:
                @block.sync
                def _(sp):
                    def duo(i, slots):
                        for k in slots:
                            t = 2 * i + k
                            after(sp, s_tr, 2 * i)
                            sp.dma_start(xs[k][:, :], s.sorted_d[bass.ds(t * TN, TN), :]).then_inc(s_xs[k], 16)
                    def store(i, slots):
                        for k in slots:
                            t = 2 * i + k
                            sp.wait_ge(s_o, t + 1)
                            sp.dma_start(s.done_d[bass.ds(t * TN, TN), :], o[k][:, :]).then_inc(s_out[k], 16)

                    duos(sp, r.tiles, (0, duo), (2, store))
                    for k in range(2):
                        sp.wait_ge(s_out[k], 16 * len(range(k, r.tiles, 2)))

                @block.scalar
                def _(act):
                    def duo(i, slots):
                        for k in slots:
                            t = 2 * i + k
                            act.wait_ge(s_tr, t + 1)
                            for c in range(KD):
                                nc.scalar.activation(xT[k][:, c, :], psT[k][:, c * TN:(c + 1) * TN], ACT.Identity,
                                                     bias=be[:, c:c + 1], scale=ga[:, c:c + 1]).then_inc(s_xT, 1)
                        for k in slots:
                            t = 2 * i + k
                            act.wait_ge(s_hb, t + 1)
                            nc.scalar.activation(h[k][:, :], h[k][:, :], ACT.Gelu).then_inc(s_hg, 1)
                    duos(act, r.tiles, (0, duo))

                @block.vector
                def _(dve):
                    dve.wait_ge(s_w, 16 * (2 * X0 + 2))

                    def bias(i, slots):
                        for k in slots:
                            t = 2 * i + k
                            e = expert_of(r, dve, t)
                            dve.wait_ge(s_h, t + 1)
                            after(dve, s_u, 2 * i)
                            nc.vector.tensor_tensor(h[k][:, :], psH[k][0:TN, :], flat(b1[:, bass.ds(e, 1), :]), ALU.add).then_inc(s_hb, 1)

                    def keep_turned(i, slots):
                        for k in slots:
                            dve.wait_ge(s_u, 2 * i + k + 1)
                            nc.vector.tensor_copy(hT[k][:, :, :], psU[k][:, 0:C1 * TN].rearrange("p (k n) -> p k n", k=C1)).then_inc(s_hT, 1)

                    def finish(i, slots):
                        for k in slots:
                            t = 2 * i + k
                            e = expert_of(r, dve, t)
                            dve.wait_ge(s_yy, t + 1)
                            after(dve, s_out[k], 16 * i)
                            nc.vector.tensor_tensor(o[k][:, :], psY[k][0:TN, 0:D], flat(b2[:, bass.ds(e, 1), :]), ALU.add).then_inc(s_o, 1)
                    duos(dve, r.tiles, (1, keep_turned), (0, bias), (1, finish))

                @block.tensor
                def _(pe):
                    pe.wait_ge(s_w, 16 * (2 * X0 + 2))

                    def turn(i, slots):
                        for k in slots:
                            pe.wait_ge(s_xs[k], 16 * i + 16)
                            for c in range(KD):
                                last = nc.tensor.transpose(psT[k][:, c * TN:(c + 1) * TN], xs[k][:, c * P:(c + 1) * P], s.ident[0:TN, 0:TN])
                            last.then_inc(s_tr, 1)

                    def up(i, slots):
                        for k in slots:
                            t = 2 * i + k
                            e = expert_of(r, pe, t)
                            pe.wait_ge(s_xT, KD * t + KD)
                            for c in range(KD):
                                last = nc.tensor.matmul(psH[k][0:TN, :], xT[k][:, c, :], w1[:, bass.ds(e, 1), c, :].rearrange("p a n -> p (a n)"),
                                                        start=(c == 0), stop=(c == KD - 1))
                            last.then_inc(s_h, 1)

                    def turn_hidden(i, slots):
                        for k in slots:
                            t = 2 * i + k
                            pe.wait_ge(s_hg, t + 1)
                            for c in range(C1):
                                last = nc.tensor.transpose(psU[k][:, c * TN:(c + 1) * TN], h[k][:, c * P:(c + 1) * P], s.ident[0:TN, 0:TN])
                            last.then_inc(s_u, 1)

                    def down(i, slots):
                        for k in slots:
                            t = 2 * i + k
                            e = expert_of(r, pe, t)
                            pe.wait_ge(s_hT, t + 1)
                            after(pe, s_o, 2 * i)
                            for c in range(C1):
                                last = nc.tensor.matmul(psY[k][0:TN, 0:D], hT[k][:, c, :], w2[:, bass.ds(e, 1), c, :].rearrange("p a n -> p (a n)"),
                                                        start=(c == 0), stop=(c == C1 - 1))
                            last.then_inc(s_yy, 1)
                    duos(pe, r.tiles, (0, turn), (1, turn_hidden), (0, up), (1, down))
        stage_combine(nc, s, r, out, "zc_")


def program(nc, ins, outs):
    with ExitStack() as ctx:
        ctx.enter_context(nc.allow_non_contiguous_dma(reason="bias vectors, one element to a partition"))
        s = build_shared(nc, ctx, ins)
        with ExitStack() as first:
            with layer(nc, s):
                stage_prepare(nc, s, ins)
                stage_ln(nc, s, s.x, "x")
                build_layer0(nc, s, first)
                stage_project(nc, s, ins)
                stage_attention(nc, s, ins)
            with layer(nc, s):
                stage_fold(nc, s, ins)
                stage_mix_attend(nc, s, ins)
                stage_ln(nc, s, s.y, "m")
                stage_mix_mlp(nc, s, ins)
                stage_ln(nc, s, s.x, "e")
        with layer(nc, s):
            stage_experts0(nc, s, ins)
        with layer(nc, s):
            stage_ln(nc, s, s.x, "f")
            with ExitStack() as mixer:
                build_layer1(nc, s, mixer)
                build_moments(nc, s, mixer)
                with ExitStack() as keys:
                    build_keys(nc, s, keys)
                    stage_project1(nc, s, ins)
                    stage_moments(nc, s, 0)
                    stage_moments(nc, s, 1)
                stage_relations_mix1(nc, s, ins)
                stage_batchnorm(nc, s, ins)
        with layer(nc, s):
            stage_ln(nc, s, s.x, "g")
            stage_normalise(nc, s)
            stage_ln(nc, s, s.y, "h")
            stage_experts1(nc, s, ins, outs[0])




_INS = ['x', 'src', 'dst', 'edge_type_8', 'L0_gnn_Wq', 'L0_gnn_Wk', 'L0_gnn_Wv', 'L0_mix_w_qkv', 'L0_mix_b_qkv', 'L0_mix_norm_g', 'L0_mix_norm_b', 'L0_mix_w_fc1', 'L0_mix_b_fc1', 'L0_mix_w_fc2', 'L0_mix_b_fc2', 'L0_ffn_W1', 'L0_ffn_b1', 'L0_ffn_Wg', 'L0_ffn_bg', 'L0_ffn_Wd', 'L0_ffn_bd', 'L1_gnn_weight', 'L1_gnn_gamma', 'L1_gnn_beta', 'L1_mix_Wqkv', 'L1_mix_bqkv', 'L1_mix_Wproj', 'L1_mix_bproj', 'L1_mix_temperature', 'L1_ffn_gamma', 'L1_ffn_beta', 'L1_ffn_Wr', 'L1_ffn_br', 'L1_ffn_W1', 'L1_ffn_b1', 'L1_ffn_W2', 'L1_ffn_b2']
_OUTS = [((3125, 256), 'float32')]


def kernel(**inputs):
    import numpy as _np
    import concourse.bacc as _bacc
    from concourse import mybir as _mybir
    from concourse.bass_utils import run_bass_kernel_spmd as _run

    nc = _bacc.Bacc("TRN2", target_bir_lowering=False, num_devices=1)
    arrays, args = {}, {}
    for name in _INS:
        a = _np.ascontiguousarray(inputs[name])
        arrays[f"in_{name}_dram"] = a
        args[name] = nc.dram_tensor(f"in_{name}_dram", a.shape, _mybir.dt.from_np(a.dtype), kind="ExternalInput").ap()
    outs = []
    for i, (shape, dtype) in enumerate(_OUTS):
        dt = _mybir.dt.from_np(_np.dtype(dtype))
        outs.append(nc.dram_tensor(f"out_{i}_dram", shape, dt, kind="ExternalOutput").ap())
    program(nc, args, outs)
    r = _run(nc, [arrays], core_ids=[0])
    return r.results[0]["out_0_dram"]
```
